# Optimizing a Trainium2 kernel written in Bass

```python
import numpy as np
import jax
import jax.numpy as jnp

def _softmax(x, axis=-1):
    return jax.nn.softmax(x, axis=axis)

def _gelu(x):
    return jax.nn.gelu(x, approximate=True)

def _silu(x):
    return jax.nn.silu(x)

def _sigmoid(x):
    return jax.nn.sigmoid(x)

def _layernorm(x, axis=-1, eps=1e-05):
    m = jnp.mean(x, axis=axis, keepdims=True)
    v = jnp.var(x, axis=axis, keepdims=True)
    return (x - m) / jnp.sqrt(v + eps)

def _scatter_add(tgt, idx, src, axis=0):
    return tgt.at[idx].add(src)

def _segment_sum(src, seg, n):
    return jax.ops.segment_sum(src, seg, n)
kernel_name = 'mk_adaln_attn_ffn_d1_seqx_r4_05c4d5'

def setup_inputs(seed: int=0):
    np.random.seed(seed)
    _w = jnp.asarray

    def _rec_inputs():
        import jax
        import jax.numpy as jnp
        _rk = jax.random.key(seed)
        x = -0.0001538 + 1 * jax.random.normal(jax.random.fold_in(_rk, 1), (2, 1024, 256), jnp.float32)
        _lenS = 1024 - jax.random.randint(jax.random.fold_in(_rk, 7), (2,), 0, max(1, 1024 // 4) + 1, jnp.int32)
        _lenS2 = 1024 - jax.random.randint(jax.random.fold_in(_rk, 8), (2,), 0, max(1, 1024 // 4) + 1, jnp.int32)
        cond_1024 = 0.00782532 + 1.00527 * jax.random.normal(jax.random.fold_in(_rk, 11), (2, 256), jnp.float32)
        return (x, cond_1024)
    x, cond_1024 = _rec_inputs()

    def _L0_cond_setup():
        import jax, jax.numpy as jnp
        import numpy as np
        NUM_EXPERTS = 4
        TOP_K = 2
        key = jax.random.key(seed)
        ks = jax.random.split(key, 16)
        B, L, D, E, H = (8, 192, 256, NUM_EXPERTS, 1024)
        s = 0.02
        return {'context_c': jax.random.normal(ks[0], (B, L, D), jnp.float32), 'time_cond': jax.random.normal(ks[1], (B, D), jnp.float32), 'gate_w': jax.random.normal(ks[2], (3 * D, E), jnp.float32) * s, 'gate_b': jnp.zeros((E,), jnp.float32), 'time_w': jax.random.normal(ks[3], (D, 2 * E), jnp.float32) * s, 'time_b': jnp.zeros((2 * E,), jnp.float32), 'ew1': jax.random.normal(ks[4], (E, D, H), jnp.float32) * s, 'eb1': jnp.zeros((E, H), jnp.float32), 'ew2': jax.random.normal(ks[5], (E, H, D), jnp.float32) * s, 'eb2': jnp.zeros((E, D), jnp.float32), 'sw1': jax.random.normal(ks[6], (D, H), jnp.float32) * s, 'sb1': jnp.zeros((H,), jnp.float32), 'sw2': jax.random.normal(ks[7], (H, D), jnp.float32) * s, 'sb2': jnp.zeros((D,), jnp.float32)}
    _L0_cond_all = _L0_cond_setup()
    _L0_cond_in = {k: v for k, v in _L0_cond_all.items() if k in ('gate_w', 'gate_b', 'time_w', 'time_b', 'ew1', 'eb1', 'ew2', 'eb2', 'sw1', 'sb1', 'sw2', 'sb2')}
    del _L0_cond_all

    def _L0_attn_setup():
        import jax, jax.numpy as jnp
        import numpy as np
        H = 16
        RMS_EPS = 1.1920928955078125e-07
        NORM_EPS = 1e-12

        def _rms_norm(t):
            ms = jnp.mean(t * t, axis=-1, keepdims=True)
            return t * jax.lax.rsqrt(ms + RMS_EPS)
        key = jax.random.key(seed)
        k1, k2, k3 = jax.random.split(key, 3)
        B, N, C = (2, 512, 256)
        x = jax.random.normal(k1, (B, N, C), dtype=jnp.float32)
        w_qkv = jax.random.normal(k2, (3 * C, C), dtype=jnp.float32) * C ** (-0.5)
        w_proj = jax.random.normal(k3, (C, C), dtype=jnp.float32) * C ** (-0.5)
        return {'x': x, 'w_qkv': w_qkv, 'w_proj': w_proj}
    _L0_attn_all = _L0_attn_setup()
    _L0_attn_in = {k: v for k, v in _L0_attn_all.items() if k in ('w_qkv', 'w_proj')}
    del _L0_attn_all

    def _L0_cond2_setup():
        import jax, jax.numpy as jnp
        import numpy as np
        key = jax.random.key(seed)
        ks = jax.random.split(key, 8)
        B, L, D, N, K = (4, 1024, 256, 64, 4)
        return {'x': jax.random.normal(ks[0], (B, L, D), dtype=jnp.float32), 'conv_w': jax.random.normal(ks[1], (K, 1, D), dtype=jnp.float32) * 0.1, 'conv_b': jnp.zeros((D,), dtype=jnp.float32), 'Wp': jax.random.normal(ks[2], (D, 2 * N), dtype=jnp.float32) * (1.0 / np.sqrt(D)), 'bp': jnp.zeros((2 * N,), dtype=jnp.float32), 'Ws': jax.random.normal(ks[3], (D, N), dtype=jnp.float32) * (1.0 / np.sqrt(D)), 'bs': jnp.zeros((N,), dtype=jnp.float32), 'A_log': jax.random.normal(ks[4], (N,), dtype=jnp.float32) * 0.02, 'dt_log': jax.random.normal(ks[5], (N,), dtype=jnp.float32) * 0.02, 'Wo': jax.random.normal(ks[6], (N, D), dtype=jnp.float32) * (1.0 / np.sqrt(N)), 'bo': jnp.zeros((D,), dtype=jnp.float32)}
    _L0_cond2_all = _L0_cond2_setup()
    _L0_cond2_in = {k: v for k, v in _L0_cond2_all.items() if k in ('conv_b', 'Wp', 'bp', 'Ws', 'bs', 'A_log', 'dt_log', 'Wo', 'bo')}
    del _L0_cond2_all

    def _L0_ffn_setup():
        import jax, jax.numpy as jnp
        import numpy as np
        B, S, H, FFN, E = (2, 512, 256, 1024, 8)
        key = jax.random.key(seed)
        k0, k1, k2, k3 = jax.random.split(key, 4)
        return {'hidden_states': jax.random.normal(k0, (B, S, H), dtype=jnp.float32), 'Wr': jax.random.normal(k1, (H, E), dtype=jnp.float32) * 0.02, 'br': jnp.zeros((E,), dtype=jnp.float32), 'W1': jax.random.normal(k2, (E, H, FFN), dtype=jnp.float32) * 0.02, 'W2': jax.random.normal(k3, (E, FFN, H), dtype=jnp.float32) * 0.02}
    _L0_ffn_all = _L0_ffn_setup()
    _L0_ffn_in = {k: v for k, v in _L0_ffn_all.items() if k in ('Wr', 'br', 'W1', 'W2')}
    del _L0_ffn_all
    return {'x': x, 'cond_1024': cond_1024, 'L0_cond_gate_w': _L0_cond_in['gate_w'], 'L0_cond_gate_b': _L0_cond_in['gate_b'], 'L0_cond_time_w': _L0_cond_in['time_w'], 'L0_cond_time_b': _L0_cond_in['time_b'], 'L0_cond_ew1': _L0_cond_in['ew1'], 'L0_cond_eb1': _L0_cond_in['eb1'], 'L0_cond_ew2': _L0_cond_in['ew2'], 'L0_cond_eb2': _L0_cond_in['eb2'], 'L0_cond_sw1': _L0_cond_in['sw1'], 'L0_cond_sb1': _L0_cond_in['sb1'], 'L0_cond_sw2': _L0_cond_in['sw2'], 'L0_cond_sb2': _L0_cond_in['sb2'], 'L0_attn_w_qkv': _L0_attn_in['w_qkv'], 'L0_attn_w_proj': _L0_attn_in['w_proj'], 'L0_cond2_conv_b': _L0_cond2_in['conv_b'], 'L0_cond2_Wp': _L0_cond2_in['Wp'], 'L0_cond2_bp': _L0_cond2_in['bp'], 'L0_cond2_Ws': _L0_cond2_in['Ws'], 'L0_cond2_bs': _L0_cond2_in['bs'], 'L0_cond2_A_log': _L0_cond2_in['A_log'], 'L0_cond2_dt_log': _L0_cond2_in['dt_log'], 'L0_cond2_Wo': _L0_cond2_in['Wo'], 'L0_cond2_bo': _L0_cond2_in['bo'], 'L0_ffn_Wr': _L0_ffn_in['Wr'], 'L0_ffn_br': _L0_ffn_in['br'], 'L0_ffn_W1': _L0_ffn_in['W1'], 'L0_ffn_W2': _L0_ffn_in['W2']}

def reference(x, cond_1024, L0_cond_gate_w, L0_cond_gate_b, L0_cond_time_w, L0_cond_time_b, L0_cond_ew1, L0_cond_eb1, L0_cond_ew2, L0_cond_eb2, L0_cond_sw1, L0_cond_sb1, L0_cond_sw2, L0_cond_sb2, L0_attn_w_qkv, L0_attn_w_proj, L0_cond2_conv_b, L0_cond2_Wp, L0_cond2_bp, L0_cond2_Ws, L0_cond2_bs, L0_cond2_A_log, L0_cond2_dt_log, L0_cond2_Wo, L0_cond2_bo, L0_ffn_Wr, L0_ffn_br, L0_ffn_W1, L0_ffn_W2):
    import jax
    import jax.numpy as jnp

    def _L0_cond_ref(context_c, time_cond, gate_w, gate_b, time_w, time_b, ew1, eb1, ew2, eb2, sw1, sb1, sw2, sb2):
        import jax, jax.numpy as jnp
        import numpy as np
        NUM_EXPERTS = 4
        TOP_K = 2
        B, L, D = context_c.shape
        E, K = (NUM_EXPERTS, TOP_K)
        L_head = L_wrist = L // 3
        head = context_c[:, :L_head]
        wrist = context_c[:, L_head:L_head + L_wrist]
        proprio = context_c[:, L_head + L_wrist:]
        full_agg = context_c.mean(axis=1)
        hp_agg = jnp.concatenate([head, proprio], axis=1).mean(axis=1)
        wp_agg = jnp.concatenate([wrist, proprio], axis=1).mean(axis=1)
        gate_in = jnp.concatenate([full_agg, hp_agg, wp_agg], axis=-1)
        gate_logits = gate_in @ gate_w + gate_b
        mod = jax.nn.silu(time_cond) @ time_w + time_b
        scale, shift = jnp.split(mod, 2, axis=-1)
        gate_logits = gate_logits * (1.0 + scale) + shift
        gate_scores = jax.nn.softmax(gate_logits, axis=-1)
        topk_w, topk_i = jax.lax.top_k(gate_scores, K)
        topk_w = topk_w / (topk_w.sum(axis=-1, keepdims=True) + 1e-08)
        onehot = (topk_i[..., None] == jnp.arange(E)[None, None, :]).astype(context_c.dtype)
        w_be = jnp.sum(topk_w[..., None] * onehot, axis=1)
        mask = np.ones((E, L), dtype=np.float32)
        mask[1, L_head:L_head + L_wrist] = 0.0
        mask[2, :L_head] = 0.0
        mask = jnp.asarray(mask)
        out = jnp.zeros_like(context_c)
        for e in range(E):
            h = jax.nn.gelu(context_c @ ew1[e] + eb1[e], approximate=True)
            y = h @ ew2[e] + eb2[e]
            out = out + w_be[:, e][:, None, None] * mask[e][None, :, None] * y
        shared = jax.nn.gelu(context_c @ sw1 + sb1, approximate=True) @ sw2 + sb2
        return out + shared

    def _L0_attn_ref(x, w_qkv, w_proj):
        import jax, jax.numpy as jnp
        import numpy as np
        H = 16
        RMS_EPS = 1.1920928955078125e-07
        NORM_EPS = 1e-12

        def _rms_norm(t):
            ms = jnp.mean(t * t, axis=-1, keepdims=True)
            return t * jax.lax.rsqrt(ms + RMS_EPS)
        B, N, C = x.shape
        D = C // H
        scale = D ** (-0.5)
        qkv = x @ w_qkv.T
        qkv = qkv.reshape(B, N, 3, H, D)
        q = qkv[:, :, 0].transpose(0, 2, 1, 3)
        k = qkv[:, :, 1].transpose(0, 2, 1, 3)
        v = qkv[:, :, 2].transpose(0, 2, 1, 3)
        q = _rms_norm(q)
        k = _rms_norm(k)
        attn = jnp.einsum('bhnd,bhmd->bhnm', q, k) * scale
        attn = jax.nn.softmax(attn, axis=-1)
        y = jnp.einsum('bhnm,bhmd->bhnd', attn, v)
        vnorm = jnp.linalg.norm(v, axis=-1, keepdims=True)
        Vn = v / jnp.maximum(vnorm, NORM_EPS)
        y = y - jnp.sum(y * Vn, axis=-1, keepdims=True) * Vn
        out = y.transpose(0, 2, 1, 3).reshape(B, N, C)
        return out @ w_proj.T

    def _L0_cond2_ref(x, conv_w, conv_b, Wp, bp, Ws, bs, A_log, dt_log, Wo, bo):
        import jax, jax.numpy as jnp
        import numpy as np
        B, L, D = x.shape
        K = conv_w.shape[0]
        N = Ws.shape[1]
        x_pad = jnp.pad(x, ((0, 0), (K - 1, 0), (0, 0)))
        conv = conv_b + sum((x_pad[:, k:k + L, :] * conv_w[k, 0] for k in range(K)))
        proj = conv @ Wp + bp
        B_t = jax.nn.softplus(proj[..., :N])
        C_t = jnp.tanh(proj[..., N:])
        u = x @ Ws + bs
        A = -jax.nn.softplus(A_log)
        dt = jax.nn.softplus(dt_log)
        decay = 1.0 + dt * A

        def step(state, inputs):
            u_t, b_t, c_t = inputs
            state = decay * state + dt * b_t * u_t
            return (state, c_t * state)
        init = jnp.zeros((B, N), dtype=x.dtype)
        xs = tuple((jnp.swapaxes(a, 0, 1) for a in (u, B_t, C_t)))
        _, ys = jax.lax.scan(step, init, xs, unroll=4)
        y = jnp.swapaxes(ys, 0, 1)
        return y @ Wo + bo

    def _L0_ffn_ref(hidden_states, Wr, br, W1, W2):
        import jax, jax.numpy as jnp
        import numpy as np
        B, S, H, FFN, E = (2, 512, 256, 1024, 8)
        b, s, h = hidden_states.shape
        x = hidden_states.reshape(-1, h)
        route = jax.nn.sigmoid(x @ Wr + br)
        max_prob = jnp.max(route, axis=1, keepdims=True)
        max_ind = jnp.argmax(route, axis=1)
        out = jnp.zeros_like(x)
        n_experts = Wr.shape[1]
        for e in range(n_experts):
            mask = (max_ind == e)[:, None].astype(x.dtype)
            y = jax.nn.gelu(x @ W1[e], approximate=False) @ W2[e]
            out = out + mask * y
        out = out * max_prob
        return out.reshape(b, s, h)
    x = x + _L0_attn_ref(_L0_cond_ref(x, cond_1024, L0_cond_gate_w, L0_cond_gate_b, L0_cond_time_w, L0_cond_time_b, L0_cond_ew1, L0_cond_eb1, L0_cond_ew2, L0_cond_eb2, L0_cond_sw1, L0_cond_sb1, L0_cond_sw2, L0_cond_sb2), L0_attn_w_qkv, L0_attn_w_proj)
    x = x + _L0_ffn_ref(_L0_cond2_ref(x, cond_1024[:, None, :], L0_cond2_conv_b, L0_cond2_Wp, L0_cond2_bp, L0_cond2_Ws, L0_cond2_bs, L0_cond2_A_log, L0_cond2_dt_log, L0_cond2_Wo, L0_cond2_bo), L0_ffn_Wr, L0_ffn_br, L0_ffn_W1, L0_ffn_W2)
    return x

_drawn_inputs = setup_inputs


def setup_inputs(seed=0):
    import zlib

    import numpy as np

    out = dict(_drawn_inputs(seed))
    spreads = {'L0_cond_gate_b': (0.0, 2.0),
     'L0_cond_time_b': (0.0, 0.8),
     'L0_cond_eb1': (0.0, 0.552),
     'L0_cond_eb2': (0.0, 0.1),
     'L0_cond_sb1': (0.0, 0.368),
     'L0_cond_sb2': (0.0, 0.1),
     'L0_cond2_conv_b': (0.0, 0.484),
     'L0_cond2_bp': (0.0, 0.495),
     'L0_cond2_bs': (0.0, 0.376),
     'L0_cond2_bo': (0.0, 0.397),
     'L0_ffn_br': (0.0, 0.1)}
    factors = {'L0_cond_gate_w': 64.0,
     'L0_cond2_A_log': 22.126,
     'L0_cond2_dt_log': 8.0,
     'L0_cond_time_w': 6.092}
    for name, (base, spread) in spreads.items():
        noise = np.random.default_rng([zlib.crc32(name.encode()), seed]).standard_normal(out[name].shape)
        drawn = base * np.exp(spread * noise) if base else spread * noise
        out[name] = jnp.asarray(drawn.astype(out[name].dtype))
    for name, factor in factors.items():
        out[name] = (out[name] * factor).astype(out[name].dtype)
    return out
```

```python
from contextlib import ExitStack

import concourse.bass as bass
from concourse import mybir

F32 = mybir.dt.float32
F32R = mybir.dt.float32r
BF16 = mybir.dt.bfloat16
I32 = mybir.dt.int32
ALU = mybir.AluOpType
ACT = mybir.ActivationFunctionType
AX = mybir.AxisListType.X

P = 128
NB, L, C = 2, 1024, 256
CK = C // P
T = NB * L
LT = L // P
TT = T // P
FF = 1024
FC = FF // P
NE, TOPK = 4, 2
STEPS = NB * (1 + TOPK)
QUADS = STEPS * FC // 4
QB = QUADS // NB
H, D = 16, 16
HG = 4
GROUPS = NB * H // HG
VW = 32
N = 64
RE = 8
TILES = (T - RE) // P + RE
L3 = L // 3
REGION = [(0, L3), (L3, 2 * L3), (2 * L3, L)]
CUTS = [[(max(a, 512 * t) - 512 * t, min(z, 512 * t + 512) - 512 * t, r)
         for r, (a, z) in enumerate(REGION) if max(a, 512 * t) < min(z, 512 * t + 512)] for t in range(2)]
Q_PART = (0, 0, 1, 0, 2, 1)
K_PART = (0, 1, 0, 2, 0, 1)
TERMS = len(Q_PART)
RMS_EPS = 1.1920928955078125e-07
NORM_EPS = 1e-12


def layer_kernel(nc, a, out):
    with ExitStack() as ctx:
        def sem(name):
            return ctx.enter_context(nc.semaphore(name))

        base = -(-nc.sbuf_base // 64) * 64
        ARENA = 204 * 1024
        ctx.enter_context(nc.sbuf_tensor("arena", [P, ARENA // 4], F32))
        cursor = [base]

        def sb(name, shape, dt, at=None):
            size = 1
            for s in shape[1:]:
                size *= s
            size *= 2 if dt == BF16 else 4
            if at is None:
                at = cursor
            off = at[0]
            at[0] = off + -(-size // 32) * 32
            assert at[0] <= base + ARENA, (name, at[0] - base - ARENA)
            return nc.alloc_sbuf_tensor_at(name, shape, dt, offset=off)

        ident = sb("ident", [P, P], F32)
        x_tm = sb("x_tm", [P, TT, C], F32)
        v_tm = sb("v_tm", [P, TT, C], F32)
        projT = sb("projT", [P, CK, C], F32)
        cond_col = sb("cond_col", [P, CK, NB], F32)
        gate_rows = sb("gate_rows", [P, 3 * CK, NE], F32)
        time_rows = sb("time_rows", [P, CK, 2 * NE], F32)
        gate_bias = sb("gate_bias", [NB, NE], F32)
        time_bias = sb("time_bias", [NB, 2 * NE], F32)
        eb2_col = sb("eb2_col", [P, CK, NE], F32)
        sb2_col = sb("sb2_col", [P, CK], F32)
        b1_col = sb("b1_col", [P, STEPS * FC], F32)
        convb_col = sb("convb_col", [P, CK], F32)
        bp_b = sb("bp_b", [P, 1], F32)
        bp_c = sb("bp_c", [P, 1], F32)
        bs_col = sb("bs_col", [P, 1], F32)
        wp_sb = sb("wp_sb", [P, CK, 2 * N], F32)
        ws_sb = sb("ws_sb", [P, CK, N], F32)
        wo_sb = sb("wo_sb", [P, C], F32)
        bo_row = sb("bo_row", [P, C], F32)
        bo_col = sb("bo_col", [P, CK], F32)
        wr_sb = sb("wr_sb", [P, CK, RE], F32)
        br_row = sb("br_row", [P, RE], F32)
        region_mask = sb("region_mask", [P, LT, 3], F32)
        tri = sb("tri", [P, P], F32)
        ones = sb("ones", [P, P], F32)
        iota_e = sb("iota_e", [P, RE], F32)
        iota_tok = sb("iota_tok", [P, TT], F32)
        iota_tile = sb("iota_tile", [P, TILES], F32)
        pick_row = sb("pick_row", [NB, NB, P], F32)
        reg_sum = sb("reg_sum", [P, CK, NB, 3], F32)
        gate_in = sb("gate_in", [P, 3, CK, NB], F32)
        sil = sb("sil", [P, 3, CK, NB], F32)
        gs = sb("gs", [NB, 12, 8], F32)
        gsc = sb("gsc", [NB, 12], F32)
        picked = sb("picked", [P, NB, 8], F32)
        scale_col = sb("scale_col", [P, QUADS, 3], F32)
        eb2w = sb("eb2w", [P, CK, NB, NE], F32)
        bias_col = sb("bias_col", [P, CK, NB, 3], F32)
        expert_i = sb("expert_i", [1, NB, TOPK], I32)
        decay = sb("decay", [P, 7], F32)
        route = sb("route", [P, TT, RE], F32)
        prob = sb("prob", [P, TT], F32)
        slot_i = sb("slot_i", [P, TT], I32)
        tile_i = sb("tile_i", [P, TILES], I32)
        stage = cursor[0]

        at = [stage]
        qk_tm = sb("qk_tm", [P, TT, 2 * C], F32, at)
        after_qk = at[0]
        x_hi = sb("x_hi", [P, CK, T], F32R, at)
        x_lo = sb("x_lo", [P, CK, T], F32R, at)
        raw1 = [sb(f"raw1_{i}", [P, CK, 2 * P], F32, at) for i in range(2)]
        raw2 = [sb(f"raw2_{i}", [P, 2, C], F32, at) for i in range(2)]
        w1h = [sb(f"w1h_{i}", [P, CK, P], F32R, at) for i in range(4)]
        w1l = [sb(f"w1l_{i}", [P, CK, P], F32R, at) for i in range(4)]
        w2h = [sb(f"w2h_{i}", [P, C], F32R, at) for i in range(4)]
        w2l = [sb(f"w2l_{i}", [P, C], F32R, at) for i in range(4)]
        hid = [sb(f"hid_{i}", [P, 512], F32, at) for i in range(4)]
        hh = [sb(f"hh_{i}", [P, 512], F32R, at) for i in range(4)]
        hl = [sb(f"hl_{i}", [P, 512], F32R, at) for i in range(4)]
        y_hi = sb("y_hi", [P, CK, L], F32R, at)
        y_lo = sb("y_lo", [P, CK, L], F32R, at)
        wq_h = sb("wq_h", [P, CK, 3 * C], F32R, at)
        wq_l = sb("wq_l", [P, CK, 3 * C], F32R, at)
        qkv_raw = sb("qkv_raw", [P, 3 * CK, C], F32, [stage])
        proj_raw = sb("proj_raw", [P, CK, C], F32, [stage + 8192])
        zero_row = sb("zero_row", [P, C], F32, [stage + 16384])
        at = [after_qk]
        vn_tm = sb("vn_tm", [P, TT, C], F32, at)
        parts = [sb(f"parts_{i}", [P, 3, L], BF16, at) for i in range(2)]
        rest = [sb(f"rest_{i}", [P, 512], F32, at) for i in range(2)]
        after_parts = at[0]
        square = sb("square", [P, LT, 3 * C], F32, at)
        ssum = sb("ssum", [P, LT, 3 * H], F32, at)
        pexp = [sb(f"pexp_{i}", [P, HG, L], F32, [stage + i * 16384]) for i in range(2)]
        at = [after_parts]
        q_stack = [sb(f"q_stack_{i}", [TERMS * D, HG, L], BF16, at) for i in range(2)]
        k_stack = [sb(f"k_stack_{i}", [TERMS * D, HG, L], BF16, at) for i in range(2)]
        v_ones = [sb(f"v_ones_{i}", [P, LT, HG, VW], F32, at) for i in range(2)]
        yT = sb("yT", [P, L], F32, at)
        y_tm = sb("y_tm", [P, LT, HG, D], F32, at)
        y_dot = sb("y_dot", [P, LT, HG, D], F32, at)
        y_r = sb("y_r", [P, LT, HG], F32, at)
        y_d = sb("y_d", [P, LT, HG], F32, at)
        ctx_tm = sb("ctx_tm", [P, TT, C], F32, at)
        ctxT = [sb(f"ctxT_{i}", [P, 2, CK, P], F32, at) for i in range(2)]
        after_b = at[0]
        WE = 16384
        top = base + ARENA - RE * WE
        w_all = sb("w_all", [P, RE, CK * FF + FC * C], F32, [top])
        spare = (base + ARENA - after_b) // WE
        at = [stage]
        x2T = sb("x2T", [P, CK, T], F32, at)
        convT = sb("convT", [P, CK, T], F32, at)
        gate_b = sb("gate_b", [P, L], F32, at)
        gate_e = sb("gate_e", [P, L], F32, at)
        seq_u = sb("seq_u", [P, L], F32, at)
        gate_c = sb("gate_c", [P, L], F32, at)
        under_seq = -(-(at[0] - top) // WE)
        x3T = sb("x3T", [P, CK, T], F32, [stage])
        x3_tm = sb("x3_tm", [P, TT, C], F32, [stage + 16384])
        rt = [sb(f"rt_{i}", [P, TT, RE], F32, at) for i in range(9)]
        rk = [sb(f"rk_{i}", [P, RE, TT], F32, at) for i in range(2)]
        re = [sb(f"re_{i}", [P, RE], F32, at) for i in range(4)]
        tl = sb("tl", [P, TILES, RE], F32, at)
        tf = sb("tf", [P, TILES], F32, at)
        sl = sb("sl", [P, TT], F32, at)
        under_route = -(-(at[0] - top) // WE)
        at = [stage]
        xs = [sb(f"xs_{i}", [P, C], F32, at) for i in range(2)]
        xsT = [sb(f"xsT_{i}", [P, CK, P], F32, at) for i in range(2)]
        fh = [sb(f"fh_{i}", [P, FF], F32, at) for i in range(2)]
        fhT = [sb(f"fhT_{i}", [P, FC, P], F32, at) for i in range(2)]
        fo = [sb(f"fo_{i}", [P, C], F32, at) for i in range(2)]
        assert at[0] <= top
        ffn_tm = v_tm

        psum = ctx.enter_context(nc.psum_tensor("psum", [P, 8, 512], F32))

        def bank(i):
            return psum[:, i, :]

        parts_d = nc.dram_tensor("parts_d", [NB, 4, 3, P, L], BF16).ap()
        sorted_d = nc.dram_tensor("sorted_d", [TILES * P, C], F32).ap()
        ffn_d = nc.dram_tensor("ffn_d", [TILES * P, C], F32).ap()

        x_in = [sem(f"x_in{b}") for b in range(NB)]
        const_in = sem("const_in")
        wproj_in = sem("wproj_in")
        b1_in = sem("b1_in")
        consts_made = sem("consts_made")
        pool_step = sem("pool_step")
        setup_filled = sem("setup_filled")
        hi_out = sem("hi_out")
        lo_out = sem("lo_out")
        region_sums = sem("region_sums")
        gate_in_made = sem("gate_in_made")
        gate_logits = sem("gate_logits")
        gate_exp = sem("gate_exp")
        gate_step = sem("gate_step")
        gate_rows_made = sem("gate_rows_made")
        gate_wide = sem("gate_wide")
        experts_known = sem("experts_known")
        zero_filled = sem("zero_filled")
        act_passed = sem("act_passed")
        pool_passed = sem("pool_passed")
        raw_in = [sem(f"raw_in{i}") for i in range(2)]
        w_split = sem("w_split")
        w_part = sem("w_part")
        hid_made = sem("hid_made")
        gelu_done = sem("gelu_done")
        h_part = sem("h_part")
        h_split = sem("h_split")
        unit_done = sem("unit_done")
        y_part = sem("y_part")
        y_split = sem("y_split")
        qkv_made = sem("qkv_made")
        qkv_out = sem("qkv_out")
        squared = sem("squared")
        norm_step = sem("norm_step")
        var_made = sem("var_made")
        rooted = sem("rooted")
        normed = sem("normed")
        turned = sem("turned")
        part1 = sem("part1")
        part2 = sem("part2")
        rest1 = sem("rest1")
        part3 = sem("part3")
        parts_out = [sem(f"parts_out{i}") for i in range(2)]
        stack_in = [sem(f"stack_in{i}") for i in range(2)]
        v_ready = sem("v_ready")
        v_base = sem("v_base")
        scored = sem("scored")
        exp_done = sem("exp_done")
        av_done = sem("av_done")
        yT_out = sem("yT_out")
        y_turned = sem("y_turned")
        y_read = sem("y_read")
        post_step = sem("post_step")
        ctx_done = sem("ctx_done")
        ctx_turned = sem("ctx_turned")
        ctxT_out = sem("ctxT_out")
        proj_made = sem("proj_made")
        x2_done = sem("x2_done")
        x2_turned = sem("x2_turned")
        x2T_out = sem("x2T_out")
        conv_part = sem("conv_part")
        conv_done = sem("conv_done")
        seq_made = sem("seq_made")
        seq_step = sem("seq_step")
        decay_step = sem("decay_step")
        decay_step2 = sem("decay_step2")
        decay_e = sem("decay_e")
        neg_abs = sem("neg_abs")
        soft_log = sem("soft_log")
        soft_exp = sem("soft_exp")
        u_made = sem("u_made")
        tanh_done = sem("tanh_done")
        state_out = sem("state_out")
        x3T_made = sem("x3T_made")
        x3T_out = sem("x3T_out")
        x3_made = sem("x3_made")
        x3_out = sem("x3_out")
        logits_made = sem("logits_made")
        logits_out = sem("logits_out")
        route_done = sem("route_done")
        onehot_done = sem("onehot_done")
        ranks_made = sem("ranks_made")
        rstep = sem("rstep")
        slots_done = sem("slots_done")
        scattered = sem("scattered")
        expert_in = [sem(f"expert_in{e}") for e in range(RE)]
        xs_in = [sem(f"xs_in{i}") for i in range(2)]
        xs_turned = sem("xs_turned")
        xsT_out = sem("xsT_out")
        fh_made = sem("fh_made")
        fh_out = sem("fh_out")
        fh_turned = sem("fh_turned")
        fhT_act = sem("fhT_act")
        fhT_dve = sem("fhT_dve")
        fo_made = sem("fo_made")
        fo_out = sem("fo_out")
        fo_stored = [sem(f"fo_stored{i}") for i in range(2)]
        gathered = sem("gathered")
        scaled = sem("scaled")
        out_ready = sem("out_ready")
        out_stored = sem("out_stored")

        def wide(ap, axis, n):
            v = ap.unsqueeze(axis)
            shape = list(v.shape)
            shape[axis] = n
            return v.to_broadcast(shape)

        def after(eng, s, value):
            if not isinstance(value, int) or value > 0:
                eng.wait_ge(s, value)

        CONSTS = 28
        row = lambda ap: ap.rearrange("(a n) -> a n", a=1)
        col = lambda ap: ap.rearrange("(k p) -> p k", p=P)
        half = [slice(N * b, N * b + N) for b in range(NB)]

        block = ctx.enter_context(nc.Block())

        @block.sync
        def _(sp):
            for b in range(NB):
                sp.dma_start(x_tm[:, b * LT:(b + 1) * LT, :],
                             a["x"][b].rearrange("(i p) c -> p i c", p=P)).then_inc(x_in[b], 16)
            sp.dma_start(qkv_raw[:], a["w_qkv"].rearrange("(r p) c -> p r c", p=P)).then_inc(wproj_in, 16)
            sp.dma_start(proj_raw[:], a["w_proj"].rearrange("(r p) c -> p r c", p=P)).then_inc(wproj_in, 16)

            chosen = {}

            def load_pair(s, i, k):
                n = 4 * s + 2 * i + k
                after(sp, w_split, 2 * n - 2)
                f0 = (2 * i + k) * 2 * P
                if s % 3 == 0:
                    w1, w2 = a["sw1"], a["sw2"]
                else:
                    e = chosen[s]
                    w1 = a["ew1"][bass.ds(e, 1), :, :].rearrange("e c f -> (e c) f")
                    w2 = a["ew2"][bass.ds(e, 1), :, :].rearrange("e f c -> (e f) c")
                sp.dma_start(raw1[k][:], w1.rearrange("(k p) f -> p k f", p=P)[:, :, bass.ds(f0, 2 * P)])\
                    .then_inc(raw_in[k], 16)
                sp.dma_start(raw2[k][:], w2.rearrange("(f p) c -> p f c", p=P)[:, bass.ds(f0 // P, 2), :])\
                    .then_inc(raw_in[k], 16)

            sp.dma_start(b1_col[:, 0:FC], col(a["sb1"]),
                         allow_slow_non_contiguous=True).then_inc(b1_in, 16)
            for s in range(STEPS):
                if s == 1:
                    sp.wait_ge(experts_known, 1)
                    sp.wait_ge(zero_filled, 1)
                    sp.dma_start(sorted_d.rearrange("(s p) c -> p s c", p=P),
                                 wide(zero_row[:], 1, TILES)).then_inc(zero_filled, 16)
                    for s1 in range(1, STEPS):
                        src = a["sb1"]
                        if s1 % 3:
                            b, k = s1 // 3, s1 % 3 - 1
                            chosen[s1] = sp.value_load(expert_i[0:1, b, k:k + 1], min_val=0, max_val=NE - 1)
                            src = a["eb1"][bass.ds(chosen[s1], 1), :].rearrange("e f -> (e f)")
                        sp.dma_start(b1_col[:, s1 * FC:(s1 + 1) * FC], col(src),
                                     allow_slow_non_contiguous=True).then_inc(b1_in, 16)
                for i in range(2):
                    for k in range(2):
                        load_pair(s, i, k)

            for b in range(NB):
                for k in range(4):
                    u = 4 * b + k
                    sp.wait_ge(part3, 2 * u + 2)
                    sp.dma_start(parts_d[b, k].rearrange("s p n -> p s n"), parts[u % 2][:])\
                        .then_inc(parts_out[u % 2], 16)

            def load_stacks(g):
                b, hg = g // (H // HG), g % (H // HG)
                cq = hg // 2
                r = slice(HG * D * (hg % 2), HG * D * (hg % 2) + HG * D)
                if g >= 2:
                    sp.wait_ge(scored, HG * LT * (g - 1))
                for kk, (stack, order) in enumerate(((q_stack, Q_PART), (k_stack, K_PART))):
                    if g < 2 or hg % 2 == 0:
                        u = 4 * b + cq + 2 * kk
                        sp.wait_ge(parts_out[u % 2], 16 * (u // 2 + 1))
                    for t, s in enumerate(order):
                        sp.dma_start(stack[g % 2][D * t:D * t + D, :, :],
                                     parts_d[b, cq + 2 * kk, s, r, :].rearrange("(j d) n -> d j n", j=HG))\
                            .then_inc(stack_in[g % 2], 16)

            def load_expert(e):
                at_e = w_all[:, RE - 1 - e, :]
                sp.dma_start(at_e[:, 0:CK * FF].rearrange("p (k f) -> p k f", k=CK),
                             a["W1"][e].rearrange("(k p) f -> p k f", p=P)).then_inc(expert_in[e], 16)
                sp.dma_start(at_e[:, CK * FF:].rearrange("p (f c) -> p f c", f=FC),
                             a["W2"][e].rearrange("(f p) c -> p f c", p=P)).then_inc(expert_in[e], 16)

            for g in range(GROUPS):
                load_stacks(g)
                if g == 1:
                    for e in range(spare):
                        load_expert(e)
            sp.wait_ge(proj_made, TT // 2)
            sp.wait_ge(ctxT_out, TT // 2)
            for e in range(spare, RE - under_route):
                load_expert(e)
            sp.wait_ge(slots_done, 2)
            sp.wait_ge(x3_made, TT // 2)
            for e in range(RE - under_route, RE):
                load_expert(e)

            sp.wait_ge(scattered, 16 * TT)

            def load_tile(s, i):
                after(sp, xs_turned, s - 1)
                sp.dma_start(xs[i][:], sorted_d[bass.ds(s * P, P), :]).then_inc(xs_in[i], 16)

            def store_tile(s, i):
                sp.wait_ge(fo_out, s + 1)
                sp.dma_start(ffn_d[bass.ds(s * P, P), :], fo[i][:]).then_inc(fo_stored[i], 16)

            load_tile(0, 0)
            load_tile(1, 1)
            store_tile(0, 0)
            with sp.Fori(1, TILES - 2, 2) as s:
                load_tile(s + 1, 0)
                store_tile(s, 1)
                load_tile(s + 2, 1)
                store_tile(s + 1, 0)
            load_tile(TILES - 1, 0)
            store_tile(TILES - 2, 1)
            store_tile(TILES - 1, 0)
            for b in range(NB):
                sp.wait_ge(out_ready, b + 1)
                sp.dma_start(out[b].rearrange("(i p) c -> p i c", p=P), ffn_tm[:, b * LT:(b + 1) * LT, :])\
                    .then_inc(out_stored, 16)
            sp.wait_ge(out_stored, 16 * NB)
            sp.wait_ge(zero_filled, 17)

        @block.gpsimd
        def _(pool):
            steps = [0]

            def link(ins):
                steps[0] += 1
                ins.then_inc(pool_step, 1)
                pool.wait_ge(pool_step, steps[0])

            pool.memset(ident[:], 0.0)
            pool.memset(ones[:], 1.0)
            pool.memset(tri[:], 1.0)
            pool.memset(region_mask[:], 1.0)
            link(pool.memset(pick_row[:], 0.0))
            pool.affine_select(out=ident[:], in_=ident[:], compare_op=ALU.not_equal, fill=1.0, base=0,
                               pattern=[[-1, P]], channel_multiplier=1)
            pool.affine_select(out=tri[:], in_=tri[:], compare_op=ALU.is_gt, fill=0.0, base=0,
                               pattern=[[1, P]], channel_multiplier=-1)
            pool.affine_select(out=pick_row[:], in_=pick_row[:], compare_op=ALU.not_equal, fill=1.0, base=0,
                               pattern=[[-1, NB], [0, P]], channel_multiplier=1)
            for r, (first, last) in enumerate(REGION):
                link(pool.affine_select(out=region_mask[:, :, r], in_=region_mask[:, :, r],
                                        compare_op=ALU.is_ge, fill=0.0, base=last - 1,
                                        pattern=[[-P, LT]], channel_multiplier=-1))
            for r, (first, last) in enumerate(REGION):
                pool.affine_select(out=region_mask[:, :, r], in_=region_mask[:, :, r],
                                   compare_op=ALU.is_ge, fill=0.0, base=-first,
                                   pattern=[[P, LT]], channel_multiplier=1)
            pool.iota(iota_e[:], pattern=[[1, RE]], base=0, channel_multiplier=0,
                      allow_small_or_imprecise_dtypes=True)
            pool.iota(iota_tok[:], pattern=[[P, TT]], base=0, channel_multiplier=0,
                      allow_small_or_imprecise_dtypes=True)
            pool.iota(iota_tile[:], pattern=[[1, TILES]], base=0, channel_multiplier=0,
                      allow_small_or_imprecise_dtypes=True).then_inc(consts_made, 1)
            pool.memset(zero_row[:], 0.0).then_inc(zero_filled, 1)

            def split_quad(q):
                for k in range(4):
                    u = 4 * q + k
                    pair, j = k // 2, k % 2
                    if j == 0:
                        pool.wait_ge(raw_in[pair], 32 * (q + 1))
                    after(pool, unit_done, 2 * u - 6)
                    pool.sem_inc(pool_passed, 1)
                    r1, r2 = raw1[pair][:, :, j * P:(j + 1) * P], raw2[pair][:, j, :]
                    pool.tensor_copy(w1h[k][:], r1)
                    pool.tensor_copy(w2h[k][:], r2).then_inc(w_part, 1)
                    pool.wait_ge(w_part, u + 1)
                    pool.tensor_tensor(w1l[k][:], r1, w1h[k][:].bitcast(F32), ALU.subtract)
                    pool.tensor_tensor(w2l[k][:], r2, w2h[k][:].bitcast(F32), ALU.subtract)\
                        .then_inc(w_split, 1)

            split_quad(0)
            with pool.Fori(1, QUADS) as q:
                split_quad(q)

            pool.wait_ge(normed, 2)
            for i in range(2):
                pool.memset(v_ones[i][:, :, :, D:VW], 0.0).then_inc(v_base, 1)
            for i in range(2):
                pool.wait_ge(v_base, i + 1)
                pool.memset(v_ones[i][:, :, :, D:D + 1], 1.0).then_inc(v_base, 1)
            for g in range(GROUPS):
                b, hg = g // (H // HG), g % (H // HG)
                if g >= 2:
                    pool.wait_ge(av_done, LT * (g - 1))
                else:
                    pool.wait_ge(v_base, 3 + g)
                pool.tensor_copy(v_ones[g % 2][:, :, :, 0:D],
                                 v_tm[:, b * LT:(b + 1) * LT, hg * HG * D:(hg + 1) * HG * D]
                                 .rearrange("p i (j d) -> p i j d", j=HG)).then_inc(v_ready, 1)

            pool.wait_ge(zero_filled, 17)
            pool.wait_ge(slots_done, 1)
            pool.wait_ge(x3_out, TT // 2)
            for i in range(TT):
                pool.indirect_dma_start(out=sorted_d[:, :],
                                        out_offset=bass.IndirectOffsetOnAxis(ap=slot_i[:, i:i + 1], axis=0),
                                        in_=x3_tm[:, i, :], in_offset=None,
                                        bounds_check=TILES * P - 1).then_inc(scattered, 16)
            for i in range(2):
                pool.wait_ge(fo_stored[i], 16 * ((TILES + 1 - i) // 2))
            for i in range(TT):
                pool.indirect_dma_start(out=ffn_tm[:, i, :], out_offset=None, in_=ffn_d[:, :],
                                        in_offset=bass.IndirectOffsetOnAxis(ap=slot_i[:, i:i + 1], axis=0),
                                        bounds_check=TILES * P - 1).then_inc(gathered, 16)

        @block.scalar
        def _(act):
            for dst, src in ((cond_col[:, 0, :], a["cond"][:, 0:P].rearrange("b p -> p b")),
                             (cond_col[:, 1, :], a["cond"][:, P:C].rearrange("b p -> p b")),
                             (gate_rows[:], a["gate_w"].rearrange("(r p) e -> p r e", p=P)),
                             (time_rows[:], a["time_w"].rearrange("(r p) e -> p r e", p=P)),
                             (gate_bias[:], a["gate_b"].partition_broadcast(NB)),
                             (time_bias[:], a["time_b"].partition_broadcast(NB)),
                             (eb2_col[:, 0, :], a["eb2"][:, 0:P].rearrange("e p -> p e")),
                             (eb2_col[:, 1, :], a["eb2"][:, P:C].rearrange("e p -> p e")),
                             (sb2_col[:], col(a["sb2"])),
                             (convb_col[:], col(a["conv_b"])),
                             (bo_col[:], col(a["bo"])),
                             (bo_row[:], a["bo"].partition_broadcast(P)),
                             (wp_sb[:], a["Wp"].rearrange("(k p) n -> p k n", p=P)),
                             (ws_sb[:], a["Ws"].rearrange("(k p) n -> p k n", p=P)),
                             (wr_sb[:], a["Wr"].rearrange("(k p) e -> p k e", p=P)),
                             (br_row[:], a["br"].partition_broadcast(P))):
                act.dma_start(dst, src, allow_slow_non_contiguous=True).then_inc(const_in, 16)
            for b in range(NB):
                h = half[b]
                one = lambda ap: ap.rearrange("(n a) -> n a", a=1)
                for dst, src in ((wo_sb[h, :], a["Wo"]), (bp_b[h, :], one(a["bp"][0:N])),
                                 (bp_c[h, :], one(a["bp"][N:2 * N])), (bs_col[h, :], one(a["bs"])),
                                 (decay[h, 0:1], one(a["A_log"])), (decay[h, 1:2], one(a["dt_log"]))):
                    act.dma_start(dst, src, allow_slow_non_contiguous=True).then_inc(const_in, 16)

            def hi_parts(m):
                act.wait_ge(setup_filled, m + 1)
                b, src = m % 8, bank(m % 8)
                if m < 8:
                    dst = x_hi[:, m % 2, 512 * (m // 2):512 * (m // 2) + 512]
                elif m < 10:
                    dst = wq_h[:, m - 8, 0:512]
                else:
                    src = src.rearrange("p (k r) -> p k r", k=CK)
                    dst = wq_h[:, :, 512:768] if m == 10 else projT[:]
                act.copy(dst, src).then_inc(hi_out, 1)

            for m in range(12):
                hi_parts(m)
            act.wait_ge(const_in, 16 * CONSTS)
            act.activation(sil[:, 0], cond_col[:], ACT.Exp, scale=-1.0).then_inc(gate_exp, 1)
            act.wait_ge(decay_step, 2)
            act.activation(decay[:, 2:4], decay[:, 2:4], ACT.Exp).then_inc(decay_e, 1)
            act.wait_ge(gate_logits, 2)
            act.activation(gs[:, 6, 0:NE], gs[:, 5, 0:NE], ACT.Exp).then_inc(gate_exp, 1)
            act.wait_ge(decay_e, 1)
            act.activation(decay[:, 2:4], decay[:, 2:4], ACT.Ln, bias=1.0).then_inc(decay_e, 1)


            def gelu_quad(q):
                for k in range(8):
                    v = 8 * q + k
                    act.wait_ge(hid_made, v + 1)
                    after(act, h_split, v - 3)
                    act.sem_inc(act_passed, 1)
                    act.activation(hid[k % 4][:], bank(k % 4), ACT.Gelu_apprx_tanh,
                                   bias=b1_col[:, bass.ds(4 * q + k // 2, 1)]).then_inc(gelu_done, 1)

            def qkv_to_sbuf(b):
                for i in range(LT):
                    act.wait_ge(qkv_made, b * LT + i + 1)
                    act.copy(qk_tm[:, b * LT + i, :], bank(2 * i % 4))
                    act.copy(v_tm[:, b * LT + i, :], bank((2 * i + 1) % 4)[:, 0:C]).then_inc(qkv_out, 1)

            act.wait_ge(b1_in, 16)
            gelu_quad(0)
            gelu_quad(1)
            act.wait_ge(b1_in, 16 * STEPS)
            with act.Fori(2, QB) as q:
                gelu_quad(q)
            act.wait_ge(zero_filled, 17)
            qkv_to_sbuf(0)
            with act.Fori(QB, QUADS) as q:
                gelu_quad(q)
            qkv_to_sbuf(1)

            act.wait_ge(qkv_out, TT)
            for b in range(NB):
                r = slice(b * LT, (b + 1) * LT)
                after(act, var_made, b)
                act.activation(square[:, :, 0:2 * C], qk_tm[:, r, :], ACT.Square)
                act.activation(square[:, :, 2 * C:], v_tm[:, r, :], ACT.Square).then_inc(squared, 1)
                act.wait_ge(var_made, b + 1)
                act.activation(ssum[:], ssum[:], ACT.Sqrt).then_inc(rooted, 1)

            def part_two(w):
                act.wait_ge(rest1, w + 1)
                act.copy(parts[w // 2 % 2][:, 1, 512 * (w % 2):512 * (w % 2) + 512], rest[w % 2][:])\
                    .then_inc(part2, 1)

            UNITS = NB * 8
            for w in range(UNITS):
                act.wait_ge(turned, w + 1)
                after(act, parts_out[w // 2 % 2], 16 * (w // 4))
                act.copy(parts[w // 2 % 2][:, 0, 512 * (w % 2):512 * (w % 2) + 512], bank(w % 4))\
                    .then_inc(part1, 1)
                if w:
                    part_two(w - 1)
            part_two(UNITS - 1)

            def exps(g):
                for u in range(HG * LT):
                    mt, j = u // HG, u % HG
                    r = (u + (u >= 16)) % 3
                    act.wait_ge(scored, HG * LT * g + u + 1)
                    if j == 0:
                        after(act, av_done, LT * g + mt - 1)
                    act.activation(pexp[mt % 2][:, j, :].rearrange("p (h n) -> p h n", h=2),
                                   psum[:, 2 * r:2 * r + 2, :], ACT.Exp, scale=D ** -0.5)\
                        .then_inc(exp_done, 1)

            exps(0)
            with act.Fori(1, GROUPS) as g:
                exps(g)

            for w in range(TT // 2):
                act.wait_ge(ctx_turned, w + 1)
                after(act, proj_made, w - 1)
                act.copy(ctxT[w % 2][:].rearrange("p i k n -> p (i k n)"), bank(w % 2))\
                    .then_inc(ctxT_out, 1)
            for w in range(TT // 2):
                act.wait_ge(x2_turned, w + 1)
                act.copy(x2T[:, w % 2, 512 * (w // 2):512 * (w // 2) + 512], bank(4 + w % 4))\
                    .then_inc(x2T_out, 1)

            for n in range(2):
                c = slice(512 * n, 512 * n + 512)
                act.wait_ge(seq_made, 3 * n + 3)
                act.activation(gate_c[:, c], bank(4 + n), ACT.Tanh, bias=bp_c[:, 0:1]).then_inc(tanh_done, 1)
            for n in range(2):
                c = slice(512 * n, 512 * n + 512)
                act.wait_ge(neg_abs, n + 1)
                act.activation(gate_e[:, c], gate_e[:, c], ACT.Exp).then_inc(soft_exp, 1)
            for n in range(2):
                c = slice(512 * n, 512 * n + 512)
                act.wait_ge(soft_exp, n + 1)
                act.activation(gate_e[:, c], gate_e[:, c], ACT.Ln, bias=1.0).then_inc(soft_log, 1)
            for w in range(8):
                act.wait_ge(x3T_made, w + 1)
                act.activation(x3T[:, w % 2, 512 * (w // 2):512 * (w // 2) + 512], bank(w % 4), ACT.Identity,
                               bias=bo_col[:, w % 2:w % 2 + 1]).then_inc(x3T_out, 1)
            act.wait_ge(logits_out, 1)
            act.activation(route[:], route[:], ACT.Sigmoid).then_inc(route_done, 1)

            def gelu_tile(s, i):
                act.wait_ge(fh_made, s + 1)
                after(act, fh_turned, s - 1)
                act.activation(fh[i][:].rearrange("p (h n) -> p h n", h=2), psum[:, 2 * i:2 * i + 2, :],
                               ACT.Gelu).then_inc(fh_out, 1)

            def turn_tile(s, i):
                act.wait_ge(fh_turned, s + 1)
                after(act, fo_made, s - 1)
                act.copy(fhT[i][:, 0:4, :].rearrange("p f n -> p (f n)"), bank(4)).then_inc(fhT_act, 1)

            act.wait_ge(scattered, 16 * TT)
            gelu_tile(0, 0)
            turn_tile(0, 0)
            with act.Fori(1, TILES, 2) as s:
                gelu_tile(s, 1)
                turn_tile(s, 1)
                gelu_tile(s + 1, 0)
                turn_tile(s + 1, 0)

        @block.vector
        def _(dve):
            def chain(s):
                n = [0]

                def link(ins, *also):
                    n[0] += 1
                    ins.then_inc(s, 1)
                    dve.wait_ge(s, n[0])
                return link

            def stt(out, in0, scalar, in1, op0, op1):
                return dve.scalar_tensor_tensor(out=out, in0=in0, scalar=scalar, in1=in1, op0=op0, op1=op1)

            dve.wait_ge(const_in, 16 * CONSTS)
            dve.tensor_scalar(decay[:, 2:4], decay[:, 0:2], -1.0, None, ALU.mult).then_inc(decay_step, 1)
            dve.wait_ge(decay_step, 1)
            dve.tensor_tensor(decay[:, 2:4], decay[:, 2:4], decay[:, 0:2], ALU.min).then_inc(decay_step, 1)

            for m in range(11):
                dve.wait_ge(hi_out, m + 1)
                src = bank(m % 8)
                if m < 8:
                    c = slice(512 * (m // 2), 512 * (m // 2) + 512)
                    dst, hi = x_lo[:, m % 2, c], x_hi[:, m % 2, c]
                elif m < 10:
                    dst, hi = wq_l[:, m - 8, 0:512], wq_h[:, m - 8, 0:512]
                else:
                    src = src.rearrange("p (k r) -> p k r", k=CK)
                    dst, hi = wq_l[:, :, 512:768], wq_h[:, :, 512:768]
                dve.tensor_tensor(dst, src, hi.bitcast(F32), ALU.subtract).then_inc(lo_out, 1)

            link = chain(gate_step)
            dve.wait_ge(gate_exp, 1)
            link(dve.tensor_scalar(sil[:, 1], sil[:, 0], 1.0, None, ALU.add))
            link(dve.reciprocal(sil[:, 0], sil[:, 1]))
            link(dve.tensor_tensor(sil[:, 2], sil[:, 0], cond_col[:], ALU.mult))
            dve.wait_ge(region_sums, 1)
            link(dve.tensor_copy(reg_sum[:], bank(4)[:, 0:12].rearrange("p (k b r) -> p k b r", k=CK, b=NB)))
            part = [reg_sum[:, :, :, r] for r in range(3)]
            link(dve.tensor_tensor(gate_in[:, 1], part[0], part[2], ALU.add))
            link(dve.tensor_tensor(gate_in[:, 0], gate_in[:, 1], part[1], ALU.add))
            link(dve.tensor_tensor(gate_in[:, 2], part[1], part[2], ALU.add))
            link(dve.tensor_scalar(gate_in[:, 0], gate_in[:, 0], 1.0 / L, None, ALU.mult))
            dve.tensor_scalar(gate_in[:, 1:3], gate_in[:, 1:3], 1.0 / (L - L3), None, ALU.mult)\
                .then_inc(gate_in_made, 1)
            dve.wait_ge(gate_logits, 1)
            link(dve.tensor_tensor(gs[:, 0, 0:NE], bank(5)[0:NB, 0:NE], gate_bias[:], ALU.add))
            link(dve.tensor_tensor(gs[:, 1, :], bank(5)[0:NB, 8:16], time_bias[:], ALU.add))
            link(dve.tensor_scalar(gs[:, 2, 0:NE], gs[:, 1, 0:NE], 1.0, None, ALU.add))
            link(dve.tensor_tensor(gs[:, 3, 0:NE], gs[:, 0, 0:NE], gs[:, 2, 0:NE], ALU.mult))
            link(dve.tensor_tensor(gs[:, 4, 0:NE], gs[:, 3, 0:NE], gs[:, 1, NE:2 * NE], ALU.add))
            link(dve.tensor_reduce(gsc[:, 0:1], gs[:, 4, 0:NE], AX, ALU.max))
            dve.tensor_scalar(gs[:, 5, 0:NE], gs[:, 4, 0:NE], gsc[:, 0:1], None, ALU.subtract)\
                .then_inc(gate_logits, 1)
            dve.wait_ge(gate_exp, 2)
            link(dve.tensor_reduce(gsc[:, 1:2], gs[:, 6, 0:NE], AX, ALU.add))
            link(dve.reciprocal(gsc[:, 2:3], gsc[:, 1:2]))
            link(dve.tensor_scalar(gs[:, 7, 0:NE], gs[:, 6, 0:NE], gsc[:, 2:3], None, ALU.mult))
            for k in range(TOPK):
                left = gs[:, 7 if k == 0 else 10, 0:NE]
                link(dve.tensor_reduce(gsc[:, 3 + k:4 + k], left, AX, ALU.max))
                link(dve.tensor_scalar(gs[:, 11, 0:NE], left, gsc[:, 3 + k:4 + k], None, ALU.is_equal))
                link(stt(gs[:, 11, 0:NE], gs[:, 11, 0:NE], -8.0, iota_e[0:NB, 0:NE], ALU.mult, ALU.add))
                link(dve.tensor_reduce(gsc[:, 5 + k:6 + k], gs[:, 11, 0:NE], AX, ALU.min))
                link(dve.tensor_scalar(gs[:, 8 + k, 0:NE], gs[:, 11, 0:NE], gsc[:, 5 + k:6 + k], None,
                                       ALU.is_equal))
                if k == 0:
                    link(stt(gs[:, 10, 0:NE], gs[:, 8, 0:NE], -2.0, left, ALU.mult, ALU.add))
            link(dve.tensor_scalar(gsc[:, 7:8], gsc[:, 3:4], gsc[:, 4:5], 1e-8, ALU.add, ALU.add))
            link(dve.reciprocal(gsc[:, 8:9], gsc[:, 7:8]))
            link(dve.tensor_scalar(gs[:, 5, 0:2], gsc[:, 3:5], gsc[:, 8:9], None, ALU.mult))
            link(dve.tensor_scalar(gs[:, 5, 2:4], gsc[:, 5:7], 8.0, None, ALU.add))
            link(dve.tensor_scalar(gs[:, 10, 0:NE], gs[:, 8, 0:NE], gs[:, 5, 0:1], None, ALU.mult))
            stt(gs[:, 5, 4:8], gs[:, 9, 0:NE], gs[:, 5, 1:2], gs[:, 10, 0:NE], ALU.mult, ALU.add)\
                .then_inc(gate_rows_made, 1)
            dve.wait_ge(gate_wide, 1)
            link(dve.tensor_copy(picked[:].rearrange("p b n -> p (b n)"), bank(6)[:, 0:16]))
            dve.tensor_copy(expert_i[:], picked[0:1, :, 2:4]).then_inc(experts_known, 1)
            link(dve.memset(scale_col[:], 1.0))
            by_pass = scale_col[:].rearrange("p (b j q) r -> p b j q r", b=NB, j=3)
            for q in range(2):
                for r, left_out in ((0, 2.0), (1, 1.0)):
                    stt(by_pass[:, :, 1:3, q, r], picked[:, :, 2:4], left_out, picked[:, :, 0:2],
                        ALU.not_equal, ALU.mult)
                dve.tensor_copy(by_pass[:, :, 1:3, q, 2], picked[:, :, 0:2])
            link(dve.tensor_tensor(eb2w[:], wide(eb2_col[:], 2, NB), wide(picked[:, :, 4:8], 1, CK), ALU.mult))
            of = [eb2w[:, :, :, e] for e in range(NE)]
            bias = [bias_col[:, :, :, r] for r in range(3)]
            link(dve.tensor_tensor(bias[2], of[0], of[3], ALU.add))
            link(dve.tensor_tensor(bias[0], bias[2], of[1], ALU.add))
            link(dve.tensor_tensor(bias[1], bias[2], of[2], ALU.add))
            link(dve.tensor_tensor(bias[2], bias[0], of[2], ALU.add))
            for b in range(NB):
                link(dve.tensor_tensor(bias_col[:, :, b, :], bias_col[:, :, b, :], wide(sb2_col[:], 2, 3),
                                       ALU.add))

            def split_quad(q):
                for k in range(8):
                    v = 8 * q + k
                    dve.wait_ge(gelu_done, v + 1)
                    after(dve, unit_done, v - 3)
                    cuts = CUTS[k % 2]
                    w = [scale_col[:, bass.ds(q, 1), r].rearrange("p q -> p q") for r in range(3)]
                    for n, (x0, x1, r) in enumerate(cuts):
                        ins = dve.tensor_scalar(hh[k % 4][:, x0:x1], hid[k % 4][:, x0:x1], w[r], None, ALU.mult)
                    ins.then_inc(h_part, 1)
                    dve.wait_ge(h_part, v + 1)
                    for n, (x0, x1, r) in enumerate(cuts):
                        ins = stt(hl[k % 4][:, x0:x1], hid[k % 4][:, x0:x1], w[r],
                                  hh[k % 4][:, x0:x1].bitcast(F32), ALU.mult, ALU.subtract)
                    ins.then_inc(h_split, 1)

            def y_out(b):
                dve.wait_ge(unit_done, (b + 1) * 2 * 3 * FC)
                after(dve, qkv_made, b * LT)
                for n in range(4):
                    t, c = n // 2, n % 2
                    y = bank(4 + n)
                    for x0, x1, r in CUTS[t]:
                        ins = dve.tensor_scalar(y_hi[:, c, 512 * t + x0:512 * t + x1], y[:, x0:x1],
                                                bias_col[:, c, b, r:r + 1], None, ALU.add)
                    ins.then_inc(y_part, 1)
                for n in range(4):
                    t, c = n // 2, n % 2
                    y = bank(4 + n)
                    dve.wait_ge(y_part, 4 * b + n + 1)
                    for x0, x1, r in CUTS[t]:
                        ins = stt(y_lo[:, c, 512 * t + x0:512 * t + x1], y[:, x0:x1],
                                  bias_col[:, c, b, r:r + 1],
                                  y_hi[:, c, 512 * t + x0:512 * t + x1].bitcast(F32), ALU.add, ALU.subtract)
                    ins.then_inc(y_split, 1)

            split_quad(0)
            with dve.Fori(1, QB) as q:
                split_quad(q)
            y_out(0)
            with dve.Fori(QB, QUADS) as q:
                split_quad(q)
            y_out(1)

            link = chain(norm_step)
            for b in range(NB):
                r = slice(b * LT, (b + 1) * LT)
                dve.wait_ge(squared, b + 1)
                after(dve, normed, b)
                link(dve.tensor_reduce(ssum[:], square[:].rearrange("p i (h d) -> p i h d", d=D), AX, ALU.add))
                dve.tensor_scalar(ssum[:, :, 0:2 * H], ssum[:, :, 0:2 * H], 1.0 / D, RMS_EPS, ALU.mult, ALU.add)\
                    .then_inc(var_made, 1)
                dve.wait_ge(rooted, b + 1)
                link(dve.tensor_scalar(ssum[:, :, 2 * H:], ssum[:, :, 2 * H:], NORM_EPS, None, ALU.max))
                link(dve.reciprocal(ssum[:], ssum[:]))
                for n in range(2):
                    qk = qk_tm[:, r, n * C:(n + 1) * C].rearrange("p i (h d) -> p i h d", d=D)
                    dve.tensor_tensor(qk, qk, wide(ssum[:, :, n * H:(n + 1) * H], 3, D), ALU.mult)
                dve.tensor_tensor(vn_tm[:, r, :].rearrange("p i (h d) -> p i h d", d=D),
                                  v_tm[:, r, :].rearrange("p i (h d) -> p i h d", d=D),
                                  wide(ssum[:, :, 2 * H:], 3, D), ALU.mult).then_inc(normed, 1)

            def part_three(w):
                dve.wait_ge(part2, w + 1)
                c = slice(512 * (w % 2), 512 * (w % 2) + 512)
                dve.tensor_tensor(parts[w // 2 % 2][:, 2, c], rest[w % 2][:], parts[w // 2 % 2][:, 1, c],
                                  ALU.subtract).then_inc(part3, 1)

            UNITS = NB * 8
            for w in range(UNITS):
                dve.wait_ge(part1, w + 1)
                c = slice(512 * (w % 2), 512 * (w % 2) + 512)
                after(dve, part3, w - 1)
                dve.tensor_tensor(rest[w % 2][:], bank(w % 4), parts[w // 2 % 2][:, 0, c], ALU.subtract)\
                    .then_inc(rest1, 1)
                if w:
                    part_three(w - 1)
            part_three(UNITS - 1)

            def finish_group(b, hg):
                g = (H // HG) * b + hg
                dve.wait_ge(av_done, LT * (g + 1))
                after(dve, ctx_done, g)
                after(dve, y_turned, g)
                dve.tensor_copy(yT[:].rearrange("p (h n) -> p h n", h=2), psum[:, 6:8, :]).then_inc(yT_out, 1)
                dve.wait_ge(y_turned, g + 1)
                y = psum[:, 2:4, :].rearrange("p h (i j d) -> p (h i) j d", j=HG, d=VW)
                dve.reciprocal(y_r[:], y[:, :, :, D]).then_inc(post_step, 1)
                dve.wait_ge(post_step, 4 * g + 1)
                vn = vn_tm[:, bass.ds(b * LT, LT), bass.ds(hg * HG * D, HG * D)].rearrange(
                    "p i (j d) -> p i j d", d=D)
                dve.tensor_tensor(y_tm[:], y[:, :, :, 0:D], wide(y_r[:], 3, D), ALU.mult).then_inc(y_read, 1)
                dve.wait_ge(y_read, g + 1)
                dve.tensor_tensor(y_dot[:], y_tm[:], vn, ALU.mult).then_inc(post_step, 1)
                dve.wait_ge(post_step, 4 * g + 2)
                dve.tensor_reduce(y_d[:], y_dot[:], AX, ALU.add).then_inc(post_step, 1)
                dve.wait_ge(post_step, 4 * g + 3)
                dve.tensor_tensor(y_dot[:], vn, wide(y_d[:], 3, D), ALU.mult).then_inc(post_step, 1)
                dve.wait_ge(post_step, 4 * g + 4)
                dve.tensor_tensor(ctx_tm[:, bass.ds(b * LT, LT), bass.ds(hg * HG * D, HG * D)].rearrange(
                    "p i (j d) -> p i j d", d=D), y_tm[:], y_dot[:], ALU.subtract).then_inc(ctx_done, 1)

            finish_group(0, 0)
            with dve.Fori(1, H // HG) as hg:
                finish_group(0, hg)
            with dve.Fori(0, H // HG) as hg:
                finish_group(1, hg)

            for w in range(TT // 2):
                dve.wait_ge(proj_made, w + 1)
                two = x_tm[:, 2 * w:2 * w + 2, :]
                dve.tensor_tensor(two, bank(2 + w % 2).rearrange("p (i c) -> p i c", i=2), two, ALU.add)\
                    .then_inc(x2_done, 1)

            for b in range(NB):
                dve.wait_ge(x2T_out, 4 * b + 4)
                for c in range(CK):
                    s = slice(b * L, (b + 1) * L)
                    dve.tensor_scalar(convT[:, c, s], x2T[:, c, s], cond_col[:, c, 1:2], convb_col[:, c:c + 1],
                                      ALU.mult, ALU.add).then_inc(conv_part, 1)
                for c in range(CK):
                    dve.wait_ge(conv_part, 2 * b + c + 1)
                    s = slice(b * L + 1, (b + 1) * L)
                    ins = stt(convT[:, c, s], x2T[:, c, b * L:(b + 1) * L - 1], cond_col[:, c, 0:1],
                              convT[:, c, s], ALU.mult, ALU.add)
                ins.then_inc(conv_done, 1)

            dve.wait_ge(decay_e, 2)
            link = chain(decay_step2)
            link(stt(decay[:, 4:6], decay[:, 0:2], 0.0, decay[:, 2:4], ALU.max, ALU.add))
            link(dve.tensor_tensor(decay[:, 6:7], decay[:, 4:5], decay[:, 5:6], ALU.mult))
            link(dve.tensor_scalar(decay[:, 6:7], decay[:, 6:7], -1.0, 1.0, ALU.mult, ALU.add))
            link = chain(seq_step)
            for n in range(2):
                c = slice(512 * n, 512 * n + 512)
                dve.wait_ge(seq_made, 3 * n + 1)
                link(dve.tensor_scalar(gate_b[:, c], bank(n), bp_b[:, 0:1], None, ALU.add))
                stt(gate_e[:, c], gate_b[:, c], -1.0, gate_b[:, c], ALU.mult, ALU.min).then_inc(neg_abs, 1)
                dve.wait_ge(seq_made, 3 * n + 2)
                link(dve.tensor_scalar(seq_u[:, c], bank(2 + n), bs_col[:, 0:1], None, ALU.add))
            for n in range(2):
                c = slice(512 * n, 512 * n + 512)
                dve.wait_ge(soft_log, n + 1)
                link(stt(gate_b[:, c], gate_b[:, c], 0.0, gate_e[:, c], ALU.max, ALU.add))
                link(stt(gate_b[:, c], gate_b[:, c], decay[:, 5:6], seq_u[:, c], ALU.mult, ALU.mult))
            link(dve.tensor_tensor_scan(gate_e[:], decay[:, 6:7].to_broadcast([P, L]), gate_b[:], 0.0,
                                        ALU.mult, ALU.add))
            dve.wait_ge(tanh_done, 2)
            dve.tensor_tensor(gate_e[:], gate_e[:], gate_c[:], ALU.mult).then_inc(state_out, 1)

            for w in range(TT // 2):
                dve.wait_ge(x3_made, w + 1)
                dve.tensor_tensor(x3_tm[:, 2 * w:2 * w + 2, :],
                                  bank(4 + w % 3).rearrange("p (i c) -> p i c", i=2), wide(bo_row[:], 1, 2),
                                  ALU.add).then_inc(x3_out, 1)

            link = chain(rstep)
            dve.wait_ge(logits_made, 1)
            dve.tensor_tensor(route[:], bank(7)[:, 0:TT * RE].rearrange("p (i e) -> p i e", e=RE),
                              wide(br_row[:], 1, TT), ALU.add).then_inc(logits_out, 1)
            dve.wait_ge(route_done, 1)
            link(dve.tensor_reduce(prob[:], route[:], AX, ALU.max))
            link(dve.tensor_tensor(rt[0][:], route[:], wide(prob[:], 2, RE), ALU.is_equal))
            link(stt(rt[1][:], rt[0][:], -float(RE), wide(iota_e[:], 1, TT), ALU.mult, ALU.add))
            link(dve.tensor_reduce(sl[:], rt[1][:], AX, ALU.min))
            onehot = rt[2]
            stt(onehot[:], wide(iota_e[:], 1, TT), -float(RE), wide(sl[:], 2, RE), ALU.add, ALU.is_equal)\
                .then_inc(onehot_done, 1)
            dve.wait_ge(ranks_made, 1)
            within = bank(0)[:, 0:TT * RE].rearrange("p (i e) -> p i e", e=RE)
            link(dve.tensor_copy(rt[3][:].rearrange("p i e -> p (i e)"), bank(1)[:, 0:TT * RE]))
            total, k, step = rt[3], 3, 1
            while step < TT:
                src, dst = rt[k], rt[k + 1]
                dve.tensor_copy(dst[:, 0:step, :], src[:, 0:step, :])
                link(dve.tensor_tensor(dst[:, step:, :], src[:, step:, :], src[:, 0:TT - step, :], ALU.add))
                k, step = k + 1, 2 * step
            running = rt[k]
            link(dve.tensor_tensor(rt[0][:], running[:], total[:], ALU.subtract))
            link(dve.tensor_tensor(rt[1][:], within, rt[0][:], ALU.add))
            link(dve.tensor_tensor(rk[0][:], wide(running[:, TT - 1, :], 2, TT), wide(iota_tok[:], 1, RE),
                                   ALU.is_gt))
            link(dve.tensor_reduce(re[0][:], rk[0][:], AX, ALU.add))
            link(dve.tensor_scalar(re[1][:], re[0][:], 1.0, None, ALU.max))
            link(dve.tensor_tensor_scan(re[2][:], ones[:, 0:RE], re[1][:], 0.0, ALU.mult, ALU.add))
            link(dve.tensor_tensor(re[3][:], re[2][:], re[1][:], ALU.subtract))
            link(stt(rt[8][:], wide(re[3][:], 1, TT), float(P), rt[1][:], ALU.mult, ALU.add))
            link(dve.tensor_tensor(rt[0][:], rt[8][:], onehot[:], ALU.mult))
            link(dve.tensor_reduce(sl[:], rt[0][:], AX, ALU.add))
            dve.tensor_copy(slot_i[:], sl[:]).then_inc(slots_done, 1)
            link(dve.tensor_tensor(tl[:], wide(iota_tile[:], 2, RE), wide(re[2][:], 1, TILES), ALU.is_ge))
            link(dve.tensor_reduce(tf[:], tl[:], AX, ALU.add))
            link(dve.tensor_scalar(tf[:], tf[:], float(RE - 1), None, ALU.min))
            dve.tensor_scalar(tile_i[:], tf[:], -1.0, float(RE - 1), ALU.mult, ALU.add).then_inc(slots_done, 1)

            def x_tile(s, i):
                dve.wait_ge(xs_turned, s + 1)
                after(dve, fh_made, s - 1)
                dve.tensor_copy(xsT[i][:].rearrange("p k n -> p (k n)"), bank(6)[:, 0:C]).then_inc(xsT_out, 1)

            def h_tile(s, i):
                dve.wait_ge(fh_turned, s + 1)
                after(dve, fo_made, s - 1)
                dve.tensor_copy(fhT[i][:, 4:8, :].rearrange("p f n -> p (f n)"), bank(5)).then_inc(fhT_dve, 1)

            def o_tile(s, i):
                dve.wait_ge(fo_made, s + 1)
                if not isinstance(s, int) or s >= 2:
                    dve.wait_ge(fo_stored[i], 8 * (s - i))
                dve.tensor_copy(fo[i][:], bank(7)[:, 0:C]).then_inc(fo_out, 1)

            dve.wait_ge(scattered, 16 * TT)
            x_tile(0, 0)
            x_tile(1, 1)
            for s in range(2):
                h_tile(s, s)
                o_tile(s, s)
                x_tile(s + 2, s)
            with dve.Fori(2, TILES - 3, 2) as s:
                for i in range(2):
                    h_tile(s + i, i)
                    o_tile(s + i, i)
                    x_tile(s + i + 2, i)
            for s in range(TILES - 3, TILES):
                h_tile(s, s % 2)
                o_tile(s, s % 2)
                if s + 2 < TILES:
                    x_tile(s + 2, s % 2)

            dve.wait_ge(gathered, 16 * TT)
            for i in range(TT):
                ins = stt(ffn_tm[:, i, :], ffn_tm[:, i, :], prob[:, i:i + 1], x_tm[:, i, :], ALU.mult, ALU.add)
                if i % LT == LT - 1:
                    ins.then_inc(out_ready, 1)

        @block.tensor
        def _(pe):
            pe.wait_ge(consts_made, 1)
            for m in range(12):
                if m == 0 or m == 4:
                    pe.wait_ge(x_in[m // 4], 16)
                if m == 8:
                    pe.wait_ge(wproj_in, 32)
                if m >= 8:
                    pe.wait_ge(lo_out, m - 7)
                for n in range(4):
                    if m < 8:
                        c, i = m % 2, 4 * (m // 2) + n
                        src = x_tm[:, i, c * P:(c + 1) * P]
                    elif m < 10:
                        src = qkv_raw[:, n, (m - 8) * P:(m - 7) * P]
                    else:
                        c, r = n // 2, n % 2
                        src = (qkv_raw[:, 4 + r, :] if m == 10 else proj_raw[:, r, :])[:, c * P:(c + 1) * P]
                    ins = pe.transpose(bank(m % 8)[:, n * P:(n + 1) * P], src, ident[:])
                ins.then_inc(setup_filled, 1)

            pe.wait_ge(lo_out, 8)
            for c in range(CK):
                for b in range(NB):
                    o = bank(4)[:, (c * NB + b) * 3:(c * NB + b) * 3 + 3]
                    for i in range(LT):
                        ins = pe.matmul(o, x_tm[:, b * LT + i, c * P:(c + 1) * P], region_mask[:, i, :],
                                        start=(i == 0), stop=(i == LT - 1))
            ins.then_inc(region_sums, 1)
            pe.wait_ge(gate_in_made, 1)
            pe.wait_ge(const_in, 16 * CONSTS)
            for c in range(CK):
                pe.matmul(bank(5)[0:NB, 8:16], sil[:, 2, c, :], time_rows[:, c, :], start=(c == 0), stop=(c == CK - 1))
            for n in range(3 * CK):
                ins = pe.matmul(bank(5)[0:NB, 0:NE], gate_in[:, n // CK, n % CK, :], gate_rows[:, n, :],
                                start=(n == 0), stop=(n == 3 * CK - 1))
            ins.then_inc(gate_logits, 1)
            pe.wait_ge(gate_rows_made, 1)
            for b in range(NB):
                ins = pe.matmul(bank(6)[:, 8 * b:8 * b + 8], pick_row[:, b, :], gs[:, 5, :], start=True, stop=True)
            ins.then_inc(gate_wide, 1)

            def three(o, w, x, first, last):
                for n, (i, j) in enumerate(((0, 0), (0, 1), (1, 0))):
                    ins = pe.matmul(o, w[i], x[j], start=first and n == 0, stop=last and n == 2)
                return ins

            def up(b, v, k):
                j, t = k // 2, k % 2
                u = v // 2 if isinstance(v, int) else None
                if t == 0:
                    pe.wait_ge(w_split, 4 * (v - k) // 8 + j + 1 if u is not None else (v - k) // 2 + j + 1)
                after(pe, gelu_done, v - 3)
                s = slice(b * L + 512 * t, b * L + 512 * t + 512)
                for c in range(CK):
                    ins = three(bank(k % 4), (w1h[j][:, c, :], w1l[j][:, c, :]), (x_hi[:, c, s], x_lo[:, c, s]),
                                c == 0, c == CK - 1)
                ins.then_inc(hid_made, 1)

            def down(b, v, k, first, last):
                j, t = k // 2, k % 2
                pe.wait_ge(h_split, v + 1)
                for c in range(CK):
                    s = slice(c * P, (c + 1) * P)
                    ins = three(bank(4 + 2 * t + c), (w2h[j][:, s], w2l[j][:, s]), (hh[k % 4][:], hl[k % 4][:]),
                                first, last)
                ins.then_inc(unit_done, 1)

            def quad(b, q, first=False, last=False):
                for k in range(8):
                    if k < 6:
                        up(b, 8 * q + k + 2, k + 2)
                    elif not last:
                        up_next(b, q, k - 6)
                    down(b, 8 * q + k, k, first and k < 2, last and k >= 6)

            def up_next(b, q, k):
                up(b, 8 * (q + 1) + k, k)

            for b in range(NB):
                q0 = b * QB
                if b:
                    pe.wait_ge(qkv_out, b * LT)
                up(b, 8 * q0, 0)
                up(b, 8 * q0 + 1, 1)
                if b:
                    pe.wait_ge(y_split, 4 * b)
                quad(b, q0, first=True)
                with pe.Fori(q0 + 1, q0 + QB - 1) as q:
                    quad(b, q)
                quad(b, q0 + QB - 1, last=True)
                pe.wait_ge(y_split, 4 * b + 4)
                pe.wait_ge(lo_out, 11)
                pe.wait_ge(gelu_done, (b + 1) * 8 * QB)
                for i in range(LT):
                    if i >= 2:
                        pe.wait_ge(qkv_out, b * LT + i - 1)
                    s = slice(i * P, (i + 1) * P)
                    for c in range(CK):
                        three(bank(2 * i % 4), (y_hi[:, c, s], y_lo[:, c, s]),
                              (wq_h[:, c, 0:2 * C], wq_l[:, c, 0:2 * C]), c == 0, c == CK - 1)
                    for c in range(CK):
                        ins = three(bank((2 * i + 1) % 4)[:, 0:C], (y_hi[:, c, s], y_lo[:, c, s]),
                                    (wq_h[:, c, 2 * C:], wq_l[:, c, 2 * C:]), c == 0, c == CK - 1)
                    ins.then_inc(qkv_made, 1)

            for w in range(NB * 8):
                b, k, n4 = w // 8, w // 2 % 4, w % 2
                pe.wait_ge(normed, b + 1)
                after(pe, rest1, w - 3)
                for n in range(4):
                    ins = pe.transpose(bank(w % 4)[:, n * P:(n + 1) * P],
                                       qk_tm[:, b * LT + 4 * n4 + n, k * P:(k + 1) * P], ident[:])
                ins.then_inc(turned, 1)

            PER = HG * LT

            def turn(g):
                pe.wait_ge(yT_out, g + 1)
                pe.wait_ge(exp_done, PER * (g + 1) + 14 if not last_turn[0] else PER * (g + 1))
                for i in range(LT):
                    ins = pe.transpose(psum[:, 2 + i // 4, (i % 4) * P:(i % 4 + 1) * P],
                                       yT[:, i * P:(i + 1) * P], ident[:])
                ins.then_inc(y_turned, 1)

            last_turn = [False]

            def scores(g, i, u, first):
                mt, j = u // HG, u % HG
                pos = u + (u >= 16)
                if pos - 3 == 16:
                    after(pe, y_read, g)
                    if first:
                        pe.wait_ge(exp_done, 14)
                elif pos >= 3:
                    before = pos - 3 - (pos - 3 > 16)
                    pe.wait_ge(exp_done, PER * g + before + 1)
                else:
                    after(pe, exp_done, PER * g + u - 2)
                for h in range(2):
                    ins = pe.matmul(psum[:, 2 * (pos % 3) + h, :], k_stack[i][:, j, mt * P:(mt + 1) * P],
                                    q_stack[i][:, j, 512 * h:512 * h + 512], start=True, stop=True)
                ins.then_inc(scored, 1)

            def values(g, i, mt, h):
                if h == 0:
                    pe.wait_ge(exp_done, PER * g + HG * (mt + 1))
                    if mt == 0:
                        pe.wait_ge(v_ready, g + 1)
                        after(pe, yT_out, g)
                for j in range(HG):
                    ins = pe.matmul(psum[VW * j:VW * j + VW, 6 + h, :], v_ones[i][:, mt, j, :],
                                    pexp[mt % 2][:, j, 512 * h:512 * h + 512],
                                    start=(mt == 0), stop=(mt == LT - 1))
                if h == 1:
                    ins.then_inc(av_done, 1)

            def group(g, i, first=False):
                if isinstance(g, int) and g < 2:
                    pe.wait_ge(stack_in[i], 16 * 2 * TERMS)
                else:
                    pe.wait_ge(stack_in[i], 16 * TERMS * (g - i) + 16 * 2 * TERMS)
                for u in range(PER):
                    scores(g, i, u, first)
                    mt, j = u // HG, u % HG
                    if u == 15 and not first:
                        turn(g - 1)
                    if j % 2 and not (first and mt == 0):
                        if mt == 0:
                            values(g - 1, 1 - i, LT - 1, j // 2)
                        else:
                            values(g, i, mt - 1, j // 2)

            group(0, 0, first=True)
            group(1, 1)
            with pe.Fori(2, GROUPS, 2) as g:
                group(g, 0)
                group(g + 1, 1)
            values(GROUPS - 1, 1, LT - 1, 0)
            values(GROUPS - 1, 1, LT - 1, 1)
            last_turn[0] = True
            turn(GROUPS - 1)

            def turn_ctx(w):
                pe.wait_ge(ctx_done, 4 if w < 4 else 8)
                after(pe, ctxT_out, w - 1)
                for n in range(4):
                    ins = pe.transpose(bank(w % 2)[:, n * P:(n + 1) * P],
                                       ctx_tm[:, 2 * w + n // 2, (n % 2) * P:(n % 2 + 1) * P], ident[:])
                ins.then_inc(ctx_turned, 1)

            pe.wait_ge(y_read, GROUPS)
            turn_ctx(0)
            for w in range(TT // 2):
                if w + 1 < TT // 2:
                    turn_ctx(w + 1)
                pe.wait_ge(ctxT_out, w + 1)
                after(pe, x2_done, w - 1)
                for n in range(4):
                    i, c = n // 2, n % 2
                    ins = pe.matmul(bank(2 + w % 2)[:, i * C:(i + 1) * C], ctxT[w % 2][:, i, c, :], projT[:, c, :],
                                    start=(c == 0), stop=(c == CK - 1))
                ins.then_inc(proj_made, 1)
            for w in range(TT // 2):
                pe.wait_ge(x2_done, 2 * (w // 2) + 2)
                after(pe, x2T_out, w - 3)
                for n in range(4):
                    ins = pe.transpose(bank(4 + w % 4)[:, n * P:(n + 1) * P],
                                       x_tm[:, 4 * (w // 2) + n, (w % 2) * P:(w % 2 + 1) * P], ident[:])
                ins.then_inc(x2_turned, 1)

            pe.wait_ge(conv_done, NB)
            pe.wait_ge(x2T_out, TT // 2)
            for n in range(2):
                for k, (w, src) in enumerate(((wp_sb[:, :, 0:N], convT), (ws_sb[:], x2T),
                                              (wp_sb[:, :, N:2 * N], convT))):
                    for c in range(CK):
                        for b in range(NB):
                            s = slice(b * L + 512 * n, b * L + 512 * n + 512)
                            ins = pe.matmul(psum[half[b], 2 * k + n, :], w[:, c, :], src[:, c, s],
                                            start=(c == 0), stop=(c == CK - 1))
                    ins.then_inc(seq_made, 1)
            pe.wait_ge(state_out, 1)
            for w in range(8):
                b, n, c = w // 4, w // 2 % 2, w % 2
                after(pe, x3T_out, w - 3)
                pe.matmul(bank(w % 4), wo_sb[half[b], c * P:(c + 1) * P], gate_e[half[b], 512 * n:512 * n + 512],
                          start=True, stop=True).then_inc(x3T_made, 1)
            for w in range(TT // 2):
                b = w // 4
                after(pe, x3_out, w - 2)
                for n in range(2):
                    s = slice((2 * w + n - b * LT) * P, (2 * w + n - b * LT + 1) * P)
                    ins = pe.matmul(bank(4 + w % 3)[:, n * C:(n + 1) * C], gate_e[half[b], s], wo_sb[half[b], :],
                                    start=True, stop=True)
                ins.then_inc(x3_made, 1)
            pe.wait_ge(x3T_out, 8)
            for i in range(TT):
                for c in range(CK):
                    ins = pe.matmul(bank(7)[:, i * RE:(i + 1) * RE], x3T[:, c, i * P:(i + 1) * P], wr_sb[:, c, :],
                                    start=(c == 0), stop=(c == CK - 1))
            ins.then_inc(logits_made, 1)
            pe.wait_ge(onehot_done, 1)
            flat = rt[2][:].rearrange("p i e -> p (i e)")
            pe.matmul(bank(0)[:, 0:TT * RE], tri[:], flat, start=True, stop=True)
            pe.matmul(bank(1)[:, 0:TT * RE], ones[:], flat, start=True, stop=True).then_inc(ranks_made, 1)

            def turn_x(s, i, n):
                pe.wait_ge(xs_in[i], 16 * n)
                after(pe, xsT_out, s)
                for c in range(CK):
                    ins = pe.transpose(bank(6)[:, c * P:(c + 1) * P], xs[i][:, c * P:(c + 1) * P], ident[:])
                ins.then_inc(xs_turned, 1)

            def expert_of(s):
                return pe.value_load(tile_i[0:1, bass.ds(s, 1)], min_val=0, max_val=RE - 1)

            def expert_up(s, i):
                if isinstance(s, int) and s < RE:
                    pe.wait_ge(expert_in[s], 32)
                e = expert_of(s)
                pe.wait_ge(xsT_out, s + 1)
                after(pe, fh_out, s - 1)
                for h in range(2):
                    for c in range(CK):
                        w = w_all[:, bass.ds(e, 1), c * FF + 512 * h:c * FF + 512 * h + 512]
                        ins = pe.matmul(psum[:, 2 * i + h, :], xsT[i][:, c, :], w.rearrange("p e n -> p (e n)"),
                                        start=(c == 0), stop=(c == CK - 1))
                ins.then_inc(fh_made, 1)
                return e

            def turn_h(s, i):
                pe.wait_ge(fh_out, s + 1)
                after(pe, fhT_act, s)
                after(pe, fhT_dve, s)
                for f in range(FC):
                    ins = pe.transpose(psum[:, 4 + f // 4, (f % 4) * P:(f % 4 + 1) * P],
                                       fh[i][:, f * P:(f + 1) * P], ident[:])
                ins.then_inc(fh_turned, 1)

            def expert_down(s, i):
                e = expert_of(s)
                pe.wait_ge(fhT_act, s + 1)
                pe.wait_ge(fhT_dve, s + 1)
                after(pe, fo_out, s)
                for f in range(FC):
                    w = w_all[:, bass.ds(e, 1), CK * FF + f * C:CK * FF + (f + 1) * C]
                    ins = pe.matmul(bank(7)[:, 0:C], fhT[i][:, f, :], w.rearrange("p e n -> p (e n)"),
                                    start=(f == 0), stop=(f == FC - 1))
                ins.then_inc(fo_made, 1)

            def tile(s, i, n, up=True, turn=True):
                turn_h(s, i)
                if up:
                    expert_up(s + 1, 1 - i)
                expert_down(s, i)
                if turn:
                    turn_x(s + 2, i, n)

            pe.wait_ge(slots_done, 2)
            turn_x(0, 0, 1)
            expert_up(0, 0)
            turn_x(1, 1, 1)
            for s in range(RE - 1):
                tile(s, s % 2, s // 2 + 2)
            with pe.Fori((RE - 1) // 2, (TILES - 3) // 2) as m:
                tile(2 * m + 1, 1, m + 2)
                tile(2 * m + 2, 0, m + 3)
            tile(TILES - 2, 1, 0, turn=False)
            tile(TILES - 1, 0, 0, up=False, turn=False)


_INS = {"x": "x", "cond": "cond_1024", "gate_w": "L0_cond_gate_w", "gate_b": "L0_cond_gate_b",
        "time_w": "L0_cond_time_w", "time_b": "L0_cond_time_b", "ew1": "L0_cond_ew1", "eb1": "L0_cond_eb1",
        "ew2": "L0_cond_ew2", "eb2": "L0_cond_eb2", "sw1": "L0_cond_sw1", "sb1": "L0_cond_sb1",
        "sw2": "L0_cond_sw2", "sb2": "L0_cond_sb2", "w_qkv": "L0_attn_w_qkv", "w_proj": "L0_attn_w_proj",
        "conv_b": "L0_cond2_conv_b", "Wp": "L0_cond2_Wp", "bp": "L0_cond2_bp", "Ws": "L0_cond2_Ws",
        "bs": "L0_cond2_bs", "A_log": "L0_cond2_A_log", "dt_log": "L0_cond2_dt_log", "Wo": "L0_cond2_Wo",
        "bo": "L0_cond2_bo", "Wr": "L0_ffn_Wr", "br": "L0_ffn_br", "W1": "L0_ffn_W1", "W2": "L0_ffn_W2"}


def kernel(**inputs):
    import numpy as _np
    import concourse.bacc as _bacc
    from concourse import mybir as _mybir
    from concourse.bass_utils import run_bass_kernel_spmd as _run

    nc = _bacc.Bacc("TRN2", target_bir_lowering=False, num_devices=1)
    arrays, args = {}, {}
    for short, name in _INS.items():
        v = _np.ascontiguousarray(inputs[name])
        arrays[f"in_{name}"] = v
        args[short] = nc.dram_tensor(f"in_{name}", v.shape, _mybir.dt.from_np(v.dtype), kind="ExternalInput").ap()
    out = nc.dram_tensor("out_0", (NB, L, C), F32, kind="ExternalOutput").ap()
    layer_kernel(nc, args, out)
    r = _run(nc, [arrays], core_ids=[0])
    return r.results[0]["out_0"]
```

```python
from contextlib import ExitStack

import concourse.bass as bass
from concourse import mybir

F32 = mybir.dt.float32
F32R = mybir.dt.float32r
BF16 = mybir.dt.bfloat16
I32 = mybir.dt.int32
ALU = mybir.AluOpType
ACT = mybir.ActivationFunctionType
AX = mybir.AxisListType.X

P = 128
NB, L, C = 2, 1024, 256
CK = C // P
T = NB * L
LT = L // P
TT = T // P
FF = 1024
FC = FF // P
NE, TOPK = 4, 2
STEPS = NB * (1 + TOPK)
QUADS = STEPS * FC // 4
QB = QUADS // NB
H, D = 16, 16
HG = 4
GROUPS = NB * H // HG
VW = 32
N = 64
RE = 8
ROW = C + 2
NO_TOKEN = 2.0 * T
TILES = (T - RE) // P + RE
L3 = L // 3
REGION = [(0, L3), (L3, 2 * L3), (2 * L3, L)]
CUTS = [[(max(a, 512 * t) - 512 * t, min(z, 512 * t + 512) - 512 * t, r)
         for r, (a, z) in enumerate(REGION) if max(a, 512 * t) < min(z, 512 * t + 512)] for t in range(2)]
Q_PART = (0, 0, 1, 0, 2, 1)
K_PART = (0, 1, 0, 2, 0, 1)
TERMS = len(Q_PART)
RMS_EPS = 1.1920928955078125e-07
NORM_EPS = 1e-12


def layer_kernel(nc, a, out):
    with ExitStack() as ctx:
        def sem(name):
            return ctx.enter_context(nc.semaphore(name))

        base = -(-nc.sbuf_base // 64) * 64
        ARENA = 204 * 1024
        ctx.enter_context(nc.sbuf_tensor("arena", [P, ARENA // 4], F32))
        cursor = [base]

        def sb(name, shape, dt, at=None):
            size = 1
            for s in shape[1:]:
                size *= s
            size *= 2 if dt == BF16 else 4
            if at is None:
                at = cursor
            off = at[0]
            at[0] = off + -(-size // 32) * 32
            assert at[0] <= base + ARENA, (name, at[0] - base - ARENA)
            return nc.alloc_sbuf_tensor_at(name, shape, dt, offset=off)

        ident = sb("ident", [P, P], F32)
        x_tm = sb("x_tm", [P, TT, C], F32)
        v_tm = sb("v_tm", [P, TT, C], F32)
        projT = sb("projT", [P, CK, C], F32)
        cond_col = sb("cond_col", [P, CK, NB], F32)
        gate_rows = sb("gate_rows", [P, 3 * CK, NE], F32)
        time_rows = sb("time_rows", [P, CK, 2 * NE], F32)
        gate_bias = sb("gate_bias", [NB, NE], F32)
        time_bias = sb("time_bias", [NB, 2 * NE], F32)
        eb2_col = sb("eb2_col", [P, CK, NE], F32)
        sb2_col = sb("sb2_col", [P, CK], F32)
        b1_col = sb("b1_col", [P, STEPS * FC], F32)
        convb_col = sb("convb_col", [P, CK], F32)
        bp_b = sb("bp_b", [P, 1], F32)
        bp_c = sb("bp_c", [P, 1], F32)
        bs_col = sb("bs_col", [P, 1], F32)
        wp_sb = sb("wp_sb", [P, CK, 2 * N], F32)
        ws_sb = sb("ws_sb", [P, CK, N], F32)
        wo_sb = sb("wo_sb", [P, NB, C], F32)
        bo_col = sb("bo_col", [P, CK], F32)
        wr_sb = sb("wr_sb", [P, CK, RE], F32)
        br_row = sb("br_row", [P, RE], F32)
        region_mask = sb("region_mask", [P, LT, 3], F32)
        tri = sb("tri", [P, P], F32)
        ones = sb("ones", [P, P], F32)
        iota_e = sb("iota_e", [P, RE], F32)
        iota_tok = sb("iota_tok", [P, TT], F32)
        token = sb("token", [P, TT], F32)
        iota_tile = sb("iota_tile", [P, TILES], F32)
        pick_row = sb("pick_row", [NB, NB, P], F32)
        reg_sum = sb("reg_sum", [P, CK, NB, 3], F32)
        gate_in = sb("gate_in", [P, 3, CK, NB], F32)
        sil = sb("sil", [P, 3, CK, NB], F32)
        gs = sb("gs", [NB, 12, 8], F32)
        gsc = sb("gsc", [NB, 12], F32)
        picked = sb("picked", [P, NB, 8], F32)
        scale_col = sb("scale_col", [P, QUADS, 3], F32)
        eb2w = sb("eb2w", [P, CK, NB, NE], F32)
        bias_col = sb("bias_col", [P, CK, NB, 3], F32)
        expert_i = sb("expert_i", [1, NB, TOPK], I32)
        decay = sb("decay", [P, 7], F32)
        route = sb("route", [P, TT, RE], F32)
        prob = sb("prob", [P, TT], F32)
        v_inv2 = sb("v_inv2", [P, TT, H], F32)
        slot_i = sb("slot_i", [P, TT], I32)
        tile_i = sb("tile_i", [P, TILES], I32)
        stage = cursor[0]

        at = [stage]
        qk_tm = [sb(f"qk_tm{b}", [P, LT, 2 * C], F32, at) for b in range(NB)]
        x_at, x_hi, x_lo = [], [], []
        for b in range(NB):
            x_at.append(at[0])
            x_hi.append(sb(f"x_hi{b}", [P, CK, L], F32R, at))
            x_lo.append(sb(f"x_lo{b}", [P, CK, L], F32R, at))
        after_x = at[0]
        raw1 = [sb(f"raw1_{i}", [P, CK, 2 * P], F32, at) for i in range(2)]
        raw2 = [sb(f"raw2_{i}", [P, 2, C], F32, at) for i in range(2)]
        w1h = [sb(f"w1h_{i}", [P, CK, P], F32R, at) for i in range(4)]
        w1l = [sb(f"w1l_{i}", [P, CK, P], F32R, at) for i in range(4)]
        w2h = [sb(f"w2h_{i}", [P, C], F32R, at) for i in range(4)]
        w2l = [sb(f"w2l_{i}", [P, C], F32R, at) for i in range(4)]
        hid = [sb(f"hid_{i}", [P, 512], F32, at) for i in range(4)]
        hh = [sb(f"hh_{i}", [P, 512], F32R, at) for i in range(4)]
        hl = [sb(f"hl_{i}", [P, 512], F32R, at) for i in range(4)]
        y_at = at[0]
        y_hi = sb("y_hi", [P, CK, L], F32R, at)
        y_lo = sb("y_lo", [P, CK, L], F32R, at)
        wq_at = at[0]
        wq_h = sb("wq_h", [P, CK, 3 * C], F32R, at)
        wq_l = sb("wq_l", [P, CK, 3 * C], F32R, at)
        qkv_raw = sb("qkv_raw", [P, 3 * CK, C], F32, [stage])
        proj_raw = sb("proj_raw", [P, CK, C], F32, [stage + 8192])
        empty_row = sb("empty_row", [P, ROW], F32, [stage + 16384])
        at = [x_at[0]]
        parts = [sb(f"parts_{i}", [P, 3, L], BF16, at) for i in range(2)]
        rest = sb("rest", [P, 2, 512], F32, at)
        assert at[0] <= x_at[1]
        at = [y_at]
        square = [sb(f"square_{i}", [P, 2, 3 * C], F32, at) for i in range(2)]
        ssum = sb("ssum", [P, LT, 3 * H], F32, at)
        assert at[0] <= wq_at
        pexp = [sb("pexp_0", [P, HG, L], F32, [stage]), sb("pexp_1", [P, HG, L], F32, [x_at[1]])]
        at = [after_x]
        q_stack, k_stack = [], []
        for i in range(2):
            q_stack.append(sb(f"q_stack_{i}", [TERMS * D, HG, L], BF16, at))
            k_stack.append(sb(f"k_stack_{i}", [TERMS * D, HG, L], BF16, at))
        v_ones = [sb(f"v_ones_{i}", [P, LT, HG, VW], F32, at) for i in range(2)]
        yT = sb("yT", [P, L], F32, at)
        y_tm = sb("y_tm", [P, LT, HG, D], F32, at)
        y_dot = sb("y_dot", [P, LT, HG, D], F32, at)
        assert at[0] <= y_at
        at = [wq_at]
        y_r = sb("y_r", [P, LT, HG], F32, at)
        y_d = sb("y_d", [P, LT, HG], F32, at)
        ctx_tm = sb("ctx_tm", [P, TT, C], F32, at)
        ctxT = [sb(f"ctxT_{i}", [P, 2, CK, P], F32, at) for i in range(2)]
        after_b = at[0]
        WE = 16384
        top = base + ARENA - RE * WE
        w_all = sb("w_all", [P, RE, CK * FF + FC * C], F32, [top])
        spare = (base + ARENA - after_b) // WE
        at = [stage]
        x2T = sb("x2T", [P, CK, T], F32, at)
        convT = sb("convT", [P, CK, T], F32, at)
        gate_b = sb("gate_b", [P, L], F32, at)
        gate_e = sb("gate_e", [P, L], F32, at)
        seq_u = sb("seq_u", [P, L], F32, at)
        gate_c = sb("gate_c", [P, L], F32, at)
        under_seq = -(-(at[0] - top) // WE)
        x3T = sb("x3T", [P, CK, T], F32, [stage])
        x3_tm = sb("x3_tm", [P, TT, ROW], F32, [stage + 16384])
        rt = [sb(f"rt_{i}", [P, TT, RE], F32, at) for i in range(9)]
        rk = [sb(f"rk_{i}", [P, RE, TT], F32, at) for i in range(2)]
        re = [sb(f"re_{i}", [P, RE], F32, at) for i in range(4)]
        tl = sb("tl", [P, TILES, RE], F32, at)
        tf = sb("tf", [P, TILES], F32, at)
        sl = sb("sl", [P, TT], F32, at)
        under_route = -(-(at[0] - top) // WE)
        at = [stage]
        xs = [sb(f"xs_{i}", [P, ROW], F32, at) for i in range(2)]
        x2s = [sb(f"x2s_{i}", [P, C], F32, at) for i in range(2)]
        prob_s = [sb(f"prob_s{i}", [P, 1], F32, at) for i in range(2)]
        tok_s = [sb(f"tok_s{i}", [P, 1], I32, at) for i in range(2)]
        xsT = [sb(f"xsT_{i}", [P, CK, P], F32, at) for i in range(2)]
        fh = [sb(f"fh_{i}", [P, FF], F32, at) for i in range(2)]
        fhT = [sb(f"fhT_{i}", [P, FC, P], F32, at) for i in range(2)]
        fo = [sb(f"fo_{i}", [P, C], F32, at) for i in range(2)]
        assert at[0] <= top

        psum = ctx.enter_context(nc.psum_tensor("psum", [P, 8, 512], F32))

        def bank(i):
            return psum[:, i, :]

        parts_d = nc.dram_tensor("parts_d", [NB, 4, 3, P, L], BF16).ap()
        sorted_d = nc.dram_tensor("sorted_d", [TILES * P, ROW], F32).ap()
        x2_d = nc.dram_tensor("x2_d", [T, C], F32).ap()
        out_rows = out.rearrange("b l c -> (b l) c")

        x_in = [sem(f"x_in{b}") for b in range(NB)]
        const_in = sem("const_in")
        wproj_in = sem("wproj_in")
        b1_in = sem("b1_in")
        bias_in = sem("bias_in")
        late_in = sem("late_in")
        wo_base = sem("wo_base")
        consts_made = sem("consts_made")
        pool_step = sem("pool_step")
        setup_filled = sem("setup_filled")
        hi_out = sem("hi_out")
        lo_out = sem("lo_out")
        region_sums = sem("region_sums")
        sums_out = sem("sums_out")
        gate_in_made = sem("gate_in_made")
        gate_logits = sem("gate_logits")
        gate_exp = sem("gate_exp")
        gate_step = sem("gate_step")
        gate_rows_made = sem("gate_rows_made")
        gate_wide = sem("gate_wide")
        experts_known = sem("experts_known")
        empty_filled = sem("empty_filled")
        act_passed = sem("act_passed")
        pool_passed = sem("pool_passed")
        raw_in = [sem(f"raw_in{i}") for i in range(2)]
        w_split = sem("w_split")
        w_part = sem("w_part")
        hid_made = sem("hid_made")
        gelu_done = sem("gelu_done")
        h_part = sem("h_part")
        h_split = sem("h_split")
        unit_done = sem("unit_done")
        y_part = sem("y_part")
        y_split = sem("y_split")
        qkv_made = sem("qkv_made")
        qkv_out = sem("qkv_out")
        squared = [sem(f"squared{b}") for b in range(NB)]
        summed = sem("summed")
        norm_step = sem("norm_step")
        var_made = sem("var_made")
        rooted = sem("rooted")
        normed = sem("normed")
        turned = sem("turned")
        turned_b = sem("turned_b")
        part_step = sem("part_step")
        turned_b_read = sem("turned_b_read")
        part1 = sem("part1")
        part2 = sem("part2")
        rest1 = sem("rest1")
        part3 = sem("part3")
        parts_out = [sem(f"parts_out{i}") for i in range(2)]
        stack_in = [sem(f"stack_in{i}") for i in range(2)]
        v_ready = sem("v_ready")
        v_base = sem("v_base")
        scored = sem("scored")
        exp_done = sem("exp_done")
        av_done = sem("av_done")
        yT_out = sem("yT_out")
        y_turned = sem("y_turned")
        y_read = sem("y_read")
        post_step = sem("post_step")
        ctx_done = sem("ctx_done")
        ctx_turned = sem("ctx_turned")
        ctxT_out = sem("ctxT_out")
        proj_made = sem("proj_made")
        x2_done = sem("x2_done")
        x2_turned = sem("x2_turned")
        x2T_out = sem("x2T_out")
        conv_part = sem("conv_part")
        conv_done = sem("conv_done")
        seq_made = sem("seq_made")
        seq_step = sem("seq_step")
        decay_step = sem("decay_step")
        decay_step2 = sem("decay_step2")
        decay_e = sem("decay_e")
        neg_abs = sem("neg_abs")
        soft_log = sem("soft_log")
        soft_exp = sem("soft_exp")
        u_made = sem("u_made")
        tanh_done = sem("tanh_done")
        state_out = sem("state_out")
        x3T_made = sem("x3T_made")
        x3T_out = sem("x3T_out")
        x3_turned = sem("x3_turned")
        x3_out = sem("x3_out")
        logits_made = sem("logits_made")
        logits_out = sem("logits_out")
        route_done = sem("route_done")
        onehot_done = sem("onehot_done")
        ranks_made = sem("ranks_made")
        rstep = sem("rstep")
        slots_done = sem("slots_done")
        scattered = sem("scattered")
        expert_in = [sem(f"expert_in{e}") for e in range(RE)]
        xs_in = [sem(f"xs_in{i}") for i in range(2)]
        xs_turned = sem("xs_turned")
        xsT_out = sem("xsT_out")
        fh_made = sem("fh_made")
        fh_out = sem("fh_out")
        fh_turned = sem("fh_turned")
        fhT_act = sem("fhT_act")
        fhT_dve = sem("fhT_dve")
        fo_made = sem("fo_made")
        fo_out = sem("fo_out")
        tail_read = sem("tail_read")
        tail_made = sem("tail_made")
        x2_stored = sem("x2_stored")
        x2s_base = sem("x2s_base")
        x2s_in = [sem(f"x2s_in{i}") for i in range(2)]
        out_stored = [sem(f"out_stored{i}") for i in range(2)]

        def wide(ap, axis, n):
            v = ap.unsqueeze(axis)
            shape = list(v.shape)
            shape[axis] = n
            return v.to_broadcast(shape)

        def after(eng, s, value):
            if not isinstance(value, int) or value > 0:
                eng.wait_ge(s, value)

        CONSTS = 6
        col = lambda ap: ap.rearrange("(k p) -> p k", p=P)
        half = [slice(N * b, N * b + N) for b in range(NB)]

        one = lambda ap: ap.rearrange("(n a) -> n a", a=1)
        late_consts = [(convb_col[:], col(a["conv_b"])), (bo_col[:], col(a["bo"])),
                       (wp_sb[:], a["Wp"].rearrange("(k p) n -> p k n", p=P)),
                       (ws_sb[:], a["Ws"].rearrange("(k p) n -> p k n", p=P)),
                       (wr_sb[:], a["Wr"].rearrange("(k p) e -> p k e", p=P)),
                       (br_row[:], a["br"].partition_broadcast(P))]
        for b in range(NB):
            late_consts += [(wo_sb[half[b], b, :], a["Wo"]), (bp_b[half[b], :], one(a["bp"][0:N])),
                            (bp_c[half[b], :], one(a["bp"][N:2 * N])), (bs_col[half[b], :], one(a["bs"])),
                            (decay[half[b], 0:1], one(a["A_log"])), (decay[half[b], 1:2], one(a["dt_log"]))]
        LATE = len(late_consts)

        def turns(g):
            units = [("scores", u) for u in range(HG * LT)]
            if isinstance(g, int) and g == 0:
                return units + [("qk", 0)]
            if isinstance(g, int) and g == 1:
                return (units[:16] + [("turn", 0)] + units[16:19] + [("qk", 1)] + units[19:23] + [("qk", 2)]
                        + units[23:27] + [("qk", 3)] + units[27:])
            return units[:16] + [("turn", 0)] + units[16:]

        def position(g, u):
            return turns(g).index(("scores", u))

        block = ctx.enter_context(nc.Block())

        @block.sync
        def _(sp):
            for b in range(NB):
                sp.dma_start(x_tm[:, b * LT:(b + 1) * LT, :],
                             a["x"][b].rearrange("(i p) c -> p i c", p=P)).then_inc(x_in[b], 16)
            sp.dma_start(qkv_raw[:], a["w_qkv"].rearrange("(r p) c -> p r c", p=P)).then_inc(wproj_in, 16)
            sp.dma_start(proj_raw[:], a["w_proj"].rearrange("(r p) c -> p r c", p=P)).then_inc(wproj_in, 16)

            chosen = {}

            def load_pair(s, i, k):
                n = 4 * s + 2 * i + k
                after(sp, w_split, 2 * n - 2)
                f0 = (2 * i + k) * 2 * P
                if s % 3 == 0:
                    w1, w2 = a["sw1"], a["sw2"]
                else:
                    e = chosen[s]
                    w1 = a["ew1"][bass.ds(e, 1), :, :].rearrange("e c f -> (e c) f")
                    w2 = a["ew2"][bass.ds(e, 1), :, :].rearrange("e f c -> (e f) c")
                sp.dma_start(raw1[k][:], w1.rearrange("(k p) f -> p k f", p=P)[:, :, bass.ds(f0, 2 * P)])\
                    .then_inc(raw_in[k], 16)
                sp.dma_start(raw2[k][:], w2.rearrange("(f p) c -> p f c", p=P)[:, bass.ds(f0 // P, 2), :])\
                    .then_inc(raw_in[k], 16)

            def store_parts(b, k):
                u = 4 * b + k
                sp.wait_ge(part3, 2 * u + 2 if b == 0 else 8 + k + 1)
                sp.dma_start(parts_d[b, k].rearrange("s p n -> p s n"), parts[u % 2][:])\
                    .then_inc(parts_out[u % 2], 16)

            sp.dma_start(b1_col[:, 0:FC], col(a["sb1"]),
                         allow_slow_non_contiguous=True).then_inc(b1_in, 16)
            for dst, src in ((eb2_col[:, 0, :], a["eb2"][:, 0:P].rearrange("e p -> p e")),
                             (eb2_col[:, 1, :], a["eb2"][:, P:C].rearrange("e p -> p e")),
                             (sb2_col[:], col(a["sb2"]))):
                sp.dma_start(dst, src, allow_slow_non_contiguous=True).then_inc(bias_in, 16)
            for s in range(STEPS):
                if s == 1:
                    sp.wait_ge(wo_base, 1)
                    for dst, src in late_consts:
                        sp.dma_start(dst, src, allow_slow_non_contiguous=True).then_inc(late_in, 16)
                    sp.wait_ge(experts_known, 1)
                    sp.wait_ge(empty_filled, 1)
                    sp.dma_start(sorted_d.rearrange("(s p) c -> p s c", p=P),
                                 wide(empty_row[:], 1, TILES)).then_inc(empty_filled, 16)
                    for s1 in range(1, STEPS):
                        src = a["sb1"]
                        if s1 % 3:
                            b, k = s1 // 3, s1 % 3 - 1
                            chosen[s1] = sp.value_load(expert_i[0:1, b, k:k + 1], min_val=0, max_val=NE - 1)
                            src = a["eb1"][bass.ds(chosen[s1], 1), :].rearrange("e f -> (e f)")
                        sp.dma_start(b1_col[:, s1 * FC:(s1 + 1) * FC], col(src),
                                     allow_slow_non_contiguous=True).then_inc(b1_in, 16)
                for i in range(2):
                    if 2 * s + i >= QUADS - 2:
                        store_parts(0, 2 * (s * 2 + i - QUADS + 2))
                        store_parts(0, 2 * (s * 2 + i - QUADS + 2) + 1)
                    for k in range(2):
                        load_pair(s, i, k)

            def load_stacks(g):
                b, hg = g // (H // HG), g % (H // HG)
                cq = hg // 2
                r = slice(HG * D * (hg % 2), HG * D * (hg % 2) + HG * D)
                if g >= 2:
                    sp.wait_ge(scored, HG * LT * (g - 1))
                for kk, (stack, order) in enumerate(((q_stack, Q_PART), (k_stack, K_PART))):
                    if g < 2 or hg % 2 == 0:
                        u = 4 * b + cq + 2 * kk
                        sp.wait_ge(parts_out[u % 2], 16 * (u // 2 + 1))
                    for t, s in enumerate(order):
                        sp.dma_start(stack[g % 2][D * t:D * t + D, :, :],
                                     parts_d[b, cq + 2 * kk, s, r, :].rearrange("(j d) n -> d j n", j=HG))\
                            .then_inc(stack_in[g % 2], 16)

            def load_expert(e):
                at_e = w_all[:, RE - 1 - e, :]
                sp.dma_start(at_e[:, 0:CK * FF].rearrange("p (k f) -> p k f", k=CK),
                             a["W1"][e].rearrange("(k p) f -> p k f", p=P)).then_inc(expert_in[e], 16)
                sp.dma_start(at_e[:, CK * FF:].rearrange("p (f c) -> p f c", f=FC),
                             a["W2"][e].rearrange("(f p) c -> p f c", p=P)).then_inc(expert_in[e], 16)

            sp.wait_ge(unit_done, 2 * FC * STEPS)
            for g in range(GROUPS):
                load_stacks(g)
                if g == 1:
                    for k in range(4):
                        store_parts(1, k)
                    for e in range(spare):
                        load_expert(e)
            for b in range(NB):
                sp.wait_ge(x2_done, (b + 1) * LT // 2)
                sp.dma_start(x2_d[b * L:(b + 1) * L, :].rearrange("(i p) c -> p i c", p=P),
                             x_tm[:, b * LT:(b + 1) * LT, :]).then_inc(x2_stored, 16)
            sp.wait_ge(proj_made, TT // 2)
            sp.wait_ge(ctxT_out, TT // 2)
            for e in range(spare, RE - under_route):
                load_expert(e)
            sp.wait_ge(slots_done, 2)
            sp.wait_ge(x3_turned, TT // 2)
            for e in range(RE - under_route, RE):
                load_expert(e)

            sp.wait_ge(scattered, 16 * TT)

            def load_tile(s, i):
                if not isinstance(s, int) or s >= 2:
                    sp.wait_ge(xs_turned, s - 1)
                    sp.wait_ge(tail_read, s - 1)
                sp.dma_start(xs[i][:], sorted_d[bass.ds(s * P, P), :]).then_inc(xs_in[i], 16)

            for s in range(3):
                load_tile(s, s % 2)
            with sp.Fori(3, TILES - 1, 2) as s:
                load_tile(s, 1)
                load_tile(s + 1, 0)
            sp.wait_ge(x2_stored, 16 * NB)
            for i in range(2):
                sp.wait_ge(out_stored[i], 16 * ((TILES + 1 - i) // 2))
            sp.wait_ge(empty_filled, 17)

        @block.gpsimd
        def _(pool):
            steps = [0]

            def link(ins):
                steps[0] += 1
                ins.then_inc(pool_step, 1)
                pool.wait_ge(pool_step, steps[0])

            pool.memset(ident[:], 0.0)
            pool.memset(ones[:], 1.0)
            pool.memset(tri[:], 1.0)
            pool.memset(region_mask[:], 1.0)
            pool.memset(wo_sb[:], 0.0).then_inc(wo_base, 1)
            link(pool.memset(pick_row[:], 0.0))
            pool.affine_select(out=ident[:], in_=ident[:], compare_op=ALU.not_equal, fill=1.0, base=0,
                               pattern=[[-1, P]], channel_multiplier=1)
            pool.affine_select(out=tri[:], in_=tri[:], compare_op=ALU.is_gt, fill=0.0, base=0,
                               pattern=[[1, P]], channel_multiplier=-1)
            pool.affine_select(out=pick_row[:], in_=pick_row[:], compare_op=ALU.not_equal, fill=1.0, base=0,
                               pattern=[[-1, NB], [0, P]], channel_multiplier=1)
            for r, (first, last) in enumerate(REGION):
                link(pool.affine_select(out=region_mask[:, :, r], in_=region_mask[:, :, r],
                                        compare_op=ALU.is_ge, fill=0.0, base=last - 1,
                                        pattern=[[-P, LT]], channel_multiplier=-1))
            for r, (first, last) in enumerate(REGION):
                pool.affine_select(out=region_mask[:, :, r], in_=region_mask[:, :, r],
                                   compare_op=ALU.is_ge, fill=0.0, base=-first,
                                   pattern=[[P, LT]], channel_multiplier=1)
            pool.iota(iota_e[:], pattern=[[1, RE]], base=0, channel_multiplier=0,
                      allow_small_or_imprecise_dtypes=True)
            pool.iota(iota_tok[:], pattern=[[P, TT]], base=0, channel_multiplier=0,
                      allow_small_or_imprecise_dtypes=True)
            pool.iota(iota_tile[:], pattern=[[1, TILES]], base=0, channel_multiplier=0,
                      allow_small_or_imprecise_dtypes=True).then_inc(consts_made, 1)
            pool.iota(token[:], pattern=[[P, TT]], base=0, channel_multiplier=1,
                      allow_small_or_imprecise_dtypes=True)
            pool.memset(empty_row[:, 0:C + 1], 0.0)
            pool.memset(empty_row[:, C + 1:], NO_TOKEN).then_inc(empty_filled, 1)

            def split_quad(q):
                for k in range(4):
                    u = 4 * q + k
                    pair, j = k // 2, k % 2
                    if j == 0:
                        pool.wait_ge(raw_in[pair], 32 * (q + 1))
                    after(pool, unit_done, 2 * u - 6)
                    pool.sem_inc(pool_passed, 1)
                    r1, r2 = raw1[pair][:, :, j * P:(j + 1) * P], raw2[pair][:, j, :]
                    pool.tensor_copy(w1h[k][:], r1)
                    pool.tensor_copy(w2h[k][:], r2).then_inc(w_part, 1)
                    pool.wait_ge(w_part, u + 1)
                    pool.tensor_tensor(w1l[k][:], r1, w1h[k][:].bitcast(F32), ALU.subtract)
                    pool.tensor_tensor(w2l[k][:], r2, w2h[k][:].bitcast(F32), ALU.subtract)\
                        .then_inc(w_split, 1)

            split_quad(0)
            with pool.Fori(1, QUADS) as q:
                split_quad(q)

            pool.wait_ge(qkv_out, TT)
            for i in range(2):
                pool.memset(v_ones[i][:, :, :, D:VW], 0.0).then_inc(v_base, 1)
            for i in range(2):
                pool.wait_ge(v_base, i + 1)
                pool.memset(v_ones[i][:, :, :, D:D + 1], 1.0).then_inc(v_base, 1)
            for g in range(GROUPS):
                b, hg = g // (H // HG), g % (H // HG)
                if g >= 2:
                    pool.wait_ge(av_done, LT * (g - 1))
                else:
                    pool.wait_ge(v_base, 3 + g)
                pool.tensor_copy(v_ones[g % 2][:, :, :, 0:D],
                                 v_tm[:, b * LT:(b + 1) * LT, hg * HG * D:(hg + 1) * HG * D]
                                 .rearrange("p i (j d) -> p i j d", j=HG)).then_inc(v_ready, 1)
                if g == 1:
                    for n in range(LT // 2):
                        after(pool, summed, 4 + n - 1)
                        q2, v2 = qk_tm[1][:, 2 * n:2 * n + 2, :], v_tm[:, LT + 2 * n:LT + 2 * n + 2, :]
                        pool.tensor_tensor(square[n % 2][:, :, 0:2 * C], q2, q2, ALU.mult)
                        pool.tensor_tensor(square[n % 2][:, :, 2 * C:], v2, v2, ALU.mult)\
                            .then_inc(squared[1], 1)

            pool.wait_ge(empty_filled, 17)
            pool.wait_ge(slots_done, 1)
            pool.wait_ge(x3_out, TT // 2)
            pool.wait_ge(tail_made, 1)
            for i in range(TT):
                pool.indirect_dma_start(out=sorted_d[:, :],
                                        out_offset=bass.IndirectOffsetOnAxis(ap=slot_i[:, i:i + 1], axis=0),
                                        in_=x3_tm[:, i, :], in_offset=None,
                                        bounds_check=TILES * P - 1).then_inc(scattered, 16)
            pool.wait_ge(scattered, 16 * TT)
            for i in range(2):
                pool.memset(x2s[i][:], 0.0).then_inc(x2s_base, 1)
            pool.wait_ge(x2s_base, 2)
            pool.wait_ge(x2_stored, 16 * NB)

            def load_x2(s, i):
                pool.wait_ge(tail_read, s + 1)
                after(pool, fo_out, s - 1)
                pool.sem_inc(pool_passed, 1)
                pool.indirect_dma_start(out=x2s[i][:], out_offset=None, in_=x2_d[:, :],
                                        in_offset=bass.IndirectOffsetOnAxis(ap=tok_s[i][:, 0:1], axis=0),
                                        bounds_check=T - 1, oob_is_err=False).then_inc(x2s_in[i], 16)

            def store_tile(s, i):
                pool.wait_ge(fo_out, s + 1)
                pool.sem_inc(pool_passed, 1)
                pool.indirect_dma_start(out=out_rows,
                                        out_offset=bass.IndirectOffsetOnAxis(ap=tok_s[i][:, 0:1], axis=0),
                                        in_=fo[i][:], in_offset=None,
                                        bounds_check=T - 1, oob_is_err=False).then_inc(out_stored[i], 16)

            load_x2(0, 0)
            load_x2(1, 1)
            store_tile(0, 0)
            with pool.Fori(1, TILES - 2, 2) as s:
                load_x2(s + 1, 0)
                store_tile(s, 1)
                load_x2(s + 2, 1)
                store_tile(s + 1, 0)
            load_x2(TILES - 1, 0)
            store_tile(TILES - 2, 1)
            store_tile(TILES - 1, 0)

        @block.scalar
        def _(act):
            for dst, src in ((cond_col[:, 0, :], a["cond"][:, 0:P].rearrange("b p -> p b")),
                             (cond_col[:, 1, :], a["cond"][:, P:C].rearrange("b p -> p b")),
                             (gate_rows[:], a["gate_w"].rearrange("(r p) e -> p r e", p=P)),
                             (time_rows[:], a["time_w"].rearrange("(r p) e -> p r e", p=P)),
                             (gate_bias[:], a["gate_b"].partition_broadcast(NB)),
                             (time_bias[:], a["time_b"].partition_broadcast(NB))):
                act.dma_start(dst, src, allow_slow_non_contiguous=True).then_inc(const_in, 16)

            def hi_parts(m):
                act.wait_ge(setup_filled, m + 1)
                b, src = m % 8, bank(m % 8)
                if m < 8:
                    dst = x_hi[m // 4][:, m % 2, 512 * (m // 2 % 2):512 * (m // 2 % 2) + 512]
                elif m < 10:
                    dst = wq_h[:, m - 8, 0:512]
                else:
                    src = src.rearrange("p (k r) -> p k r", k=CK)
                    dst = wq_h[:, :, 512:768] if m == 10 else projT[:]
                act.copy(dst, src).then_inc(hi_out, 1)

            act.wait_ge(const_in, 16 * CONSTS)
            act.activation(sil[:, 0], cond_col[:], ACT.Exp, scale=-1.0).then_inc(gate_exp, 1)
            for m in range(12):
                hi_parts(m)
            act.wait_ge(gate_logits, 2)
            act.activation(gs[:, 6, 0:NE], gs[:, 5, 0:NE], ACT.Exp).then_inc(gate_exp, 1)


            def gelu_quad(q, between=None):
                for k in range(8):
                    if between and k % 2 == 1:
                        between(k // 2)
                    v = 8 * q + k
                    act.wait_ge(hid_made, v + 1)
                    after(act, h_split, v - 3)
                    act.sem_inc(act_passed, 1)
                    act.activation(hid[k % 4][:], bank(k % 4), ACT.Gelu_apprx_tanh,
                                   bias=b1_col[:, bass.ds(4 * q + k // 2, 1)]).then_inc(gelu_done, 1)

            def qkv_to_sbuf(b):
                for i in range(LT):
                    act.wait_ge(qkv_made, b * LT + i + 1)
                    act.copy(qk_tm[b][:, i, :], bank(2 * i % 4))
                    act.copy(v_tm[:, b * LT + i, :], bank((2 * i + 1) % 4)[:, 0:C]).then_inc(qkv_out, 1)

            act.wait_ge(b1_in, 16)
            gelu_quad(0)
            gelu_quad(1)
            act.wait_ge(b1_in, 16 * STEPS)
            with act.Fori(2, QB) as q:
                gelu_quad(q)
            act.wait_ge(empty_filled, 17)
            qkv_to_sbuf(0)

            def squares(n):
                act.wait_ge(qkv_out, 2 * n + 2)
                after(act, summed, n - 1)
                act.activation(square[n % 2][:, :, 0:2 * C], qk_tm[0][:, 2 * n:2 * n + 2, :], ACT.Square)
                act.activation(square[n % 2][:, :, 2 * C:], v_tm[:, 2 * n:2 * n + 2, :], ACT.Square)\
                    .then_inc(squared[0], 1)

            def part_two(w):
                act.wait_ge(rest1, w + 1)
                act.copy(parts[w // 2 % 2][:, 1, 512 * (w % 2):512 * (w % 2) + 512], rest[:, w % 2, :])\
                    .then_inc(part2, 1)

            def parts_one_two(w0):
                for w in range(w0, w0 + 4):
                    act.wait_ge(turned, w + 1)
                    after(act, parts_out[w // 2 % 2], 16 * (w // 4))
                    act.copy(parts[w // 2 % 2][:, 0, 512 * (w % 2):512 * (w % 2) + 512], bank(2 + w % 2))\
                        .then_inc(part1, 1)
                    if w > w0:
                        part_two(w - 1)
                part_two(w0 + 3)

            def root(b):
                act.wait_ge(var_made, b + 1)
                act.activation(ssum[:, :, 0:2 * H], ssum[:, :, 0:2 * H], ACT.Sqrt).then_inc(rooted, 1)

            gelu_quad(QB, squares)
            root(0)
            gelu_quad(QB + 1)
            parts_one_two(0)
            gelu_quad(QB + 2)
            gelu_quad(QB + 3)
            parts_one_two(4)
            with act.Fori(QB + 4, QUADS) as q:
                gelu_quad(q)
            qkv_to_sbuf(1)

            def exps(g):
                for u in range(HG * LT):
                    mt, j = u // HG, u % HG
                    r = position(g, u) % 3
                    act.wait_ge(scored, HG * LT * g + u + 1)
                    if j == 0:
                        after(act, av_done, LT * g + mt - 1)
                    act.activation(pexp[mt % 2][:, j, :].rearrange("p (h n) -> p h n", h=2),
                                   psum[:, 2 * r:2 * r + 2, :], ACT.Exp, scale=D ** -0.5)\
                        .then_inc(exp_done, 1)
                    if isinstance(g, int) and g == 0 and u == 19:
                        root(1)

            act.wait_ge(decay_step, 2)
            act.activation(decay[:, 2:4], decay[:, 2:4], ACT.Exp).then_inc(decay_e, 1)
            exps(0)
            exps(1)
            with act.Fori(2, GROUPS) as g:
                exps(g)

            for w in range(TT // 2):
                act.wait_ge(ctx_turned, w + 1)
                after(act, proj_made, w - 1)
                act.copy(ctxT[w % 2][:].rearrange("p i k n -> p (i k n)"), bank(w % 2))\
                    .then_inc(ctxT_out, 1)
            for w in range(TT // 2):
                act.wait_ge(x2_turned, w + 1)
                act.copy(x2T[:, w % 2, 512 * (w // 2):512 * (w // 2) + 512], bank(4 + w % 4))\
                    .then_inc(x2T_out, 1)

            act.wait_ge(late_in, 16 * LATE)
            for n in range(2):
                c = slice(512 * n, 512 * n + 512)
                act.wait_ge(seq_made, 3 * n + 3)
                act.activation(gate_c[:, c], bank(4 + n), ACT.Tanh, bias=bp_c[:, 0:1]).then_inc(tanh_done, 1)
            for n in range(2):
                c = slice(512 * n, 512 * n + 512)
                act.wait_ge(neg_abs, n + 1)
                act.activation(gate_e[:, c], gate_e[:, c], ACT.Exp).then_inc(soft_exp, 1)
            act.wait_ge(decay_e, 1)
            act.activation(decay[:, 2:4], decay[:, 2:4], ACT.Ln, bias=1.0).then_inc(decay_e, 1)
            for n in range(2):
                c = slice(512 * n, 512 * n + 512)
                act.wait_ge(soft_exp, n + 1)
                act.activation(gate_e[:, c], gate_e[:, c], ACT.Ln, bias=1.0).then_inc(soft_log, 1)
            for w in range(8):
                act.wait_ge(x3T_made, w + 1)
                act.activation(x3T[:, w % 2, 512 * (w // 2):512 * (w // 2) + 512], bank(w % 4), ACT.Identity,
                               bias=bo_col[:, w % 2:w % 2 + 1]).then_inc(x3T_out, 1)
            act.wait_ge(logits_out, 1)
            act.activation(route[:], route[:], ACT.Sigmoid).then_inc(route_done, 1)
            for w in range(TT // 2):
                act.wait_ge(x3_turned, w + 1)
                act.copy(x3_tm[:, 2 * w:2 * w + 2, 0:C], bank(3 + w % 4).rearrange("p (i c) -> p i c", i=2))\
                    .then_inc(x3_out, 1)

            def gelu_tile(s, i):
                act.wait_ge(fh_made, s + 1)
                after(act, fh_turned, s - 1)
                act.activation(fh[i][:].rearrange("p (h n) -> p h n", h=2), psum[:, 2 * i:2 * i + 2, :],
                               ACT.Gelu).then_inc(fh_out, 1)

            def turn_tile(s, i):
                act.wait_ge(fh_turned, s + 1)
                after(act, fo_made, s - 1)
                act.copy(fhT[i][:, 0:4, :].rearrange("p f n -> p (f n)"), bank(4)).then_inc(fhT_act, 1)

            act.wait_ge(scattered, 16 * TT)
            gelu_tile(0, 0)
            turn_tile(0, 0)
            with act.Fori(1, TILES, 2) as s:
                gelu_tile(s, 1)
                turn_tile(s, 1)
                gelu_tile(s + 1, 0)
                turn_tile(s + 1, 0)

        @block.vector
        def _(dve):
            def chain(s):
                n = [0]

                def link(ins, *also):
                    n[0] += 1
                    ins.then_inc(s, 1)
                    dve.wait_ge(s, n[0])
                return link

            def stt(out, in0, scalar, in1, op0, op1):
                return dve.scalar_tensor_tensor(out=out, in0=in0, scalar=scalar, in1=in1, op0=op0, op1=op1)

            def lo_part(m):
                dve.wait_ge(hi_out, m + 1)
                src = bank(m % 8)
                if m < 8:
                    c = slice(512 * (m // 2 % 2), 512 * (m // 2 % 2) + 512)
                    dst, hi = x_lo[m // 4][:, m % 2, c], x_hi[m // 4][:, m % 2, c]
                elif m < 10:
                    dst, hi = wq_l[:, m - 8, 0:512], wq_h[:, m - 8, 0:512]
                else:
                    src = src.rearrange("p (k r) -> p k r", k=CK)
                    dst, hi = wq_l[:, :, 512:768], wq_h[:, :, 512:768]
                dve.tensor_tensor(dst, src, hi.bitcast(F32), ALU.subtract).then_inc(lo_out, 1)

            link = chain(gate_step)
            for m in range(4):
                lo_part(m)
            dve.wait_ge(gate_exp, 1)
            link(dve.tensor_scalar(sil[:, 1], sil[:, 0], 1.0, None, ALU.add))
            link(dve.reciprocal(sil[:, 0], sil[:, 1]))
            link(dve.tensor_tensor(sil[:, 2], sil[:, 0], cond_col[:], ALU.mult))
            dve.wait_ge(region_sums, 2)
            dve.tensor_copy(reg_sum[:], bank(7)[:, 0:12].rearrange("p (b k r) -> p k b r", k=CK, b=NB))\
                .then_inc(sums_out, 1)
            dve.wait_ge(sums_out, 1)
            part = [reg_sum[:, :, :, r] for r in range(3)]
            link(dve.tensor_tensor(gate_in[:, 1], part[0], part[2], ALU.add))
            link(dve.tensor_tensor(gate_in[:, 0], gate_in[:, 1], part[1], ALU.add))
            link(dve.tensor_tensor(gate_in[:, 2], part[1], part[2], ALU.add))
            link(dve.tensor_scalar(gate_in[:, 0], gate_in[:, 0], 1.0 / L, None, ALU.mult))
            dve.tensor_scalar(gate_in[:, 1:3], gate_in[:, 1:3], 1.0 / (L - L3), None, ALU.mult)\
                .then_inc(gate_in_made, 1)
            for m in range(4, 11):
                lo_part(m)
            dve.wait_ge(gate_logits, 1)
            link(dve.tensor_tensor(gs[:, 0, 0:NE], bank(5)[0:NB, 0:NE], gate_bias[:], ALU.add))
            link(dve.tensor_tensor(gs[:, 1, :], bank(5)[0:NB, 8:16], time_bias[:], ALU.add))
            link(dve.tensor_scalar(gs[:, 2, 0:NE], gs[:, 1, 0:NE], 1.0, None, ALU.add))
            link(dve.tensor_tensor(gs[:, 3, 0:NE], gs[:, 0, 0:NE], gs[:, 2, 0:NE], ALU.mult))
            link(dve.tensor_tensor(gs[:, 4, 0:NE], gs[:, 3, 0:NE], gs[:, 1, NE:2 * NE], ALU.add))
            link(dve.tensor_reduce(gsc[:, 0:1], gs[:, 4, 0:NE], AX, ALU.max))
            dve.tensor_scalar(gs[:, 5, 0:NE], gs[:, 4, 0:NE], gsc[:, 0:1], None, ALU.subtract)\
                .then_inc(gate_logits, 1)
            dve.wait_ge(gate_exp, 2)
            link(dve.tensor_reduce(gsc[:, 1:2], gs[:, 6, 0:NE], AX, ALU.add))
            link(dve.reciprocal(gsc[:, 2:3], gsc[:, 1:2]))
            link(dve.tensor_scalar(gs[:, 7, 0:NE], gs[:, 6, 0:NE], gsc[:, 2:3], None, ALU.mult))
            for k in range(TOPK):
                left = gs[:, 7 if k == 0 else 10, 0:NE]
                link(dve.tensor_reduce(gsc[:, 3 + k:4 + k], left, AX, ALU.max))
                link(dve.tensor_scalar(gs[:, 11, 0:NE], left, gsc[:, 3 + k:4 + k], None, ALU.is_equal))
                link(stt(gs[:, 11, 0:NE], gs[:, 11, 0:NE], -8.0, iota_e[0:NB, 0:NE], ALU.mult, ALU.add))
                link(dve.tensor_reduce(gsc[:, 5 + k:6 + k], gs[:, 11, 0:NE], AX, ALU.min))
                link(dve.tensor_scalar(gs[:, 8 + k, 0:NE], gs[:, 11, 0:NE], gsc[:, 5 + k:6 + k], None,
                                       ALU.is_equal))
                if k == 0:
                    link(stt(gs[:, 10, 0:NE], gs[:, 8, 0:NE], -2.0, left, ALU.mult, ALU.add))
            link(dve.tensor_scalar(gsc[:, 7:8], gsc[:, 3:4], gsc[:, 4:5], 1e-8, ALU.add, ALU.add))
            link(dve.reciprocal(gsc[:, 8:9], gsc[:, 7:8]))
            link(dve.tensor_scalar(gs[:, 5, 0:2], gsc[:, 3:5], gsc[:, 8:9], None, ALU.mult))
            link(dve.tensor_scalar(gs[:, 5, 2:4], gsc[:, 5:7], 8.0, None, ALU.add))
            link(dve.tensor_scalar(gs[:, 10, 0:NE], gs[:, 8, 0:NE], gs[:, 5, 0:1], None, ALU.mult))
            stt(gs[:, 5, 4:8], gs[:, 9, 0:NE], gs[:, 5, 1:2], gs[:, 10, 0:NE], ALU.mult, ALU.add)\
                .then_inc(gate_rows_made, 1)
            dve.wait_ge(gate_wide, 1)
            link(dve.tensor_copy(picked[:].rearrange("p b n -> p (b n)"), bank(6)[:, 0:16]))
            dve.tensor_copy(expert_i[:], picked[0:1, :, 2:4]).then_inc(experts_known, 1)
            link(dve.memset(scale_col[:], 1.0))
            by_pass = scale_col[:].rearrange("p (b j q) r -> p b j q r", b=NB, j=3)
            for q in range(2):
                for r, left_out in ((0, 2.0), (1, 1.0)):
                    stt(by_pass[:, :, 1:3, q, r], picked[:, :, 2:4], left_out, picked[:, :, 0:2],
                        ALU.not_equal, ALU.mult)
                dve.tensor_copy(by_pass[:, :, 1:3, q, 2], picked[:, :, 0:2])
            dve.wait_ge(bias_in, 16 * 3)
            link(dve.tensor_tensor(eb2w[:], wide(eb2_col[:], 2, NB), wide(picked[:, :, 4:8], 1, CK), ALU.mult))
            of = [eb2w[:, :, :, e] for e in range(NE)]
            bias = [bias_col[:, :, :, r] for r in range(3)]
            link(dve.tensor_tensor(bias[2], of[0], of[3], ALU.add))
            link(dve.tensor_tensor(bias[0], bias[2], of[1], ALU.add))
            link(dve.tensor_tensor(bias[1], bias[2], of[2], ALU.add))
            link(dve.tensor_tensor(bias[2], bias[0], of[2], ALU.add))
            for b in range(NB):
                link(dve.tensor_tensor(bias_col[:, :, b, :], bias_col[:, :, b, :], wide(sb2_col[:], 2, 3),
                                       ALU.add))

            def split_quad(q, between=None):
                for k in range(8):
                    v = 8 * q + k
                    if between and k % 2 == 1:
                        between(k // 2)
                    dve.wait_ge(gelu_done, v + 1)
                    after(dve, unit_done, v - 3)
                    cuts = CUTS[k % 2]
                    w = [scale_col[:, bass.ds(q, 1), r].rearrange("p q -> p q") for r in range(3)]
                    for n, (x0, x1, r) in enumerate(cuts):
                        ins = dve.tensor_scalar(hh[k % 4][:, x0:x1], hid[k % 4][:, x0:x1], w[r], None, ALU.mult)
                    ins.then_inc(h_part, 1)
                    dve.wait_ge(h_part, v + 1)
                    for n, (x0, x1, r) in enumerate(cuts):
                        ins = stt(hl[k % 4][:, x0:x1], hid[k % 4][:, x0:x1], w[r],
                                  hh[k % 4][:, x0:x1].bitcast(F32), ALU.mult, ALU.subtract)
                    ins.then_inc(h_split, 1)

            def y_out(b):
                dve.wait_ge(unit_done, (b + 1) * 2 * 3 * FC)
                after(dve, qkv_made, b * LT)
                for n in range(4):
                    t, c = n // 2, n % 2
                    y = bank(4 + n)
                    for x0, x1, r in CUTS[t]:
                        ins = dve.tensor_scalar(y_hi[:, c, 512 * t + x0:512 * t + x1], y[:, x0:x1],
                                                bias_col[:, c, b, r:r + 1], None, ALU.add)
                    ins.then_inc(y_part, 1)
                for n in range(4):
                    t, c = n // 2, n % 2
                    y = bank(4 + n)
                    dve.wait_ge(y_part, 4 * b + n + 1)
                    for x0, x1, r in CUTS[t]:
                        ins = stt(y_lo[:, c, 512 * t + x0:512 * t + x1], y[:, x0:x1],
                                  bias_col[:, c, b, r:r + 1],
                                  y_hi[:, c, 512 * t + x0:512 * t + x1].bitcast(F32), ALU.add, ALU.subtract)
                    ins.then_inc(y_split, 1)

            dve.wait_ge(late_in, 16 * LATE)
            dve.tensor_scalar(decay[:, 2:4], decay[:, 0:2], -1.0, None, ALU.mult).then_inc(decay_step, 1)
            dve.wait_ge(decay_step, 1)
            dve.tensor_tensor(decay[:, 2:4], decay[:, 2:4], decay[:, 0:2], ALU.min).then_inc(decay_step, 1)

            nlink = chain(norm_step)

            def sum_squares(b, n):
                dve.wait_ge(squared[b], n + 1)
                after(dve, normed, 4 * b)
                dve.tensor_reduce(ssum[:, 2 * n:2 * n + 2, :],
                                  square[n % 2][:].rearrange("p i (h d) -> p i h d", d=D), AX, ALU.add)\
                    .then_inc(summed, 1)

            def mean_squares(b):
                dve.wait_ge(summed, 4 * (b + 1))
                dve.tensor_scalar(ssum[:, :, 0:2 * H], ssum[:, :, 0:2 * H], 1.0 / D, RMS_EPS,
                                  ALU.mult, ALU.add).then_inc(var_made, 1)
                nlink(dve.tensor_scalar(ssum[:, :, 2 * H:], ssum[:, :, 2 * H:], NORM_EPS ** 2, None, ALU.max))
                dve.reciprocal(v_inv2[:, b * LT:(b + 1) * LT, :], ssum[:, :, 2 * H:])

            def norm(b, n):
                if n == 0:
                    dve.wait_ge(rooted, b + 1)
                    nlink(dve.reciprocal(ssum[:, :, 0:2 * H], ssum[:, :, 0:2 * H]))
                qk = qk_tm[b][:, 2 * n:2 * n + 2, :].rearrange("p i (h d) -> p i h d", d=D)
                dve.tensor_tensor(qk, qk, wide(ssum[:, 2 * n:2 * n + 2, 0:2 * H], 3, D), ALU.mult)\
                    .then_inc(normed, 1)

            def part_three(w):
                dve.wait_ge(part2, w + 1)
                c = slice(512 * (w % 2), 512 * (w % 2) + 512)
                dve.tensor_tensor(parts[w // 2 % 2][:, 2, c], rest[:, w % 2, :], parts[w // 2 % 2][:, 1, c],
                                  ALU.subtract).then_inc(part3, 1)

            def parts_three(w0):
                for w in range(w0, w0 + 4):
                    dve.wait_ge(part1, w + 1)
                    c = slice(512 * (w % 2), 512 * (w % 2) + 512)
                    after(dve, part3, w - 1)
                    dve.tensor_tensor(rest[:, w % 2, :], bank(2 + w % 2), parts[w // 2 % 2][:, 0, c],
                                      ALU.subtract).then_inc(rest1, 1)
                    if w > w0:
                        part_three(w - 1)
                part_three(w0 + 3)

            split_quad(0)
            with dve.Fori(1, QB) as q:
                split_quad(q)
            y_out(0)
            dve.wait_ge(qkv_made, LT)
            split_quad(QB, lambda n: sum_squares(0, n))
            mean_squares(0)
            split_quad(QB + 1, lambda n: norm(0, n))
            parts_three(0)
            split_quad(QB + 2)
            split_quad(QB + 3)
            parts_three(4)
            with dve.Fori(QB + 4, QUADS) as q:
                split_quad(q)
            y_out(1)

            for n in range(LT // 2):
                sum_squares(1, n)
            mean_squares(1)
            for n in range(LT // 2):
                norm(1, n)
            plink = chain(part_step)

            def three_parts(k):
                r = turns(min(k, 1)).index(("qk", k)) % 3
                src = psum[:, 2 * r:2 * r + 2, :]
                p1, p2, p3 = [parts[k % 2][:, n, :].rearrange("p (h n) -> p h n", h=2) for n in range(3)]
                dve.wait_ge(turned_b, k + 1)
                dve.wait_ge(parts_out[k % 2], 16 * (2 + k // 2))
                dve.wait_ge(part3, 8 + k)
                plink(dve.tensor_copy(p1, src))
                dve.tensor_tensor(rest[:], src, p1, ALU.subtract).then_inc(turned_b_read, 1)
                dve.wait_ge(turned_b_read, k + 1)
                plink(dve.tensor_copy(p2, rest[:]))
                dve.tensor_tensor(p3, rest[:], p2, ALU.subtract).then_inc(part3, 1)

            def finish_group(b, hg):
                g = (H // HG) * b + hg
                dve.wait_ge(av_done, LT * (g + 1))
                after(dve, ctx_done, g)
                after(dve, y_turned, g)
                dve.tensor_copy(yT[:].rearrange("p (h n) -> p h n", h=2), psum[:, 6:8, :]).then_inc(yT_out, 1)
                dve.wait_ge(y_turned, g + 1)
                y = psum[:, 2:4, :].rearrange("p h (i j d) -> p (h i) j d", j=HG, d=VW)
                dve.reciprocal(y_r[:], y[:, :, :, D]).then_inc(post_step, 1)
                dve.wait_ge(post_step, 5 * g + 1)
                v = v_tm[:, bass.ds(b * LT, LT), bass.ds(hg * HG * D, HG * D)].rearrange(
                    "p i (j d) -> p i j d", d=D)
                dve.tensor_tensor(y_tm[:], y[:, :, :, 0:D], wide(y_r[:], 3, D), ALU.mult).then_inc(y_read, 1)
                dve.wait_ge(y_read, g + 1)
                dve.tensor_tensor(y_dot[:], y_tm[:], v, ALU.mult).then_inc(post_step, 1)
                dve.wait_ge(post_step, 5 * g + 2)
                dve.tensor_reduce(y_d[:], y_dot[:], AX, ALU.add).then_inc(post_step, 1)
                dve.wait_ge(post_step, 5 * g + 3)
                dve.tensor_tensor(y_d[:], y_d[:], v_inv2[:, bass.ds(b * LT, LT), bass.ds(hg * HG, HG)], ALU.mult)\
                    .then_inc(post_step, 1)
                dve.wait_ge(post_step, 5 * g + 4)
                dve.tensor_tensor(y_dot[:], v, wide(y_d[:], 3, D), ALU.mult).then_inc(post_step, 1)
                dve.wait_ge(post_step, 5 * g + 5)
                dve.tensor_tensor(ctx_tm[:, bass.ds(b * LT, LT), bass.ds(hg * HG * D, HG * D)].rearrange(
                    "p i (j d) -> p i j d", d=D), y_tm[:], y_dot[:], ALU.subtract).then_inc(ctx_done, 1)

            three_parts(0)
            finish_group(0, 0)
            for k in range(1, 4):
                three_parts(k)
            finish_group(0, 1)
            with dve.Fori(2, H // HG) as hg:
                finish_group(0, hg)
            with dve.Fori(0, H // HG) as hg:
                finish_group(1, hg)

            for w in range(TT // 2):
                dve.wait_ge(proj_made, w + 1)
                two = x_tm[:, 2 * w:2 * w + 2, :]
                dve.tensor_tensor(two, bank(2 + w % 2).rearrange("p (i c) -> p i c", i=2), two, ALU.add)\
                    .then_inc(x2_done, 1)

            dve.wait_ge(late_in, 16 * LATE)
            for b in range(NB):
                dve.wait_ge(x2T_out, 4 * b + 4)
                for c in range(CK):
                    s = slice(b * L, (b + 1) * L)
                    dve.tensor_scalar(convT[:, c, s], x2T[:, c, s], cond_col[:, c, 1:2], convb_col[:, c:c + 1],
                                      ALU.mult, ALU.add).then_inc(conv_part, 1)
                for c in range(CK):
                    dve.wait_ge(conv_part, 2 * b + c + 1)
                    s = slice(b * L + 1, (b + 1) * L)
                    ins = stt(convT[:, c, s], x2T[:, c, b * L:(b + 1) * L - 1], cond_col[:, c, 0:1],
                              convT[:, c, s], ALU.mult, ALU.add)
                ins.then_inc(conv_done, 1)

            link = chain(seq_step)
            for n in range(2):
                c = slice(512 * n, 512 * n + 512)
                dve.wait_ge(seq_made, 3 * n + 1)
                link(dve.tensor_scalar(gate_b[:, c], bank(n), bp_b[:, 0:1], None, ALU.add))
                stt(gate_e[:, c], gate_b[:, c], -1.0, gate_b[:, c], ALU.mult, ALU.min).then_inc(neg_abs, 1)
                dve.wait_ge(seq_made, 3 * n + 2)
                link(dve.tensor_scalar(seq_u[:, c], bank(2 + n), bs_col[:, 0:1], None, ALU.add))
            dve.wait_ge(decay_e, 2)
            decay_link = chain(decay_step2)
            decay_link(stt(decay[:, 4:6], decay[:, 0:2], 0.0, decay[:, 2:4], ALU.max, ALU.add))
            decay_link(dve.tensor_tensor(decay[:, 6:7], decay[:, 4:5], decay[:, 5:6], ALU.mult))
            decay_link(dve.tensor_scalar(decay[:, 6:7], decay[:, 6:7], -1.0, 1.0, ALU.mult, ALU.add))
            for n in range(2):
                c = slice(512 * n, 512 * n + 512)
                dve.wait_ge(soft_log, n + 1)
                link(stt(gate_b[:, c], gate_b[:, c], 0.0, gate_e[:, c], ALU.max, ALU.add))
                link(stt(gate_b[:, c], gate_b[:, c], decay[:, 5:6], seq_u[:, c], ALU.mult, ALU.mult))
            link(dve.tensor_tensor_scan(gate_e[:], decay[:, 6:7].to_broadcast([P, L]), gate_b[:], 0.0,
                                        ALU.mult, ALU.add))
            dve.wait_ge(tanh_done, 2)
            dve.tensor_tensor(gate_e[:], gate_e[:], gate_c[:], ALU.mult).then_inc(state_out, 1)

            link = chain(rstep)
            dve.wait_ge(logits_made, 1)
            dve.tensor_tensor(route[:], bank(7)[:, 0:TT * RE].rearrange("p (i e) -> p i e", e=RE),
                              wide(br_row[:], 1, TT), ALU.add).then_inc(logits_out, 1)
            dve.wait_ge(route_done, 1)
            link(dve.tensor_reduce(prob[:], route[:], AX, ALU.max))
            link(dve.tensor_tensor(rt[0][:], route[:], wide(prob[:], 2, RE), ALU.is_equal))
            link(stt(rt[1][:], rt[0][:], -float(RE), wide(iota_e[:], 1, TT), ALU.mult, ALU.add))
            link(dve.tensor_reduce(sl[:], rt[1][:], AX, ALU.min))
            onehot = rt[2]
            dve.tensor_copy(x3_tm[:, :, C], prob[:])
            dve.tensor_copy(x3_tm[:, :, C + 1], token[:]).then_inc(tail_made, 1)
            stt(onehot[:], wide(iota_e[:], 1, TT), -float(RE), wide(sl[:], 2, RE), ALU.add, ALU.is_equal)\
                .then_inc(onehot_done, 1)
            dve.wait_ge(ranks_made, 1)
            within = bank(0)[:, 0:TT * RE].rearrange("p (i e) -> p i e", e=RE)
            link(dve.tensor_copy(rt[3][:].rearrange("p i e -> p (i e)"), bank(1)[:, 0:TT * RE]))
            total, k, step = rt[3], 3, 1
            while step < TT:
                src, dst = rt[k], rt[k + 1]
                dve.tensor_copy(dst[:, 0:step, :], src[:, 0:step, :])
                link(dve.tensor_tensor(dst[:, step:, :], src[:, step:, :], src[:, 0:TT - step, :], ALU.add))
                k, step = k + 1, 2 * step
            running = rt[k]
            link(dve.tensor_tensor(rt[0][:], running[:], total[:], ALU.subtract))
            link(dve.tensor_tensor(rt[1][:], within, rt[0][:], ALU.add))
            link(dve.tensor_tensor(rk[0][:], wide(running[:, TT - 1, :], 2, TT), wide(iota_tok[:], 1, RE),
                                   ALU.is_gt))
            link(dve.tensor_reduce(re[0][:], rk[0][:], AX, ALU.add))
            link(dve.tensor_scalar(re[1][:], re[0][:], 1.0, None, ALU.max))
            link(dve.tensor_tensor_scan(re[2][:], ones[:, 0:RE], re[1][:], 0.0, ALU.mult, ALU.add))
            link(dve.tensor_tensor(re[3][:], re[2][:], re[1][:], ALU.subtract))
            link(stt(rt[8][:], wide(re[3][:], 1, TT), float(P), rt[1][:], ALU.mult, ALU.add))
            link(dve.tensor_tensor(rt[0][:], rt[8][:], onehot[:], ALU.mult))
            link(dve.tensor_reduce(sl[:], rt[0][:], AX, ALU.add))
            dve.tensor_copy(slot_i[:], sl[:]).then_inc(slots_done, 1)
            link(dve.tensor_tensor(tl[:], wide(iota_tile[:], 2, RE), wide(re[2][:], 1, TILES), ALU.is_ge))
            link(dve.tensor_reduce(tf[:], tl[:], AX, ALU.add))
            link(dve.tensor_scalar(tf[:], tf[:], float(RE - 1), None, ALU.min))
            dve.tensor_scalar(tile_i[:], tf[:], -1.0, float(RE - 1), ALU.mult, ALU.add).then_inc(slots_done, 1)

            def x_tile(s, i):
                dve.wait_ge(xs_turned, s + 1)
                after(dve, fh_made, s - 1)
                dve.tensor_copy(xsT[i][:].rearrange("p k n -> p (k n)"), bank(6)[:, 0:C]).then_inc(xsT_out, 1)

            def tail(s, i, n):
                dve.wait_ge(xs_in[i], 16 * n + 16)
                after(dve, out_stored[i], 16 * n)
                dve.tensor_copy(prob_s[i][:], xs[i][:, C:C + 1])
                dve.tensor_copy(tok_s[i][:], xs[i][:, C + 1:]).then_inc(tail_read, 1)

            def h_tile(s, i):
                dve.wait_ge(fh_turned, s + 1)
                after(dve, fo_made, s - 1)
                dve.tensor_copy(fhT[i][:, 4:8, :].rearrange("p f n -> p (f n)"), bank(5)).then_inc(fhT_dve, 1)

            def o_tile(s, i, n):
                dve.wait_ge(fo_made, s + 1)
                dve.wait_ge(x2s_in[i], 16 * n + 16)
                dve.wait_ge(tail_read, s + 1)
                after(dve, out_stored[i], 16 * n)
                stt(fo[i][:], bank(7)[:, 0:C], prob_s[i][:, 0:1], x2s[i][:], ALU.mult, ALU.add)\
                    .then_inc(fo_out, 1)

            def tile(s, i, n, last=False):
                h_tile(s, i)
                if not last:
                    tail(s + 1, 1 - i, n + i)
                o_tile(s, i, n)

            dve.wait_ge(scattered, 16 * TT)
            x_tile(0, 0)
            x_tile(1, 1)
            tail(0, 0, 0)
            for s in range(3):
                tile(s, s % 2, s // 2)
                x_tile(s + 2, s % 2)
            with dve.Fori(1, (TILES - 3) // 2) as m:
                tile(2 * m + 1, 1, m)
                x_tile(2 * m + 3, 1)
                tile(2 * m + 2, 0, m + 1)
                x_tile(2 * m + 4, 0)
            tile(TILES - 2, 1, (TILES - 3) // 2)
            tile(TILES - 1, 0, (TILES - 1) // 2, last=True)

        @block.tensor
        def _(pe):
            def region_sum(b):
                for c in range(CK):
                    o = bank(7)[:, (b * CK + c) * 3:(b * CK + c) * 3 + 3]
                    for i in range(LT):
                        ins = pe.matmul(o, x_tm[:, b * LT + i, c * P:(c + 1) * P], region_mask[:, i, :],
                                        start=(i == 0), stop=(i == LT - 1))
                ins.then_inc(region_sums, 1)

            pe.wait_ge(consts_made, 1)
            for m in range(12):
                if m == 0 or m == 4:
                    pe.wait_ge(x_in[m // 4], 16)
                    region_sum(m // 4)
                if m == 7:
                    pe.wait_ge(sums_out, 1)
                if m == 8:
                    pe.wait_ge(wproj_in, 32)
                if m >= 8:
                    pe.wait_ge(lo_out, m - 7)
                for n in range(4):
                    if m < 8:
                        c, i = m % 2, 4 * (m // 2) + n
                        src = x_tm[:, i, c * P:(c + 1) * P]
                    elif m < 10:
                        src = qkv_raw[:, n, (m - 8) * P:(m - 7) * P]
                    else:
                        c, r = n // 2, n % 2
                        src = (qkv_raw[:, 4 + r, :] if m == 10 else proj_raw[:, r, :])[:, c * P:(c + 1) * P]
                    ins = pe.transpose(bank(m % 8)[:, n * P:(n + 1) * P], src, ident[:])
                ins.then_inc(setup_filled, 1)

            pe.wait_ge(gate_in_made, 1)
            pe.wait_ge(const_in, 16 * CONSTS)
            pe.wait_ge(lo_out, 6)
            for c in range(CK):
                pe.matmul(bank(5)[0:NB, 8:16], sil[:, 2, c, :], time_rows[:, c, :], start=(c == 0), stop=(c == CK - 1))
            for n in range(3 * CK):
                ins = pe.matmul(bank(5)[0:NB, 0:NE], gate_in[:, n // CK, n % CK, :], gate_rows[:, n, :],
                                start=(n == 0), stop=(n == 3 * CK - 1))
            ins.then_inc(gate_logits, 1)

            def three(o, w, x, first, last):
                for n, (i, j) in enumerate(((0, 0), (0, 1), (1, 0))):
                    ins = pe.matmul(o, w[i], x[j], start=first and n == 0, stop=last and n == 2)
                return ins

            def up(b, v, k):
                j, t = k // 2, k % 2
                u = v // 2 if isinstance(v, int) else None
                if t == 0:
                    pe.wait_ge(w_split, 4 * (v - k) // 8 + j + 1 if u is not None else (v - k) // 2 + j + 1)
                after(pe, gelu_done, v - 3)
                s = slice(512 * t, 512 * t + 512)
                for c in range(CK):
                    ins = three(bank(k % 4), (w1h[j][:, c, :], w1l[j][:, c, :]),
                                (x_hi[b][:, c, s], x_lo[b][:, c, s]),
                                c == 0, c == CK - 1)
                ins.then_inc(hid_made, 1)

            def down(b, v, k, first, last):
                j, t = k // 2, k % 2
                pe.wait_ge(h_split, v + 1)
                for c in range(CK):
                    s = slice(c * P, (c + 1) * P)
                    ins = three(bank(4 + 2 * t + c), (w2h[j][:, s], w2l[j][:, s]), (hh[k % 4][:], hl[k % 4][:]),
                                first, last)
                ins.then_inc(unit_done, 1)

            def quad(b, q, first=False, last=False):
                for k in range(8):
                    if k < 6:
                        up(b, 8 * q + k + 2, k + 2)
                    elif not last:
                        up_next(b, q, k - 6)
                    down(b, 8 * q + k, k, first and k < 2, last and k >= 6)

            def up_next(b, q, k):
                up(b, 8 * (q + 1) + k, k)

            def turn_qk(w0):
                for w in range(w0, w0 + 4):
                    if w == w0:
                        pe.wait_ge(normed, 4)
                        pe.wait_ge(gelu_done, 8 * (QB + 2 + w0 // 2))
                    elif w >= w0 + 2:
                        pe.wait_ge(rest1, w - 1)
                    for n in range(4):
                        ins = pe.transpose(bank(2 + w % 2)[:, n * P:(n + 1) * P],
                                           qk_tm[0][:, 4 * (w % 2) + n, (w // 2) * P:(w // 2 + 1) * P], ident[:])
                    ins.then_inc(turned, 1)
                pe.wait_ge(rest1, w0 + 4)

            for b in range(NB):
                q0 = b * QB
                if b:
                    pe.wait_ge(qkv_out, b * LT)
                else:
                    pe.wait_ge(lo_out, 11)
                    pe.wait_ge(hi_out, 12)
                up(b, 8 * q0, 0)
                up(b, 8 * q0 + 1, 1)
                if b:
                    pe.wait_ge(y_split, 4 * b)
                else:
                    pe.wait_ge(gate_rows_made, 1)
                    for n in range(NB):
                        ins = pe.matmul(bank(6)[:, 8 * n:8 * n + 8], pick_row[:, n, :], gs[:, 5, :],
                                        start=True, stop=True)
                    ins.then_inc(gate_wide, 1)
                    pe.wait_ge(experts_known, 1)
                quad(b, q0, first=True)
                if b:
                    quad(b, q0 + 1)
                    turn_qk(0)
                    quad(b, q0 + 2)
                    quad(b, q0 + 3)
                    turn_qk(4)
                    quad(b, q0 + 4)
                else:
                    with pe.Fori(q0 + 1, q0 + QB - 1) as q:
                        quad(b, q)
                quad(b, q0 + QB - 1, last=True)
                pe.wait_ge(y_split, 4 * b + 4)
                pe.wait_ge(lo_out, 11)
                pe.wait_ge(gelu_done, (b + 1) * 8 * QB)
                for i in range(LT):
                    if i >= 2:
                        pe.wait_ge(qkv_out, b * LT + i - 1)
                    s = slice(i * P, (i + 1) * P)
                    for c in range(CK):
                        three(bank(2 * i % 4), (y_hi[:, c, s], y_lo[:, c, s]),
                              (wq_h[:, c, 0:2 * C], wq_l[:, c, 0:2 * C]), c == 0, c == CK - 1)
                    for c in range(CK):
                        ins = three(bank((2 * i + 1) % 4)[:, 0:C], (y_hi[:, c, s], y_lo[:, c, s]),
                                    (wq_h[:, c, 2 * C:], wq_l[:, c, 2 * C:]), c == 0, c == CK - 1)
                    ins.then_inc(qkv_made, 1)

            PER = HG * LT

            def turn(g, r):
                pe.wait_ge(yT_out, g + 1)
                for i in range(LT):
                    ins = pe.transpose(psum[:, 2 * r + i // 4, (i % 4) * P:(i % 4 + 1) * P],
                                       yT[:, i * P:(i + 1) * P], ident[:])
                ins.then_inc(y_turned, 1)

            def turn_b(k, r):
                pe.wait_ge(normed, 8)
                for i in range(LT):
                    ins = pe.transpose(psum[:, 2 * r + i // 4, (i % 4) * P:(i % 4 + 1) * P],
                                       qk_tm[1][:, i, k * P:(k + 1) * P], ident[:])
                ins.then_inc(turned_b, 1)

            def pair_free(g, order, pos):
                if pos < 3:
                    if isinstance(g, int) and g == 0:
                        return
                    if isinstance(g, int) and g == 1:
                        if pos == 2:
                            pe.wait_ge(turned_b_read, 1)
                        else:
                            pe.wait_ge(exp_done, PER - 1 + pos)
                        return
                    pe.wait_ge(exp_done, PER * g + pos - 2)
                    return
                what, n = order[pos - 3]
                if what == "scores":
                    pe.wait_ge(exp_done, PER * g + n + 1)
                elif what == "turn":
                    pe.wait_ge(y_read, g)
                else:
                    pe.wait_ge(turned_b_read, n + 1)

            def scores(i, u, r):
                mt, j = u // HG, u % HG
                for h in range(2):
                    ins = pe.matmul(psum[:, 2 * r + h, :], k_stack[i][:, j, mt * P:(mt + 1) * P],
                                    q_stack[i][:, j, 512 * h:512 * h + 512], start=True, stop=True)
                ins.then_inc(scored, 1)

            def values(g, i, mt, h):
                if h == 0:
                    pe.wait_ge(exp_done, PER * g + HG * (mt + 1))
                    if mt == 0:
                        pe.wait_ge(v_ready, g + 1)
                        after(pe, yT_out, g)
                for j in range(HG):
                    ins = pe.matmul(psum[VW * j:VW * j + VW, 6 + h, :], v_ones[i][:, mt, j, :],
                                    pexp[mt % 2][:, j, 512 * h:512 * h + 512],
                                    start=(mt == 0), stop=(mt == LT - 1))
                if h == 1:
                    ins.then_inc(av_done, 1)

            def group(g, i, first=False):
                if isinstance(g, int) and g < 2:
                    pe.wait_ge(stack_in[i], 16 * 2 * TERMS)
                else:
                    pe.wait_ge(stack_in[i], 16 * TERMS * (g - i) + 16 * 2 * TERMS)
                order = turns(g)
                for pos, (what, u) in enumerate(order):
                    pair_free(g, order, pos)
                    if what == "turn":
                        turn(g - 1, pos % 3)
                    elif what == "qk":
                        turn_b(u, pos % 3)
                    else:
                        scores(i, u, pos % 3)
                        mt, j = u // HG, u % HG
                        if j % 2 and not (first and mt == 0):
                            if mt == 0:
                                values(g - 1, 1 - i, LT - 1, j // 2)
                            else:
                                values(g, i, mt - 1, j // 2)

            pe.wait_ge(qkv_out, TT)
            group(0, 0, first=True)
            group(1, 1)
            with pe.Fori(2, GROUPS, 2) as g:
                group(g, 0)
                group(g + 1, 1)
            values(GROUPS - 1, 1, LT - 1, 0)
            values(GROUPS - 1, 1, LT - 1, 1)
            pe.wait_ge(exp_done, PER * GROUPS)
            turn(GROUPS - 1, 1)

            def turn_ctx(w):
                pe.wait_ge(ctx_done, 4 if w < 4 else 8)
                after(pe, ctxT_out, w - 1)
                for n in range(4):
                    ins = pe.transpose(bank(w % 2)[:, n * P:(n + 1) * P],
                                       ctx_tm[:, 2 * w + n // 2, (n % 2) * P:(n % 2 + 1) * P], ident[:])
                ins.then_inc(ctx_turned, 1)

            pe.wait_ge(y_read, GROUPS)
            turn_ctx(0)
            for w in range(TT // 2):
                if w + 1 < TT // 2:
                    turn_ctx(w + 1)
                pe.wait_ge(ctxT_out, w + 1)
                after(pe, x2_done, w - 1)
                for n in range(4):
                    i, c = n // 2, n % 2
                    ins = pe.matmul(bank(2 + w % 2)[:, i * C:(i + 1) * C], ctxT[w % 2][:, i, c, :], projT[:, c, :],
                                    start=(c == 0), stop=(c == CK - 1))
                ins.then_inc(proj_made, 1)
            for w in range(TT // 2):
                pe.wait_ge(x2_done, 2 * (w // 2) + 2)
                after(pe, x2T_out, w - 3)
                for n in range(4):
                    ins = pe.transpose(bank(4 + w % 4)[:, n * P:(n + 1) * P],
                                       x_tm[:, 4 * (w // 2) + n, (w % 2) * P:(w % 2 + 1) * P], ident[:])
                ins.then_inc(x2_turned, 1)

            pe.wait_ge(late_in, 16 * LATE)
            pe.wait_ge(conv_done, NB)
            pe.wait_ge(x2T_out, TT // 2)
            for n in range(2):
                for k, (w, src) in enumerate(((wp_sb[:, :, 0:N], convT), (ws_sb[:], x2T),
                                              (wp_sb[:, :, N:2 * N], convT))):
                    for c in range(CK):
                        for b in range(NB):
                            s = slice(b * L + 512 * n, b * L + 512 * n + 512)
                            ins = pe.matmul(psum[half[b], 2 * k + n, :], w[:, c, :], src[:, c, s],
                                            start=(c == 0), stop=(c == CK - 1))
                    ins.then_inc(seq_made, 1)
            pe.wait_ge(state_out, 1)
            for w in range(8):
                b, n, c = w // 4, w // 2 % 2, w % 2
                after(pe, x3T_out, w - 3)
                pe.matmul(bank(w % 4), wo_sb[:, b, c * P:(c + 1) * P], gate_e[:, 512 * n:512 * n + 512],
                          start=True, stop=True).then_inc(x3T_made, 1)
            pe.wait_ge(x3T_out, 8)
            for i in range(TT):
                for c in range(CK):
                    ins = pe.matmul(bank(7)[:, i * RE:(i + 1) * RE], x3T[:, c, i * P:(i + 1) * P], wr_sb[:, c, :],
                                    start=(c == 0), stop=(c == CK - 1))
            ins.then_inc(logits_made, 1)
            for w in range(TT // 2):
                after(pe, x3_out, w - 3)
                for n in range(4):
                    i, c = 2 * w + n // 2, n % 2
                    ins = pe.transpose(bank(3 + w % 4)[:, n * P:(n + 1) * P],
                                       x3T[:, c, i * P:(i + 1) * P], ident[:])
                ins.then_inc(x3_turned, 1)
            pe.wait_ge(onehot_done, 1)
            flat = rt[2][:].rearrange("p i e -> p (i e)")
            pe.matmul(bank(0)[:, 0:TT * RE], tri[:], flat, start=True, stop=True)
            pe.matmul(bank(1)[:, 0:TT * RE], ones[:], flat, start=True, stop=True).then_inc(ranks_made, 1)

            def turn_x(s, i, n):
                pe.wait_ge(xs_in[i], 16 * n)
                after(pe, xsT_out, s)
                for c in range(CK):
                    ins = pe.transpose(bank(6)[:, c * P:(c + 1) * P], xs[i][:, c * P:(c + 1) * P], ident[:])
                ins.then_inc(xs_turned, 1)

            def expert_of(s):
                return pe.value_load(tile_i[0:1, bass.ds(s, 1)], min_val=0, max_val=RE - 1)

            def expert_up(s, i):
                if isinstance(s, int) and s < RE:
                    pe.wait_ge(expert_in[s], 32)
                e = expert_of(s)
                pe.wait_ge(xsT_out, s + 1)
                after(pe, fh_out, s - 1)
                for h in range(2):
                    for c in range(CK):
                        w = w_all[:, bass.ds(e, 1), c * FF + 512 * h:c * FF + 512 * h + 512]
                        ins = pe.matmul(psum[:, 2 * i + h, :], xsT[i][:, c, :], w.rearrange("p e n -> p (e n)"),
                                        start=(c == 0), stop=(c == CK - 1))
                ins.then_inc(fh_made, 1)
                return e

            def turn_h(s, i):
                pe.wait_ge(fh_out, s + 1)
                after(pe, fhT_act, s)
                after(pe, fhT_dve, s)
                for f in range(FC):
                    ins = pe.transpose(psum[:, 4 + f // 4, (f % 4) * P:(f % 4 + 1) * P],
                                       fh[i][:, f * P:(f + 1) * P], ident[:])
                ins.then_inc(fh_turned, 1)

            def expert_down(s, i):
                e = expert_of(s)
                pe.wait_ge(fhT_act, s + 1)
                pe.wait_ge(fhT_dve, s + 1)
                after(pe, fo_out, s)
                for f in range(FC):
                    w = w_all[:, bass.ds(e, 1), CK * FF + f * C:CK * FF + (f + 1) * C]
                    ins = pe.matmul(bank(7)[:, 0:C], fhT[i][:, f, :], w.rearrange("p e n -> p (e n)"),
                                    start=(f == 0), stop=(f == FC - 1))
                ins.then_inc(fo_made, 1)

            def tile(s, i, n, up=True, turn=True):
                turn_h(s, i)
                if up:
                    expert_up(s + 1, 1 - i)
                expert_down(s, i)
                if turn:
                    turn_x(s + 2, i, n)

            pe.wait_ge(slots_done, 2)
            turn_x(0, 0, 1)
            expert_up(0, 0)
            turn_x(1, 1, 1)
            for s in range(RE - 1):
                tile(s, s % 2, s // 2 + 2)
            with pe.Fori((RE - 1) // 2, (TILES - 3) // 2) as m:
                tile(2 * m + 1, 1, m + 2)
                tile(2 * m + 2, 0, m + 3)
            tile(TILES - 2, 1, 0, turn=False)
            tile(TILES - 1, 0, 0, up=False, turn=False)


_INS = {"x": "x", "cond": "cond_1024", "gate_w": "L0_cond_gate_w", "gate_b": "L0_cond_gate_b",
        "time_w": "L0_cond_time_w", "time_b": "L0_cond_time_b", "ew1": "L0_cond_ew1", "eb1": "L0_cond_eb1",
        "ew2": "L0_cond_ew2", "eb2": "L0_cond_eb2", "sw1": "L0_cond_sw1", "sb1": "L0_cond_sb1",
        "sw2": "L0_cond_sw2", "sb2": "L0_cond_sb2", "w_qkv": "L0_attn_w_qkv", "w_proj": "L0_attn_w_proj",
        "conv_b": "L0_cond2_conv_b", "Wp": "L0_cond2_Wp", "bp": "L0_cond2_bp", "Ws": "L0_cond2_Ws",
        "bs": "L0_cond2_bs", "A_log": "L0_cond2_A_log", "dt_log": "L0_cond2_dt_log", "Wo": "L0_cond2_Wo",
        "bo": "L0_cond2_bo", "Wr": "L0_ffn_Wr", "br": "L0_ffn_br", "W1": "L0_ffn_W1", "W2": "L0_ffn_W2"}


def kernel(**inputs):
    import numpy as _np
    import concourse.bacc as _bacc
    from concourse import mybir as _mybir
    from concourse.bass_utils import run_bass_kernel_spmd as _run

    nc = _bacc.Bacc("TRN2", target_bir_lowering=False, num_devices=1)
    arrays, args = {}, {}
    for short, name in _INS.items():
        v = _np.ascontiguousarray(inputs[name])
        arrays[f"in_{name}"] = v
        args[short] = nc.dram_tensor(f"in_{name}", v.shape, _mybir.dt.from_np(v.dtype), kind="ExternalInput").ap()
    out = nc.dram_tensor("out_0", (NB, L, C), F32, kind="ExternalOutput").ap()
    layer_kernel(nc, args, out)
    r = _run(nc, [arrays], core_ids=[0])
    return r.results[0]["out_0"]
```

```python
from contextlib import ExitStack

import concourse.bass as bass
from concourse import mybir

F32 = mybir.dt.float32
F32R = mybir.dt.float32r
BF16 = mybir.dt.bfloat16
I32 = mybir.dt.int32
ALU = mybir.AluOpType
ACT = mybir.ActivationFunctionType
AX = mybir.AxisListType.X

P = 128
NB, L, C = 2, 1024, 256
CK = C // P
T = NB * L
LT = L // P
TT = T // P
FF = 1024
FC = FF // P
NE, TOPK = 4, 2
STEPS = NB * (1 + TOPK)
QUADS = STEPS * FC // 4
QB = QUADS // NB
H, D = 16, 16
HG = 4
GROUPS = NB * H // HG
VW = 32
N = 64
RE = 8
NO_TOKEN = 2.0 * T
TILES = (T - RE) // P + RE
TW = TILES + TILES % 2
L3 = L // 3
REGION = [(0, L3), (L3, 2 * L3), (2 * L3, L)]
CUTS = [[(max(a, 512 * t) - 512 * t, min(z, 512 * t + 512) - 512 * t, r)
         for r, (a, z) in enumerate(REGION) if max(a, 512 * t) < min(z, 512 * t + 512)] for t in range(2)]
Q_PART = (0, 0, 1, 0, 2, 1)
K_PART = (0, 1, 0, 2, 0, 1)
TERMS = len(Q_PART)
RMS_EPS = 1.1920928955078125e-07
NORM_EPS = 1e-12


def layer_kernel(nc, a, out):
    with ExitStack() as ctx:
        def sem(name):
            return ctx.enter_context(nc.semaphore(name))

        base = -(-nc.sbuf_base // 64) * 64
        ARENA = 204 * 1024
        ctx.enter_context(nc.sbuf_tensor("arena", [P, ARENA // 4], F32))
        cursor = [base]

        def sb(name, shape, dt, at=None):
            size = 1
            for s in shape[1:]:
                size *= s
            size *= 2 if dt == BF16 else 4
            if at is None:
                at = cursor
            off = at[0]
            at[0] = off + -(-size // 32) * 32
            assert at[0] <= base + ARENA, (name, at[0] - base - ARENA)
            return nc.alloc_sbuf_tensor_at(name, shape, dt, offset=off)

        ident = sb("ident", [P, P], F32)
        split_at = cursor[0]
        x_tm = sb("x_tm", [P, TT, C], F32)
        v_tm = sb("v_tm", [P, TT, C], F32)
        w_hi = sb("w_hi", [P, 4, CK * 512], F32R, [split_at])
        w_lo = sb("w_lo", [P, 4, CK * 512], F32R, [split_at + 16384])
        projT = sb("projT", [P, CK, C], F32)
        cond_col = sb("cond_col", [P, CK, NB], F32)
        gate_rows = sb("gate_rows", [P, 3 * CK, NE], F32)
        time_rows = sb("time_rows", [P, CK, 2 * NE], F32)
        gate_bias = sb("gate_bias", [NB, NE], F32)
        time_bias = sb("time_bias", [NB, 2 * NE], F32)
        eb2_col = sb("eb2_col", [P, CK, NE], F32)
        sb2_col = sb("sb2_col", [P, CK], F32)
        b1_col = sb("b1_col", [P, STEPS * FC], F32)
        convb_col = sb("convb_col", [P, CK], F32)
        bp_b = sb("bp_b", [P, 1], F32)
        bp_c = sb("bp_c", [P, 1], F32)
        bs_col = sb("bs_col", [P, 1], F32)
        wp_sb = sb("wp_sb", [P, CK, 2 * N], F32)
        ws_sb = sb("ws_sb", [P, CK, N], F32)
        wo_sb = sb("wo_sb", [P, NB, C], F32)
        bo_col = sb("bo_col", [P, CK], F32)
        wr_sb = sb("wr_sb", [P, CK, RE], F32)
        br_row = sb("br_row", [P, RE], F32)
        tri = sb("tri", [P, P], F32)
        ones = sb("ones", [P, P], F32)
        iota_e = sb("iota_e", [P, RE], F32)
        iota_tok = sb("iota_tok", [P, TT], F32)
        token1 = sb("token1", [P, TT], F32)
        iota_start = sb("iota_start", [P, TW + 1], F32)
        iota_lane = sb("iota_lane", [P, P], F32)
        iota_tile = sb("iota_tile", [P, TILES], F32)
        pick_row = sb("pick_row", [NB, NB, P], F32)
        piece_sum = sb("piece_sum", [P, CK, NB, 4], F32)
        wrist_sum = sb("wrist_sum", [P, CK, NB], F32)
        gate_in = sb("gate_in", [P, 3, CK, NB], F32)
        sil = sb("sil", [P, 3, CK, NB], F32)
        gs = sb("gs", [NB, 12, 8], F32)
        gsc = sb("gsc", [NB, 12], F32)
        picked = sb("picked", [P, NB, 8], F32)
        scale_col = sb("scale_col", [P, QUADS, 3], F32)
        eb2w = sb("eb2w", [P, CK, NB, NE], F32)
        bias_col = sb("bias_col", [P, CK, NB, 3], F32)
        expert_i = sb("expert_i", [1, NB, TOPK], I32)
        decay = sb("decay", [P, 7], F32)
        route = sb("route", [P, TT, RE], F32)
        prob = sb("prob", [P, TT], F32)
        v_inv2 = sb("v_inv2", [P, TT, H], F32)
        token_s = sb("token_s", [P, TILES], I32)
        act_warm = sb("act_warm", [1, 1], F32)
        prob_s = sb("prob_s", [P, TILES], F32)
        tile_i = sb("tile_i", [P, TILES], I32)
        stage = cursor[0]

        at = [stage]
        qk_tm = [sb(f"qk_tm{b}", [P, LT, 2 * C], F32, at) for b in range(NB)]
        x_at, x_hi, x_lo = [], [], []
        for b in range(NB):
            x_at.append(at[0])
            x_hi.append(sb(f"x_hi{b}", [P, CK, L], F32R, at))
            x_lo.append(sb(f"x_lo{b}", [P, CK, L], F32R, at))
        after_x = at[0]
        raw1 = [sb(f"raw1_{i}", [P, CK, 2 * P], F32, at) for i in range(2)]
        raw2 = [sb(f"raw2_{i}", [P, 2, C], F32, at) for i in range(2)]
        w1h = [sb(f"w1h_{i}", [P, CK, P], F32R, at) for i in range(4)]
        w1l = [sb(f"w1l_{i}", [P, CK, P], F32R, at) for i in range(4)]
        w2h = [sb(f"w2h_{i}", [P, C], F32R, at) for i in range(4)]
        w2l = [sb(f"w2l_{i}", [P, C], F32R, at) for i in range(4)]
        hid = [sb(f"hid_{i}", [P, 512], F32, at) for i in range(4)]
        hh = [sb(f"hh_{i}", [P, 512], F32R, at) for i in range(4)]
        hl = [sb(f"hl_{i}", [P, 512], F32R, at) for i in range(4)]
        y_at = at[0]
        y_hi = sb("y_hi", [P, CK, L], F32R, at)
        y_lo = sb("y_lo", [P, CK, L], F32R, at)
        wq_at = at[0]
        wq_h = sb("wq_h", [P, CK, 3 * C], F32R, at)
        wq_l = sb("wq_l", [P, CK, 3 * C], F32R, at)
        qkv_raw = sb("qkv_raw", [P, 3 * CK, C], F32, [stage])
        proj_raw = sb("proj_raw", [P, CK, C], F32, [stage + 8192])
        at = [x_at[0]]
        parts = [sb(f"parts_{i}", [P, 3, L], BF16, at) for i in range(2)]
        rest = sb("rest", [P, 2, 512], F32, at)
        assert at[0] <= x_at[1]
        at = [y_at]
        square = [sb(f"square_{i}", [P, 2, 3 * C], F32, at) for i in range(2)]
        ssum = sb("ssum", [P, LT, 3 * H], F32, at)
        assert at[0] <= wq_at
        pexp = [sb("pexp_0", [P, HG, L], F32, [stage]), sb("pexp_1", [P, HG, L], F32, [x_at[1]])]
        at = [after_x]
        q_stack, k_stack = [], []
        for i in range(2):
            q_stack.append(sb(f"q_stack_{i}", [TERMS * D, HG, L], BF16, at))
            k_stack.append(sb(f"k_stack_{i}", [TERMS * D, HG, L], BF16, at))
        v_ones = [sb(f"v_ones_{i}", [P, LT, HG, VW], F32, at) for i in range(2)]
        yT = sb("yT", [P, L], F32, at)
        y_tm = sb("y_tm", [P, LT, HG, D], F32, at)
        y_dot = sb("y_dot", [P, LT, HG, D], F32, at)
        assert at[0] <= y_at
        at = [wq_at]
        y_r = sb("y_r", [P, LT, HG], F32, at)
        y_d = sb("y_d", [P, LT, HG], F32, at)
        ctx_tm = sb("ctx_tm", [P, TT, C], F32, at)
        ctxT = [sb(f"ctxT_{i}", [P, 2, CK, P], F32, at) for i in range(2)]
        after_b = at[0]
        WE = 16384
        top = base + ARENA - RE * WE
        w_all = sb("w_all", [P, RE, CK * FF + FC * C], F32, [top])
        spare = (base + ARENA - after_b) // WE
        at = [stage]
        x2T = sb("x2T", [P, CK, T], F32, at)
        convT = sb("convT", [P, CK, T], F32, at)
        gate_b = sb("gate_b", [P, L], F32, at)
        gate_e = sb("gate_e", [P, L], F32, at)
        seq_u = sb("seq_u", [P, L], F32, at)
        gate_c = sb("gate_c", [P, L], F32, at)
        x3T = sb("x3T", [P, CK, T], F32, [stage])
        x3_tm = sb("x3_tm", [P, TT, C], F32, [stage + 16384])
        rt = [sb(f"rt_{i}", [P, TT, RE], F32, at) for i in range(9)]
        onehot = rt[2]
        rk = [sb(f"rk_{i}", [P, RE, TT], F32, at) for i in range(2)]
        re = [sb(f"re_{i}", [P, RE], F32, at) for i in range(4)]
        tl = sb("tl", [P, TILES, RE], F32, at)
        tf = sb("tf", [P, TILES], F32, at)
        sl = sb("sl", [P, TT], F32, at)
        past = sb("past", [P, TT, TW + 1], F32, at)
        in_tile = sb("in_tile", [P, TT, TW], F32, at)
        tile_of = sb("tile_of", [P, TT], F32, at)
        lane = sb("lane", [P, TT], F32, at)
        tile_hot = sb("tile_hot", [P, TT, 3, TW], F32R, at)
        prob_hi = sb("prob_hi", [P, TT], F32R, at)
        prob_lo = sb("prob_lo", [P, TT], F32, at)
        no_token = sb("no_token", [P, TILES], F32, at)
        token_f = sb("token_f", [P, TILES], F32, at)
        lane_hot = sb("lane_hot", [P, TT, P], F32R, [stage + 32768])
        under_route = -(-(at[0] - top) // WE)
        at = [stage]
        xs = [sb(f"xs_{i}", [P, C], F32, at) for i in range(2)]
        x2s = [sb(f"x2s_{i}", [P, C], F32, at) for i in range(2)]
        xsT_hi = [sb(f"xsT_hi{i}", [P, CK, P], F32R, at) for i in range(2)]
        xsT_lo = [sb(f"xsT_lo{i}", [P, CK, P], F32R, at) for i in range(2)]
        fh = [sb(f"fh_{i}", [P, FF], F32, at) for i in range(2)]
        fhT_hi = sb("fhT_hi", [P, FC, P], F32R, at)
        fhT_lo = sb("fhT_lo", [P, FC, P], F32R, at)
        fo = [sb(f"fo_{i}", [P, C], F32, at) for i in range(2)]
        assert at[0] <= top

        psum = ctx.enter_context(nc.psum_tensor("psum", [P, 8, 512], F32))

        def bank(i):
            return psum[:, i, :]

        def x2_bank(w):
            return bank((2, 3, 6, 7)[w % 4])

        parts_d = nc.dram_tensor("parts_d", [NB, 4, 3, P, L], BF16).ap()
        x3_d = nc.dram_tensor("x3_d", [T, C], F32).ap()
        x2_d = nc.dram_tensor("x2_d", [T, C], F32).ap()
        out_rows = out.rearrange("b l c -> (b l) c")

        x_in = [sem(f"x_in{b}") for b in range(NB)]
        const_in = sem("const_in")
        wproj_in = sem("wproj_in")
        b1_in = sem("b1_in")
        bias_in = sem("bias_in")
        late_in = sem("late_in")
        wo_base = sem("wo_base")
        consts_made = sem("consts_made")
        pool_step = sem("pool_step")
        setup_filled = sem("setup_filled")
        hi_out = sem("hi_out")
        lo_out = sem("lo_out")
        gate_in_made = sem("gate_in_made")
        gate_logits = sem("gate_logits")
        gate_exp = sem("gate_exp")
        gate_step = sem("gate_step")
        gate_rows_made = sem("gate_rows_made")
        gate_wide = sem("gate_wide")
        experts_known = sem("experts_known")
        act_passed = sem("act_passed")
        pool_passed = sem("pool_passed")
        raw_in = [sem(f"raw_in{i}") for i in range(2)]
        w_split = sem("w_split")
        w_part = sem("w_part")
        hid_made = sem("hid_made")
        gelu_done = sem("gelu_done")
        h_part = sem("h_part")
        h_split = sem("h_split")
        unit_done = sem("unit_done")
        bias_made = sem("bias_made")
        y_part = sem("y_part")
        y_split = sem("y_split")
        qkv_made = sem("qkv_made")
        qkv_out = sem("qkv_out")
        squared = [sem(f"squared{b}") for b in range(NB)]
        summed = sem("summed")
        norm_step = sem("norm_step")
        var_made = sem("var_made")
        rooted = sem("rooted")
        normed = sem("normed")
        turned = sem("turned")
        turned_b = sem("turned_b")
        part_step = sem("part_step")
        turned_b_read = sem("turned_b_read")
        part1 = sem("part1")
        part2 = sem("part2")
        rest1 = sem("rest1")
        part3 = sem("part3")
        parts_out = [sem(f"parts_out{i}") for i in range(2)]
        stack_in = [sem(f"stack_in{i}") for i in range(2)]
        v_ready = sem("v_ready")
        v_base = sem("v_base")
        scored = sem("scored")
        exp_done = sem("exp_done")
        av_done = sem("av_done")
        yT_out = sem("yT_out")
        y_turned = sem("y_turned")
        y_read = sem("y_read")
        post_step = sem("post_step")
        ctx_done = sem("ctx_done")
        ctx_turned = sem("ctx_turned")
        ctxT_out = sem("ctxT_out")
        proj_made = sem("proj_made")
        x2_done = sem("x2_done")
        x2_turned = sem("x2_turned")
        x2T_out = sem("x2T_out")
        conv_done = sem("conv_done")
        seq_made = sem("seq_made")
        seq_step = sem("seq_step")
        decay_step = sem("decay_step")
        decay_e = sem("decay_e")
        neg_abs = sem("neg_abs")
        soft_log = sem("soft_log")
        soft_exp = sem("soft_exp")
        tanh_done = sem("tanh_done")
        state_out = sem("state_out")
        x3T_made = sem("x3T_made")
        x3T_out = sem("x3T_out")
        x3_turned = sem("x3_turned")
        x3_out = sem("x3_out")
        logits_made = sem("logits_made")
        logits_out = sem("logits_out")
        route_done = sem("route_done")
        onehot_done = sem("onehot_done")
        ranks_made = sem("ranks_made")
        rstep = sem("rstep")
        slots_done = sem("slots_done")
        lanes_made = sem("lanes_made")
        tokens_made = sem("tokens_made")
        tokens_known = sem("tokens_known")
        x3_stored = sem("x3_stored")
        expert_in = [sem(f"expert_in{e}") for e in range(RE)]
        xs_in = [sem(f"xs_in{i}") for i in range(2)]
        xs_turned = sem("xs_turned")
        x_hi_out = sem("x_hi_out")
        x_lo_out = sem("x_lo_out")
        w1_hi = sem("w1_hi")
        w1_split = sem("w1_split")
        w1_used = sem("w1_used")
        w2_hi = sem("w2_hi")
        w2_split = sem("w2_split")
        w2_used = sem("w2_used")
        fh_out = sem("fh_out")
        fh_turned = sem("fh_turned")
        fhT_hi_out = sem("fhT_hi_out")
        fhT_lo_out = sem("fhT_lo_out")
        fo_out = sem("fo_out")
        x2_stored = sem("x2_stored")
        rows_base = sem("rows_base")
        x2s_in = [sem(f"x2s_in{i}") for i in range(2)]
        out_stored = [sem(f"out_stored{i}") for i in range(2)]

        def wide(ap, axis, n):
            v = ap.unsqueeze(axis)
            shape = list(v.shape)
            shape[axis] = n
            return v.to_broadcast(shape)

        def after(eng, s, value):
            if not isinstance(value, int) or value > 0:
                eng.wait_ge(s, value)

        CONSTS = 6
        col = lambda ap: ap.rearrange("(k p) -> p k", p=P)
        half = [slice(N * b, N * b + N) for b in range(NB)]

        one = lambda ap: ap.rearrange("(n a) -> n a", a=1)
        late_consts = [(convb_col[:], col(a["conv_b"])), (bo_col[:], col(a["bo"])),
                       (wp_sb[:], a["Wp"].rearrange("(k p) n -> p k n", p=P)),
                       (ws_sb[:], a["Ws"].rearrange("(k p) n -> p k n", p=P)),
                       (wr_sb[:], a["Wr"].rearrange("(k p) e -> p k e", p=P)),
                       (br_row[:], a["br"].partition_broadcast(P))]
        for b in range(NB):
            late_consts += [(wo_sb[half[b], b, :], a["Wo"]), (bp_b[half[b], :], one(a["bp"][0:N])),
                            (bp_c[half[b], :], one(a["bp"][N:2 * N])), (bs_col[half[b], :], one(a["bs"])),
                            (decay[half[b], 0:1], one(a["A_log"])), (decay[half[b], 1:2], one(a["dt_log"]))]
        LATE = len(late_consts)

        def quarter(e, q):
            if q < 2:
                w = w_all[:, bass.ds(e, 1), 0:CK * FF].rearrange("p e (k h n) -> p (e k) h n", k=CK, h=2)
                return w[:, :, q, :]
            a0 = CK * FF + (q - 2) * 1024
            return w_all[:, bass.ds(e, 1), a0:a0 + 1024].rearrange("p e (k n) -> p (e k) n", k=CK)

        def split_quarter(w, q):
            return w[:, q, :].rearrange("p (k n) -> p k n", k=CK)

        def steps(eng, step):
            for s in range(-2, RE - 2):
                step(s, s % 2, s // 2)
            with eng.Fori((RE - 2) // 2, (TILES - 3) // 2) as m:
                step(2 * m, 0, m)
                step(2 * m + 1, 1, m)
            for s in range(TILES - 3, TILES - 1):
                step(s, s % 2, s // 2)

        def is_tile(s):
            return not isinstance(s, int) or 0 <= s < TILES

        def place_of_expert(eng, s):
            if is_tile(s):
                return eng.value_load(tile_i[0:1, bass.ds(s, 1)], min_val=0, max_val=RE - 1)

        def turns(g):
            units = [("scores", u) for u in range(HG * LT)]
            if isinstance(g, int) and g == 0:
                return units + [("qk", 0)]
            if isinstance(g, int) and g == 1:
                return (units[:8] + [("qk", 1)] + units[8:12] + [("qk", 2)] + units[12:17] + [("turn", 0)]
                        + units[17:27] + [("qk", 3)] + units[27:])
            return units[:16] + [("turn", 0)] + units[16:]

        def position(g, u):
            return turns(g).index(("scores", u))

        block = ctx.enter_context(nc.Block())

        @block.sync
        def _(sp):
            for b in range(NB):
                sp.dma_start(x_tm[:, b * LT:(b + 1) * LT, :],
                             a["x"][b].rearrange("(i p) c -> p i c", p=P)).then_inc(x_in[b], 16)
            sp.dma_start(qkv_raw[:], a["w_qkv"].rearrange("(r p) c -> p r c", p=P)).then_inc(wproj_in, 16)
            sp.dma_start(proj_raw[:], a["w_proj"].rearrange("(r p) c -> p r c", p=P)).then_inc(wproj_in, 16)

            chosen = {}

            def load_pair(s, i, k):
                n = 4 * s + 2 * i + k
                after(sp, w_split, 2 * n - 2)
                f0 = (2 * i + k) * 2 * P
                if s % 3 == 0:
                    w1, w2 = a["sw1"], a["sw2"]
                else:
                    e = chosen[s]
                    w1 = a["ew1"][bass.ds(e, 1), :, :].rearrange("e c f -> (e c) f")
                    w2 = a["ew2"][bass.ds(e, 1), :, :].rearrange("e f c -> (e f) c")
                sp.dma_start(raw1[k][:], w1.rearrange("(k p) f -> p k f", p=P)[:, :, bass.ds(f0, 2 * P)])\
                    .then_inc(raw_in[k], 16)
                sp.dma_start(raw2[k][:], w2.rearrange("(f p) c -> p f c", p=P)[:, bass.ds(f0 // P, 2), :])\
                    .then_inc(raw_in[k], 16)

            def store_parts(b, k):
                u = 4 * b + k
                sp.wait_ge(part3, 2 * u + 2 if b == 0 else 8 + k + 1)
                sp.dma_start(parts_d[b, k].rearrange("s p n -> p s n"), parts[u % 2][:])\
                    .then_inc(parts_out[u % 2], 16)

            sp.dma_start(b1_col[:, 0:FC], col(a["sb1"]),
                         allow_slow_non_contiguous=True).then_inc(b1_in, 16)
            for dst, src in ((eb2_col[:, 0, :], a["eb2"][:, 0:P].rearrange("e p -> p e")),
                             (eb2_col[:, 1, :], a["eb2"][:, P:C].rearrange("e p -> p e")),
                             (sb2_col[:], col(a["sb2"]))):
                sp.dma_start(dst, src, allow_slow_non_contiguous=True).then_inc(bias_in, 16)
            for s in range(STEPS):
                if s == 1:
                    sp.wait_ge(wo_base, 1)
                    for dst, src in late_consts:
                        sp.dma_start(dst, src, allow_slow_non_contiguous=True).then_inc(late_in, 16)
                    sp.wait_ge(experts_known, 1)
                    for s1 in range(1, STEPS):
                        src = a["sb1"]
                        if s1 % 3:
                            b, k = s1 // 3, s1 % 3 - 1
                            chosen[s1] = sp.value_load(expert_i[0:1, b, k:k + 1], min_val=0, max_val=NE - 1)
                            src = a["eb1"][bass.ds(chosen[s1], 1), :].rearrange("e f -> (e f)")
                        sp.dma_start(b1_col[:, s1 * FC:(s1 + 1) * FC], col(src),
                                     allow_slow_non_contiguous=True).then_inc(b1_in, 16)
                for i in range(2):
                    if 2 * s + i >= QUADS - 2:
                        store_parts(0, 2 * (s * 2 + i - QUADS + 2))
                        store_parts(0, 2 * (s * 2 + i - QUADS + 2) + 1)
                    for k in range(2):
                        load_pair(s, i, k)

            def load_stacks(g):
                b, hg = g // (H // HG), g % (H // HG)
                cq = hg // 2
                r = slice(HG * D * (hg % 2), HG * D * (hg % 2) + HG * D)
                if g >= 2:
                    sp.wait_ge(scored, HG * LT * (g - 1))
                for kk, (stack, order) in enumerate(((q_stack, Q_PART), (k_stack, K_PART))):
                    if g < 2 or hg % 2 == 0:
                        u = 4 * b + cq + 2 * kk
                        sp.wait_ge(parts_out[u % 2], 16 * (u // 2 + 1))
                    for t, s in enumerate(order):
                        sp.dma_start(stack[g % 2][D * t:D * t + D, :, :],
                                     parts_d[b, cq + 2 * kk, s, r, :].rearrange("(j d) n -> d j n", j=HG))\
                            .then_inc(stack_in[g % 2], 16)

            def load_expert(e):
                at_e = w_all[:, RE - 1 - e, :]
                sp.dma_start(at_e[:, 0:CK * FF].rearrange("p (k f) -> p k f", k=CK),
                             a["W1"][e].rearrange("(k p) f -> p k f", p=P)).then_inc(expert_in[e], 16)
                sp.dma_start(at_e[:, CK * FF:].rearrange("p (f c) -> p f c", f=FC),
                             a["W2"][e].rearrange("(f p) c -> p f c", p=P)).then_inc(expert_in[e], 16)

            sp.wait_ge(unit_done, 2 * FC * STEPS)
            for g in range(GROUPS):
                load_stacks(g)
                if g == 1:
                    store_parts(1, 0)
                if g == 2:
                    for k in range(1, 4):
                        store_parts(1, k)
                    for e in range(spare):
                        load_expert(e)
            for b in range(NB):
                sp.wait_ge(x2_done, (b + 1) * LT // 2)
                sp.dma_start(x2_d[b * L:(b + 1) * L, :].rearrange("(i p) c -> p i c", p=P),
                             x_tm[:, b * LT:(b + 1) * LT, :]).then_inc(x2_stored, 16)
            sp.wait_ge(proj_made, TT // 2)
            sp.wait_ge(ctxT_out, TT // 2)
            for e in range(spare, RE - under_route):
                load_expert(e)
            for b in range(NB):
                sp.wait_ge(x3_out, (b + 1) * LT // 2)
                sp.dma_start(x3_d[b * L:(b + 1) * L, :].rearrange("(i p) c -> p i c", p=P),
                             x3_tm[:, b * LT:(b + 1) * LT, :]).then_inc(x3_stored, 16)
            sp.wait_ge(tokens_known, 1)
            for i in range(2):
                sp.wait_ge(xs_in[i], 16)
            sp.wait_ge(x2s_in[0], 16)
            for e in range(RE - under_route, RE):
                load_expert(e)
            sp.wait_ge(x2_stored, 16 * NB)
            for i in range(2):
                sp.wait_ge(out_stored[i], 16 * ((TILES + 1 - i) // 2))

        @block.gpsimd
        def _(pool):
            steps = [0]

            def link(ins):
                steps[0] += 1
                ins.then_inc(pool_step, 1)
                pool.wait_ge(pool_step, steps[0])

            pool.memset(ident[:], 0.0)
            pool.memset(ones[:], 1.0)
            pool.memset(tri[:], 1.0)
            pool.memset(wo_sb[:], 0.0).then_inc(wo_base, 1)
            link(pool.memset(pick_row[:], 0.0))
            pool.affine_select(out=ident[:], in_=ident[:], compare_op=ALU.not_equal, fill=1.0, base=0,
                               pattern=[[-1, P]], channel_multiplier=1)
            pool.affine_select(out=tri[:], in_=tri[:], compare_op=ALU.is_gt, fill=0.0, base=0,
                               pattern=[[1, P]], channel_multiplier=-1)
            pool.affine_select(out=pick_row[:], in_=pick_row[:], compare_op=ALU.not_equal, fill=1.0, base=0,
                               pattern=[[-1, NB], [0, P]], channel_multiplier=1)
            pool.iota(iota_e[:], pattern=[[1, RE]], base=0, channel_multiplier=0,
                      allow_small_or_imprecise_dtypes=True)
            pool.iota(iota_tok[:], pattern=[[P, TT]], base=0, channel_multiplier=0,
                      allow_small_or_imprecise_dtypes=True)
            pool.iota(iota_start[:], pattern=[[P, TW + 1]], base=0, channel_multiplier=0,
                      allow_small_or_imprecise_dtypes=True)
            pool.iota(iota_lane[:], pattern=[[1, P]], base=0, channel_multiplier=0,
                      allow_small_or_imprecise_dtypes=True)
            pool.iota(token1[:], pattern=[[P, TT]], base=1, channel_multiplier=1,
                      allow_small_or_imprecise_dtypes=True)
            pool.iota(iota_tile[:], pattern=[[1, TILES]], base=0, channel_multiplier=0,
                      allow_small_or_imprecise_dtypes=True).then_inc(consts_made, 1)

            def split_quad(q):
                for k in range(4):
                    u = 4 * q + k
                    pair, j = k // 2, k % 2
                    if j == 0:
                        pool.wait_ge(raw_in[pair], 32 * (q + 1))
                    after(pool, unit_done, 2 * u - 6)
                    pool.sem_inc(pool_passed, 1)
                    r1, r2 = raw1[pair][:, :, j * P:(j + 1) * P], raw2[pair][:, j, :]
                    pool.tensor_copy(w1h[k][:], r1)
                    pool.tensor_copy(w2h[k][:], r2).then_inc(w_part, 1)
                    pool.wait_ge(w_part, u + 1)
                    pool.tensor_tensor(w1l[k][:], r1, w1h[k][:].bitcast(F32), ALU.subtract)
                    pool.tensor_tensor(w2l[k][:], r2, w2h[k][:].bitcast(F32), ALU.subtract)\
                        .then_inc(w_split, 1)

            split_quad(0)
            with pool.Fori(1, QUADS) as q:
                split_quad(q)

            pool.wait_ge(qkv_out, TT)
            for i in range(2):
                pool.memset(v_ones[i][:, :, :, D:VW], 0.0).then_inc(v_base, 1)
            for i in range(2):
                pool.wait_ge(v_base, i + 1)
                pool.memset(v_ones[i][:, :, :, D:D + 1], 1.0).then_inc(v_base, 1)
            for g in range(GROUPS):
                b, hg = g // (H // HG), g % (H // HG)
                if g >= 2:
                    pool.wait_ge(av_done, LT * (g - 1))
                else:
                    pool.wait_ge(v_base, 3 + g)
                pool.tensor_copy(v_ones[g % 2][:, :, :, 0:D],
                                 v_tm[:, b * LT:(b + 1) * LT, hg * HG * D:(hg + 1) * HG * D]
                                 .rearrange("p i (j d) -> p i j d", j=HG)).then_inc(v_ready, 1)
                if g == 1:
                    for n in range(LT // 2):
                        after(pool, summed, 4 + n - 1)
                        q2, v2 = qk_tm[1][:, 2 * n:2 * n + 2, :], v_tm[:, LT + 2 * n:LT + 2 * n + 2, :]
                        pool.tensor_tensor(square[n % 2][:, :, 0:2 * C], q2, q2, ALU.mult)
                        pool.tensor_tensor(square[n % 2][:, :, 2 * C:], v2, v2, ALU.mult)\
                            .then_inc(squared[1], 1)

            pool.wait_ge(x3_turned, TT // 2)
            for i in range(2):
                pool.memset(xs[i][:], 0.0)
                pool.memset(x2s[i][:], 0.0).then_inc(rows_base, 1)
            pool.wait_ge(rows_base, 2)
            pool.wait_ge(tokens_known, 1)
            pool.wait_ge(x2_stored, 16 * NB)
            pool.wait_ge(x3_stored, 16 * NB)

            def gather(dst, src, s, done):
                pool.indirect_dma_start(out=dst, out_offset=None, in_=src[:, :],
                                        in_offset=bass.IndirectOffsetOnAxis(ap=token_s[:, s:s + 1], axis=0),
                                        bounds_check=T - 1, oob_is_err=False).then_inc(done, 16)

            def load_x3(s):
                after(pool, xs_turned, s - 1)
                gather(xs[s % 2][:], x3_d, s, xs_in[s % 2])

            def load_x2(s):
                after(pool, fo_out, s - 1)
                gather(x2s[s % 2][:], x2_d, s, x2s_in[s % 2])

            load_x3(0)
            load_x3(1)
            load_x2(0)
            load_x3(2)
            for s in range(TILES):
                if s + 1 < TILES:
                    load_x2(s + 1)
                if s + 3 < TILES:
                    load_x3(s + 3)
                pool.wait_ge(fo_out, s + 1)
                pool.indirect_dma_start(out=out_rows,
                                        out_offset=bass.IndirectOffsetOnAxis(ap=token_s[:, s:s + 1], axis=0),
                                        in_=fo[s % 2][:], in_offset=None,
                                        bounds_check=T - 1, oob_is_err=False).then_inc(out_stored[s % 2], 16)

        @block.scalar
        def _(act):
            for dst, src in ((cond_col[:, 0, :], a["cond"][:, 0:P].rearrange("b p -> p b")),
                             (cond_col[:, 1, :], a["cond"][:, P:C].rearrange("b p -> p b")),
                             (gate_rows[:], a["gate_w"].rearrange("(r p) e -> p r e", p=P)),
                             (time_rows[:], a["time_w"].rearrange("(r p) e -> p r e", p=P)),
                             (gate_bias[:], a["gate_b"].partition_broadcast(NB)),
                             (time_bias[:], a["time_b"].partition_broadcast(NB))):
                act.dma_start(dst, src, allow_slow_non_contiguous=True).then_inc(const_in, 16)

            def hi_parts(m):
                act.wait_ge(setup_filled, m + 1)
                src = bank(m if m < 8 else m - 7)
                if m < 8:
                    dst = x_hi[m // 4][:, m % 2, 512 * (m // 2 % 2):512 * (m // 2 % 2) + 512]
                elif m < 10:
                    dst = wq_h[:, m - 8, 0:512]
                else:
                    src = src.rearrange("p (k r) -> p k r", k=CK)
                    dst = wq_h[:, :, 512:768] if m == 10 else projT[:]
                act.copy(dst, src).then_inc(hi_out, 1)

            for m in range(8):
                hi_parts(m)
            act.wait_ge(const_in, 16 * CONSTS)
            act.activation(sil[:, 0], cond_col[:], ACT.Exp, scale=-1.0).then_inc(gate_exp, 1)
            for m in range(8, 12):
                hi_parts(m)
            act.wait_ge(gate_logits, 2)
            act.activation(gs[:, 6, 0:NE], gs[:, 5, 0:NE], ACT.Exp).then_inc(gate_exp, 1)


            def gelu_quad(q, between=None, turns_from=None):
                for k in range(8):
                    if between and k % 2 == 1:
                        between(k // 2)
                    v = 8 * q + k
                    act.wait_ge(hid_made, v + 1)
                    after(act, h_split, v - 3)
                    act.sem_inc(act_passed, 1)
                    act.activation(hid[k % 4][:], bank(k % 4), ACT.Gelu_apprx_tanh,
                                   bias=b1_col[:, bass.ds(4 * q + k // 2, 1)]).then_inc(gelu_done, 1)
                    if turns_from is not None and k % 2 == 1:
                        first_part(turns_from + k // 2)
                    if turns_from is not None and k % 2 == 0 and turns_from + k // 2 >= 1:
                        second_part(turns_from + k // 2 - 1)

            def qkv_to_sbuf(b):
                for i in range(LT):
                    act.wait_ge(qkv_made, b * LT + i + 1)
                    act.copy(qk_tm[b][:, i, :], bank(2 * i % 4))
                    act.copy(v_tm[:, b * LT + i, :], bank((2 * i + 1) % 4)[:, 0:C]).then_inc(qkv_out, 1)

            def y_out(b):
                act.wait_ge(unit_done, (b + 1) * 2 * 3 * FC)
                if b == 0:
                    act.wait_ge(bias_made, 1)
                after(act, normed, 4 * b)
                for n in range(4):
                    t, c = n // 2, n % 2
                    for x0, x1, r in CUTS[t]:
                        ins = act.activation(y_hi[:, c, 512 * t + x0:512 * t + x1], bank(4 + n)[:, x0:x1],
                                             ACT.Identity, bias=bias_col[:, c, b, r:r + 1])
                    ins.then_inc(y_part, 1)

            act.wait_ge(b1_in, 16)
            gelu_quad(0)
            gelu_quad(1)
            act.wait_ge(b1_in, 16 * STEPS)
            with act.Fori(2, QB) as q:
                gelu_quad(q)
            y_out(0)
            qkv_to_sbuf(0)

            def squares(n):
                act.wait_ge(qkv_out, 2 * n + 2)
                after(act, summed, n - 1)
                act.activation(square[n % 2][:, :, 0:2 * C], qk_tm[0][:, 2 * n:2 * n + 2, :], ACT.Square)
                act.activation(square[n % 2][:, :, 2 * C:], v_tm[:, 2 * n:2 * n + 2, :], ACT.Square)\
                    .then_inc(squared[0], 1)

            def first_part(w):
                act.wait_ge(turned, w + 1)
                after(act, parts_out[w // 2 % 2], 16 * (w // 4))
                act.copy(parts[w // 2 % 2][:, 0, 512 * (w % 2):512 * (w % 2) + 512], bank(0 if w % 2 else 2))\
                    .then_inc(part1, 1)

            def second_part(w):
                act.wait_ge(rest1, w + 1)
                act.copy(parts[w // 2 % 2][:, 1, 512 * (w % 2):512 * (w % 2) + 512], rest[:, w % 2, :])\
                    .then_inc(part2, 1)

            def root(b):
                act.wait_ge(var_made, b + 1)
                act.activation(ssum[:, :, 0:2 * H], ssum[:, :, 0:2 * H], ACT.Sqrt).then_inc(rooted, 1)

            gelu_quad(QB, squares)
            root(0)
            gelu_quad(QB + 1)
            gelu_quad(QB + 2, turns_from=0)
            gelu_quad(QB + 3, turns_from=4)
            second_part(7)
            with act.Fori(QB + 4, QUADS) as q:
                gelu_quad(q)
            y_out(1)
            qkv_to_sbuf(1)

            def exps(g):
                for u in range(HG * LT):
                    mt, j = u // HG, u % HG
                    r = position(g, u) % 3
                    act.wait_ge(scored, HG * LT * g + u + 1)
                    if j == 0:
                        after(act, av_done, LT * g + mt - 1)
                    act.activation(pexp[mt % 2][:, j, :].rearrange("p (h n) -> p h n", h=2),
                                   psum[:, 2 * r:2 * r + 2, :], ACT.Exp, scale=D ** -0.5)\
                        .then_inc(exp_done, 1)
                    if isinstance(g, int) and g == 0 and u == 19:
                        root(1)

            act.wait_ge(decay_step, 2)
            act.activation(decay[:, 2:4], decay[:, 2:4], ACT.Exp).then_inc(decay_e, 1)
            exps(0)
            exps(1)
            with act.Fori(2, GROUPS) as g:
                exps(g)

            act.wait_ge(late_in, 16 * LATE)

            def ctx_to_sbuf(w):
                act.wait_ge(ctx_turned, w + 1)
                after(act, proj_made, w - 1)
                act.copy(ctxT[w % 2][:].rearrange("p i k n -> p (i k n)"), bank(w % 2))\
                    .then_inc(ctxT_out, 1)

            def x2_to_sbuf(w):
                c, s = w % 2, slice(512 * (w // 2), 512 * (w // 2) + 512)
                act.wait_ge(x2_turned, w + 1)
                act.activation(convT[:, c, s], x2_bank(w), ACT.Identity, bias=convb_col[:, c:c + 1],
                               scale=cond_col[:, c, 1:2])
                act.copy(x2T[:, c, s], x2_bank(w)).then_inc(x2T_out, 1)

            for w in range(4):
                ctx_to_sbuf(w)
            for w in range(4):
                x2_to_sbuf(w)
            for w in range(4, 7):
                ctx_to_sbuf(w)
            x2_to_sbuf(4)
            x2_to_sbuf(5)
            ctx_to_sbuf(7)
            x2_to_sbuf(6)
            x2_to_sbuf(7)

            for n in range(2):
                c = slice(512 * n, 512 * n + 512)
                act.wait_ge(neg_abs, n + 1)
                act.activation(gate_e[:, c], gate_e[:, c], ACT.Exp).then_inc(soft_exp, 1)
            act.wait_ge(decay_e, 1)
            act.activation(decay[:, 2:4], decay[:, 2:4], ACT.Ln, bias=1.0).then_inc(decay_e, 1)
            for n in range(2):
                c = slice(512 * n, 512 * n + 512)
                act.wait_ge(soft_exp, n + 1)
                act.activation(gate_e[:, c], gate_e[:, c], ACT.Ln, bias=1.0).then_inc(soft_log, 1)
            for n in range(2):
                c = slice(512 * n, 512 * n + 512)
                act.wait_ge(seq_made, 5 + n)
                act.activation(gate_c[:, c], bank(4 + n), ACT.Tanh, bias=bp_c[:, 0:1]).then_inc(tanh_done, 1)
            for w in range(8):
                n, b, c = w // 4, w // 2 % 2, w % 2
                act.wait_ge(x3T_made, w + 1)
                act.activation(x3T[:, c, b * L + 512 * n:b * L + 512 * n + 512], bank(w % 4), ACT.Identity,
                               bias=bo_col[:, c:c + 1]).then_inc(x3T_out, 1)
            act.wait_ge(logits_out, 1)
            act.activation(route[:], route[:], ACT.Sigmoid).then_inc(route_done, 1)
            for w in range(TT // 2):
                act.wait_ge(x3_turned, w + 1)
                act.copy(x3_tm[:, 2 * w:2 * w + 2, 0:C], bank(3 + w % 4).rearrange("p (i c) -> p i c", i=2))\
                    .then_inc(x3_out, 1)

            def act_step(s, i, m):
                e1 = place_of_expert(act, s + 1)
                e2 = place_of_expert(act, s + 2)
                if is_tile(s + 1):
                    act.wait_ge(w1_used, 2 * s + 4)
                    after(act, fh_turned, s)
                    act.activation(fh[1 - i][:].rearrange("p (h n) -> p h n", h=2),
                                   psum[:, 2 * (1 - i):2 * (1 - i) + 2, :], ACT.Gelu).then_inc(fh_out, 1)
                if is_tile(s + 2):
                    if not isinstance(s, int) or s != -2:
                        x_hi_part(s + 2, i)
                    if isinstance(s, int) and s + 2 < RE:
                        act.wait_ge(expert_in[s + 2], 32)
                    for h in range(2):
                        after(act, w1_used, 2 * s + 3 + h)
                        act.sem_inc(act_passed, 1)
                        act.copy(split_quarter(w_hi, h), quarter(e2, h)).then_inc(w1_hi, 1)
                    if isinstance(s, int) and s == -2:
                        x_hi_part(0, 0)
                if is_tile(s + 1):
                    for q in range(2):
                        after(act, w2_used, 2 * s + 1 + q)
                        act.sem_inc(act_passed, 1)
                        act.copy(split_quarter(w_hi, 2 + q), quarter(e1, 2 + q)).then_inc(w2_hi, 1)
                        if q == 0:
                            act.wait_ge(fh_turned, s + 2)
                            after(act, w2_used, 2 * s + 2)
                            for h in range(2):
                                act.copy(fhT_hi[:, 4 * h:4 * h + 4, :].rearrange("p f n -> p (f n)"), bank(4 + h))\
                                    .then_inc(fhT_hi_out, 1)

            def x_hi_part(s, i):
                act.wait_ge(xs_turned, s + 1)
                after(act, w1_used, 2 * s - 2)
                act.copy(xsT_hi[i][:].rearrange("p k n -> p (k n)"), bank(6)[:, 0:C]).then_inc(x_hi_out, 1)

            act.activation(act_warm[:], ones[0:1, 0:1], ACT.Gelu)
            act.wait_ge(x3_stored, 16 * NB)
            act.wait_ge(x2_stored, 16 * NB)
            act.wait_ge(slots_done, 1)
            steps(act, act_step)

        @block.vector
        def _(dve):
            def chain(s):
                n = [0]

                def link(ins):
                    n[0] += 1
                    ins.then_inc(s, 1)
                    dve.wait_ge(s, n[0])
                return link

            def stt(out, in0, scalar, in1, op0, op1):
                return dve.scalar_tensor_tensor(out=out, in0=in0, scalar=scalar, in1=in1, op0=op0, op1=op1)

            def lo_part(m):
                dve.wait_ge(hi_out, m + 1)
                src = bank(m if m < 8 else m - 7)
                if m < 8:
                    for n, (x0, x1, r) in enumerate(CUTS[m // 2 % 2]):
                        dve.tensor_reduce(piece_sum[:, m % 2, m // 4, 2 * (m // 2 % 2) + n:2 * (m // 2 % 2) + n + 1],
                                          src[:, x0:x1], AX, ALU.add)
                if m < 8:
                    c = slice(512 * (m // 2 % 2), 512 * (m // 2 % 2) + 512)
                    dst, hi = x_lo[m // 4][:, m % 2, c], x_hi[m // 4][:, m % 2, c]
                elif m < 10:
                    dst, hi = wq_l[:, m - 8, 0:512], wq_h[:, m - 8, 0:512]
                else:
                    src = src.rearrange("p (k r) -> p k r", k=CK)
                    dst, hi = wq_l[:, :, 512:768], wq_h[:, :, 512:768]
                dve.tensor_tensor(dst, src, hi.bitcast(F32), ALU.subtract).then_inc(lo_out, 1)

            link = chain(gate_step)
            for m in range(8):
                lo_part(m)
            dve.wait_ge(gate_exp, 1)
            link(dve.tensor_scalar(sil[:, 1], sil[:, 0], 1.0, None, ALU.add))
            link(dve.reciprocal(sil[:, 0], sil[:, 1]))
            link(dve.tensor_tensor(sil[:, 2], sil[:, 0], cond_col[:], ALU.mult))
            dve.wait_ge(lo_out, 8)
            link(dve.tensor_tensor(wrist_sum[:], piece_sum[:, :, :, 1], piece_sum[:, :, :, 2], ALU.add))
            part = (piece_sum[:, :, :, 0], wrist_sum[:], piece_sum[:, :, :, 3])
            link(dve.tensor_tensor(gate_in[:, 1], part[0], part[2], ALU.add))
            link(dve.tensor_tensor(gate_in[:, 0], gate_in[:, 1], part[1], ALU.add))
            link(dve.tensor_tensor(gate_in[:, 2], part[1], part[2], ALU.add))
            link(dve.tensor_scalar(gate_in[:, 0], gate_in[:, 0], 1.0 / L, None, ALU.mult))
            dve.tensor_scalar(gate_in[:, 1:3], gate_in[:, 1:3], 1.0 / (L - L3), None, ALU.mult)\
                .then_inc(gate_in_made, 1)
            for m in range(8, 11):
                lo_part(m)
            dve.wait_ge(gate_logits, 1)
            link(dve.tensor_tensor(gs[:, 0, 0:NE], bank(5)[0:NB, 0:NE], gate_bias[:], ALU.add))
            link(dve.tensor_tensor(gs[:, 1, :], bank(5)[0:NB, 8:16], time_bias[:], ALU.add))
            link(dve.tensor_scalar(gs[:, 2, 0:NE], gs[:, 1, 0:NE], 1.0, None, ALU.add))
            link(dve.tensor_tensor(gs[:, 3, 0:NE], gs[:, 0, 0:NE], gs[:, 2, 0:NE], ALU.mult))
            link(dve.tensor_tensor(gs[:, 4, 0:NE], gs[:, 3, 0:NE], gs[:, 1, NE:2 * NE], ALU.add))
            link(dve.tensor_reduce(gsc[:, 0:1], gs[:, 4, 0:NE], AX, ALU.max))
            dve.tensor_scalar(gs[:, 5, 0:NE], gs[:, 4, 0:NE], gsc[:, 0:1], None, ALU.subtract)\
                .then_inc(gate_logits, 1)
            dve.wait_ge(gate_exp, 2)
            link(dve.tensor_reduce(gsc[:, 1:2], gs[:, 6, 0:NE], AX, ALU.add))
            link(dve.reciprocal(gsc[:, 2:3], gsc[:, 1:2]))
            link(dve.tensor_scalar(gs[:, 7, 0:NE], gs[:, 6, 0:NE], gsc[:, 2:3], None, ALU.mult))
            for k in range(TOPK):
                left = gs[:, 7 if k == 0 else 10, 0:NE]
                link(dve.tensor_reduce(gsc[:, 3 + k:4 + k], left, AX, ALU.max))
                link(dve.tensor_scalar(gs[:, 11, 0:NE], left, gsc[:, 3 + k:4 + k], None, ALU.is_equal))
                link(stt(gs[:, 11, 0:NE], gs[:, 11, 0:NE], -8.0, iota_e[0:NB, 0:NE], ALU.mult, ALU.add))
                link(dve.tensor_reduce(gsc[:, 5 + k:6 + k], gs[:, 11, 0:NE], AX, ALU.min))
                link(dve.tensor_scalar(gs[:, 8 + k, 0:NE], gs[:, 11, 0:NE], gsc[:, 5 + k:6 + k], None,
                                       ALU.is_equal))
                if k == 0:
                    link(stt(gs[:, 10, 0:NE], gs[:, 8, 0:NE], -2.0, left, ALU.mult, ALU.add))
            link(dve.tensor_scalar(gsc[:, 7:8], gsc[:, 3:4], gsc[:, 4:5], 1e-8, ALU.add, ALU.add))
            link(dve.reciprocal(gsc[:, 8:9], gsc[:, 7:8]))
            link(dve.tensor_scalar(gs[:, 5, 0:2], gsc[:, 3:5], gsc[:, 8:9], None, ALU.mult))
            link(dve.tensor_scalar(gs[:, 5, 2:4], gsc[:, 5:7], 8.0, None, ALU.add))
            link(dve.tensor_scalar(gs[:, 10, 0:NE], gs[:, 8, 0:NE], gs[:, 5, 0:1], None, ALU.mult))
            stt(gs[:, 5, 4:8], gs[:, 9, 0:NE], gs[:, 5, 1:2], gs[:, 10, 0:NE], ALU.mult, ALU.add)\
                .then_inc(gate_rows_made, 1)
            dve.wait_ge(gate_wide, 1)
            link(dve.tensor_copy(picked[:].rearrange("p b n -> p (b n)"), bank(6)[:, 0:16]))
            dve.tensor_copy(expert_i[:], picked[0:1, :, 2:4]).then_inc(experts_known, 1)
            link(dve.memset(scale_col[:], 1.0))

            def split_quad(q, between=None, turns_from=None):
                for k in range(8):
                    v = 8 * q + k
                    if between and k % 2 == 1:
                        between(k // 2)
                    dve.wait_ge(gelu_done, v + 1)
                    after(dve, unit_done, v - 3)
                    cuts = CUTS[k % 2]
                    w = [scale_col[:, bass.ds(q, 1), r].rearrange("p q -> p q") for r in range(3)]
                    for x0, x1, r in cuts:
                        ins = dve.tensor_scalar(hh[k % 4][:, x0:x1], hid[k % 4][:, x0:x1], w[r], None, ALU.mult)
                    ins.then_inc(h_part, 1)
                    dve.wait_ge(h_part, v + 1)
                    for x0, x1, r in cuts:
                        ins = stt(hl[k % 4][:, x0:x1], hid[k % 4][:, x0:x1], w[r],
                                  hh[k % 4][:, x0:x1].bitcast(F32), ALU.mult, ALU.subtract)
                    ins.then_inc(h_split, 1)
                    if turns_from is not None and k % 2 == 0:
                        take_rest(turns_from + k // 2)
                    if turns_from is not None and k % 2 == 1 and turns_from + k // 2 >= 1:
                        third_part(turns_from + k // 2 - 1)

            def y_out(b):
                for n in range(4):
                    t, c = n // 2, n % 2
                    y = bank(4 + n)
                    dve.wait_ge(y_part, 4 * b + n + 1)
                    for x0, x1, r in CUTS[t]:
                        ins = stt(y_lo[:, c, 512 * t + x0:512 * t + x1], y[:, x0:x1],
                                  bias_col[:, c, b, r:r + 1],
                                  y_hi[:, c, 512 * t + x0:512 * t + x1].bitcast(F32), ALU.add, ALU.subtract)
                    ins.then_inc(y_split, 1)

            split_quad(0)
            by_pass = scale_col[:].rearrange("p (b j q) r -> p b j q r", b=NB, j=3)
            for q in range(2):
                for r, left_out in ((0, 2.0), (1, 1.0)):
                    stt(by_pass[:, :, 1:3, q, r], picked[:, :, 2:4], left_out, picked[:, :, 0:2],
                        ALU.not_equal, ALU.mult)
                dve.tensor_copy(by_pass[:, :, 1:3, q, 2], picked[:, :, 0:2])
            dve.wait_ge(bias_in, 16 * 3)
            link(dve.tensor_tensor(eb2w[:], wide(eb2_col[:], 2, NB), wide(picked[:, :, 4:8], 1, CK), ALU.mult))
            of = [eb2w[:, :, :, e] for e in range(NE)]
            bias = [bias_col[:, :, :, r] for r in range(3)]
            link(dve.tensor_tensor(bias[2], of[0], of[3], ALU.add))
            link(dve.tensor_tensor(bias[0], bias[2], of[1], ALU.add))
            link(dve.tensor_tensor(bias[1], bias[2], of[2], ALU.add))
            link(dve.tensor_tensor(bias[2], bias[0], of[2], ALU.add))
            for b in range(NB):
                ins = dve.tensor_tensor(bias_col[:, :, b, :], bias_col[:, :, b, :], wide(sb2_col[:], 2, 3), ALU.add)
            ins.then_inc(bias_made, 1)
            dve.wait_ge(bias_made, 1)

            with dve.Fori(1, QB) as q:
                split_quad(q)
            dve.wait_ge(late_in, 16 * LATE)
            dve.tensor_scalar(decay[:, 2:4], decay[:, 0:2], -1.0, None, ALU.mult).then_inc(decay_step, 1)
            dve.wait_ge(decay_step, 1)
            dve.tensor_tensor(decay[:, 2:4], decay[:, 2:4], decay[:, 0:2], ALU.min).then_inc(decay_step, 1)

            nlink = chain(norm_step)

            def sum_squares(b, n):
                dve.wait_ge(squared[b], n + 1)
                after(dve, normed, 4 * b)
                dve.tensor_reduce(ssum[:, 2 * n:2 * n + 2, :],
                                  square[n % 2][:].rearrange("p i (h d) -> p i h d", d=D), AX, ALU.add)\
                    .then_inc(summed, 1)

            def mean_squares(b):
                dve.wait_ge(summed, 4 * (b + 1))
                dve.tensor_scalar(ssum[:, :, 0:2 * H], ssum[:, :, 0:2 * H], 1.0 / D, RMS_EPS,
                                  ALU.mult, ALU.add).then_inc(var_made, 1)
                nlink(dve.tensor_scalar(ssum[:, :, 2 * H:], ssum[:, :, 2 * H:], NORM_EPS ** 2, None, ALU.max))
                dve.reciprocal(v_inv2[:, b * LT:(b + 1) * LT, :], ssum[:, :, 2 * H:])

            def norm(b, n):
                if n == 0:
                    dve.wait_ge(rooted, b + 1)
                    nlink(dve.reciprocal(ssum[:, :, 0:2 * H], ssum[:, :, 0:2 * H]))
                qk = qk_tm[b][:, 2 * n:2 * n + 2, :].rearrange("p i (h d) -> p i h d", d=D)
                dve.tensor_tensor(qk, qk, wide(ssum[:, 2 * n:2 * n + 2, 0:2 * H], 3, D), ALU.mult)\
                    .then_inc(normed, 1)

            def take_rest(w):
                dve.wait_ge(part1, w + 1)
                after(dve, part3, w - 1)
                dve.tensor_tensor(rest[:, w % 2, :], bank(0 if w % 2 else 2),
                                  parts[w // 2 % 2][:, 0, 512 * (w % 2):512 * (w % 2) + 512],
                                  ALU.subtract).then_inc(rest1, 1)

            def third_part(w):
                dve.wait_ge(part2, w + 1)
                c = slice(512 * (w % 2), 512 * (w % 2) + 512)
                dve.tensor_tensor(parts[w // 2 % 2][:, 2, c], rest[:, w % 2, :], parts[w // 2 % 2][:, 1, c],
                                  ALU.subtract).then_inc(part3, 1)

            y_out(0)
            dve.wait_ge(qkv_made, LT)
            split_quad(QB, lambda n: sum_squares(0, n))
            mean_squares(0)
            split_quad(QB + 1, lambda n: norm(0, n))
            split_quad(QB + 2, turns_from=0)
            split_quad(QB + 3, turns_from=4)
            third_part(7)
            with dve.Fori(QB + 4, QUADS) as q:
                split_quad(q)
            y_out(1)

            for n in range(LT // 2):
                sum_squares(1, n)
            mean_squares(1)
            for n in range(LT // 2):
                norm(1, n)
            plink = chain(part_step)

            def first_part(k):
                r = turns(min(k, 1)).index(("qk", k)) % 3
                src = psum[:, 2 * r:2 * r + 2, :]
                p1 = parts[k % 2][:, 0, :].rearrange("p (h n) -> p h n", h=2)
                dve.wait_ge(turned_b, k + 1)
                dve.wait_ge(parts_out[k % 2], 16 * (2 + k // 2))
                dve.wait_ge(part3, 8 + k)
                plink(dve.tensor_copy(p1, src))
                dve.tensor_tensor(rest[:], src, p1, ALU.subtract).then_inc(turned_b_read, 1)

            def other_parts(k):
                p2, p3 = [parts[k % 2][:, n, :].rearrange("p (h n) -> p h n", h=2) for n in (1, 2)]
                dve.wait_ge(turned_b_read, k + 1)
                plink(dve.tensor_copy(p2, rest[:]))
                dve.tensor_tensor(p3, rest[:], p2, ALU.subtract).then_inc(part3, 1)

            def take_output(g):
                dve.wait_ge(av_done, LT * (g + 1))
                after(dve, y_turned, g)
                dve.tensor_copy(yT[:].rearrange("p (h n) -> p h n", h=2), psum[:, 6:8, :]).then_inc(yT_out, 1)

            def finish_group(b, hg):
                g = (H // HG) * b + hg
                after(dve, ctx_done, g)
                dve.wait_ge(y_turned, g + 1)
                y = psum[:, 2:4, :].rearrange("p h (i j d) -> p (h i) j d", j=HG, d=VW)
                dve.reciprocal(y_r[:], y[:, :, :, D]).then_inc(post_step, 1)
                dve.wait_ge(post_step, 5 * g + 1)
                v = v_tm[:, bass.ds(b * LT, LT), bass.ds(hg * HG * D, HG * D)].rearrange(
                    "p i (j d) -> p i j d", d=D)
                dve.tensor_tensor(y_tm[:], y[:, :, :, 0:D], wide(y_r[:], 3, D), ALU.mult).then_inc(y_read, 1)
                dve.wait_ge(y_read, g + 1)
                dve.tensor_tensor(y_dot[:], y_tm[:], v, ALU.mult).then_inc(post_step, 1)
                dve.wait_ge(post_step, 5 * g + 2)
                dve.tensor_reduce(y_d[:], y_dot[:], AX, ALU.add).then_inc(post_step, 1)
                dve.wait_ge(post_step, 5 * g + 3)
                dve.tensor_tensor(y_d[:], y_d[:], v_inv2[:, bass.ds(b * LT, LT), bass.ds(hg * HG, HG)], ALU.mult)\
                    .then_inc(post_step, 1)
                dve.wait_ge(post_step, 5 * g + 4)
                dve.tensor_tensor(y_dot[:], v, wide(y_d[:], 3, D), ALU.mult).then_inc(post_step, 1)
                dve.wait_ge(post_step, 5 * g + 5)
                dve.tensor_tensor(ctx_tm[:, bass.ds(b * LT, LT), bass.ds(hg * HG * D, HG * D)].rearrange(
                    "p i (j d) -> p i j d", d=D), y_tm[:], y_dot[:], ALU.subtract).then_inc(ctx_done, 1)

            first_part(0)
            take_output(0)
            other_parts(0)
            for k in (1, 2):
                first_part(k)
                other_parts(k)
            finish_group(0, 0)
            first_part(3)
            other_parts(3)
            take_output(1)
            finish_group(0, 1)
            with dve.Fori(2, H // HG) as hg:
                take_output(hg)
                finish_group(0, hg)
            with dve.Fori(0, H // HG - 1) as hg:
                take_output(H // HG + hg)
                finish_group(1, hg)

            dve.wait_ge(late_in, 16 * LATE)

            def add_x(w):
                dve.wait_ge(proj_made, w + 1)
                two = x_tm[:, 2 * w:2 * w + 2, :]
                dve.tensor_tensor(two, bank(4 + w % 2).rearrange("p (i c) -> p i c", i=2), two, ALU.add)\
                    .then_inc(x2_done, 1)

            def past_tap(b):
                dve.wait_ge(x2T_out, 4 * b + 4)
                for c in range(CK):
                    s = slice(b * L + 1, (b + 1) * L)
                    ins = stt(convT[:, c, s], x2T[:, c, b * L:(b + 1) * L - 1], cond_col[:, c, 0:1],
                              convT[:, c, s], ALU.mult, ALU.add)
                ins.then_inc(conv_done, 1)

            take_output(GROUPS - 1)
            for w in range(3):
                add_x(w)
            finish_group(1, H // HG - 1)
            add_x(3)
            past_tap(0)
            for w in range(4, TT // 2):
                add_x(w)
            past_tap(1)

            link = chain(seq_step)
            for n in range(2):
                c = slice(512 * n, 512 * n + 512)
                dve.wait_ge(seq_made, n + 1)
                link(dve.tensor_scalar(seq_u[:, c], bank(2 + n), bs_col[:, 0:1], None, ALU.add))
            for n in range(2):
                c = slice(512 * n, 512 * n + 512)
                dve.wait_ge(seq_made, n + 3)
                link(dve.tensor_scalar(gate_b[:, c], bank(n), bp_b[:, 0:1], None, ALU.add))
                stt(gate_e[:, c], gate_b[:, c], -1.0, gate_b[:, c], ALU.mult, ALU.min).then_inc(neg_abs, 1)
            dve.wait_ge(decay_e, 2)
            link(stt(decay[:, 4:6], decay[:, 0:2], 0.0, decay[:, 2:4], ALU.max, ALU.add))
            link(dve.tensor_tensor(decay[:, 6:7], decay[:, 4:5], decay[:, 5:6], ALU.mult))
            link(dve.tensor_scalar(decay[:, 6:7], decay[:, 6:7], -1.0, 1.0, ALU.mult, ALU.add))
            for n in range(2):
                c = slice(512 * n, 512 * n + 512)
                dve.wait_ge(soft_log, n + 1)
                link(stt(gate_b[:, c], gate_b[:, c], 0.0, gate_e[:, c], ALU.max, ALU.add))
                link(stt(gate_b[:, c], gate_b[:, c], decay[:, 5:6], seq_u[:, c], ALU.mult, ALU.mult))
                link(dve.tensor_tensor_scan(gate_e[:, c], decay[:, 6:7].to_broadcast([P, 512]), gate_b[:, c],
                                            gate_e[:, 511:512] if n else 0.0, ALU.mult, ALU.add))
                dve.wait_ge(tanh_done, n + 1)
                dve.tensor_tensor(seq_u[:, c], gate_e[:, c], gate_c[:, c], ALU.mult).then_inc(state_out, 1)

            link = chain(rstep)
            dve.wait_ge(logits_made, 1)
            dve.tensor_tensor(route[:], bank(7)[:, 0:TT * RE].rearrange("p (i e) -> p i e", e=RE),
                              wide(br_row[:], 1, TT), ALU.add).then_inc(logits_out, 1)
            dve.wait_ge(route_done, 1)
            link(dve.tensor_reduce(prob[:], route[:], AX, ALU.max))
            link(dve.tensor_tensor(rt[0][:], route[:], wide(prob[:], 2, RE), ALU.is_equal))
            link(stt(rt[1][:], rt[0][:], -float(RE), wide(iota_e[:], 1, TT), ALU.mult, ALU.add))
            link(dve.tensor_reduce(sl[:], rt[1][:], AX, ALU.min))
            stt(onehot[:], wide(iota_e[:], 1, TT), -float(RE), wide(sl[:], 2, RE), ALU.add, ALU.is_equal)\
                .then_inc(onehot_done, 1)
            link(dve.tensor_copy(prob_hi[:], prob[:]))
            link(dve.tensor_tensor(prob_lo[:], prob[:], prob_hi[:].bitcast(F32), ALU.subtract))
            dve.wait_ge(ranks_made, 1)
            within = bank(0)[:, 0:TT * RE].rearrange("p (i e) -> p i e", e=RE)
            link(dve.tensor_copy(rt[3][:].rearrange("p i e -> p (i e)"), bank(1)[:, 0:TT * RE]))
            total, k, step = rt[3], 3, 1
            while step < TT:
                src, dst = rt[k], rt[k + 1]
                dve.tensor_copy(dst[:, 0:step, :], src[:, 0:step, :])
                link(dve.tensor_tensor(dst[:, step:, :], src[:, step:, :], src[:, 0:TT - step, :], ALU.add))
                k, step = k + 1, 2 * step
            running = rt[k]
            link(dve.tensor_tensor(rt[0][:], running[:], total[:], ALU.subtract))
            link(dve.tensor_tensor(rt[1][:], within, rt[0][:], ALU.add))
            link(dve.tensor_tensor(rk[0][:], wide(running[:, TT - 1, :], 2, TT), wide(iota_tok[:], 1, RE),
                                   ALU.is_gt))
            link(dve.tensor_reduce(re[0][:], rk[0][:], AX, ALU.add))
            link(dve.tensor_scalar(re[1][:], re[0][:], 1.0, None, ALU.max))
            link(dve.tensor_tensor_scan(re[2][:], ones[:, 0:RE], re[1][:], 0.0, ALU.mult, ALU.add))
            link(dve.tensor_tensor(re[3][:], re[2][:], re[1][:], ALU.subtract))
            link(stt(rt[8][:], wide(re[3][:], 1, TT), float(P), rt[1][:], ALU.mult, ALU.add))
            link(dve.tensor_tensor(rt[0][:], rt[8][:], onehot[:], ALU.mult))
            link(dve.tensor_reduce(sl[:], rt[0][:], AX, ALU.add))
            link(dve.tensor_tensor(past[:], wide(sl[:], 2, TW + 1), wide(iota_start[:], 1, TT), ALU.is_ge))
            dve.tensor_reduce(tile_of[:], past[:, :, 1:TW], AX, ALU.add)
            link(dve.tensor_tensor(in_tile[:], past[:, :, 0:TW], past[:, :, 1:], ALU.subtract))
            link(stt(lane[:], tile_of[:], -float(P), sl[:], ALU.mult, ALU.add))
            dve.tensor_tensor(tile_hot[:, :, 0, :], in_tile[:], wide(token1[:], 2, TW), ALU.mult)
            dve.tensor_tensor(tile_hot[:, :, 1, :], in_tile[:], wide(prob_hi[:].bitcast(F32), 2, TW), ALU.mult)
            dve.tensor_tensor(tile_hot[:, :, 2, :], in_tile[:], wide(prob_lo[:], 2, TW), ALU.mult)
            for n in range(2):
                i8 = slice(8 * n, 8 * n + 8)
                dve.tensor_tensor(lane_hot[:, i8, :], wide(lane[:, i8], 2, P), wide(iota_lane[:], 1, 8),
                                  ALU.is_equal).then_inc(lanes_made, 1)
            link(dve.tensor_tensor(tl[:], wide(iota_tile[:], 2, RE), wide(re[2][:], 1, TILES), ALU.is_ge))
            link(dve.tensor_reduce(tf[:], tl[:], AX, ALU.add))
            link(dve.tensor_scalar(tf[:], tf[:], float(RE - 1), None, ALU.min))
            dve.tensor_scalar(tile_i[:], tf[:], -1.0, float(RE - 1), ALU.mult, ALU.add).then_inc(slots_done, 1)
            dve.wait_ge(tokens_made, 1)
            link(dve.tensor_scalar(no_token[:], bank(2)[:, 0:TILES], 0.0, NO_TOKEN, ALU.is_equal, ALU.mult))
            link(stt(token_f[:], bank(2)[:, 0:TILES], -1.0, no_token[:], ALU.add, ALU.add))
            dve.tensor_copy(token_s[:], token_f[:]).then_inc(tokens_known, 1)
            link(dve.tensor_copy(prob_s[:], bank(2)[:, 2 * TW:2 * TW + TILES]))
            link(dve.tensor_tensor(prob_s[:], bank(2)[:, TW:TW + TILES], prob_s[:], ALU.add))

            def dve_step(s, i, m):
                e1 = place_of_expert(dve, s + 1)
                e2 = place_of_expert(dve, s + 2)
                if is_tile(s + 2):
                    if not isinstance(s, int) or s != -2:
                        x_lo_part(s + 2, i)
                    for h in range(2):
                        dve.wait_ge(w1_hi, 2 * s + 5 + h)
                        dve.tensor_tensor(split_quarter(w_lo, h), quarter(e2, h),
                                          split_quarter(w_hi, h).bitcast(F32), ALU.subtract).then_inc(w1_split, 1)
                    if isinstance(s, int) and s == -2:
                        x_lo_part(0, 0)
                if not isinstance(s, int) or s >= 0:
                    o_tile(s, i, m)
                if is_tile(s + 1):
                    for q in range(2):
                        dve.wait_ge(w2_hi, 2 * s + 3 + q)
                        dve.tensor_tensor(split_quarter(w_lo, 2 + q), quarter(e1, 2 + q),
                                          split_quarter(w_hi, 2 + q).bitcast(F32), ALU.subtract)\
                            .then_inc(w2_split, 1)
                        if q == 0:
                            for h in range(2):
                                dve.wait_ge(fhT_hi_out, 2 * s + 3 + h)
                                f = slice(4 * h, 4 * h + 4)
                                dve.tensor_tensor(fhT_lo[:, f, :].rearrange("p f n -> p (f n)"), bank(4 + h),
                                                  fhT_hi[:, f, :].rearrange("p f n -> p (f n)").bitcast(F32),
                                                  ALU.subtract).then_inc(fhT_lo_out, 1)

            def x_lo_part(s, i):
                dve.wait_ge(x_hi_out, s + 1)
                dve.tensor_tensor(xsT_lo[i][:].rearrange("p k n -> p (k n)"), bank(6)[:, 0:C],
                                  xsT_hi[i][:].rearrange("p k n -> p (k n)").bitcast(F32), ALU.subtract)\
                    .then_inc(x_lo_out, 1)

            def o_tile(s, i, m):
                dve.wait_ge(w2_used, 2 * s + 2)
                dve.wait_ge(x2s_in[i], 16 * m + 16)
                after(dve, out_stored[i], 16 * m)
                stt(fo[i][:], bank(7)[:, 0:C], prob_s[:, bass.ds(s, 1)], x2s[i][:], ALU.mult, ALU.add)\
                    .then_inc(fo_out, 1)

            dve.wait_ge(x3_stored, 16 * NB)
            steps(dve, dve_step)
            o_tile(TILES - 1, 0, TILES // 2)

        @block.tensor
        def _(pe):
            pe.wait_ge(consts_made, 1)
            for m in range(12):
                if m == 0 or m == 4:
                    pe.wait_ge(x_in[m // 4], 16)
                if m == 8:
                    pe.wait_ge(wproj_in, 32)
                if m >= 8:
                    pe.wait_ge(lo_out, m - 6)
                for n in range(4):
                    if m < 8:
                        c, i = m % 2, 4 * (m // 2) + n
                        src = x_tm[:, i, c * P:(c + 1) * P]
                    elif m < 10:
                        src = qkv_raw[:, n, (m - 8) * P:(m - 7) * P]
                    else:
                        c, r = n // 2, n % 2
                        src = (qkv_raw[:, 4 + r, :] if m == 10 else proj_raw[:, r, :])[:, c * P:(c + 1) * P]
                    ins = pe.transpose(bank(m if m < 8 else m - 7)[:, n * P:(n + 1) * P], src, ident[:])
                ins.then_inc(setup_filled, 1)

            pe.wait_ge(gate_in_made, 1)
            pe.wait_ge(const_in, 16 * CONSTS)
            pe.wait_ge(lo_out, 6)
            for c in range(CK):
                pe.matmul(bank(5)[0:NB, 8:16], sil[:, 2, c, :], time_rows[:, c, :], start=(c == 0), stop=(c == CK - 1))
            for n in range(3 * CK):
                ins = pe.matmul(bank(5)[0:NB, 0:NE], gate_in[:, n // CK, n % CK, :], gate_rows[:, n, :],
                                start=(n == 0), stop=(n == 3 * CK - 1))
            ins.then_inc(gate_logits, 1)

            def three(o, w, x, first, last):
                for n, (i, j) in enumerate(((0, 0), (0, 1), (1, 0))):
                    ins = pe.matmul(o, w[i], x[j], start=first and n == 0, stop=last and n == 2)
                return ins

            def up(b, v, k):
                j, t = k // 2, k % 2
                if t == 0:
                    pe.wait_ge(w_split, (v - k) // 2 + j + 1)
                after(pe, gelu_done, v - 3)
                s = slice(512 * t, 512 * t + 512)
                for c in range(CK):
                    ins = three(bank(k % 4), (w1h[j][:, c, :], w1l[j][:, c, :]),
                                (x_hi[b][:, c, s], x_lo[b][:, c, s]),
                                c == 0, c == CK - 1)
                ins.then_inc(hid_made, 1)

            def down(b, v, k, first, last):
                j, t = k // 2, k % 2
                pe.wait_ge(h_split, v + 1)
                for c in range(CK):
                    s = slice(c * P, (c + 1) * P)
                    ins = three(bank(4 + 2 * t + c), (w2h[j][:, s], w2l[j][:, s]), (hh[k % 4][:], hl[k % 4][:]),
                                first, last)
                ins.then_inc(unit_done, 1)

            def quad(b, q, first=False, last=False, turns_from=None):
                for k in range(8):
                    turning = turns_from is not None and k % 2 == 0
                    if turning:
                        turn_qk(turns_from + k // 2, q, k)
                        down(b, 8 * q + k, k, first and k < 2, last and k >= 6)
                        pe.wait_ge(rest1, turns_from + k // 2 + 1)
                    if k < 6:
                        up(b, 8 * q + k + 2, k + 2)
                    elif not last:
                        up(b, 8 * (q + 1) + k - 6, k - 6)
                    if not turning:
                        down(b, 8 * q + k, k, first and k < 2, last and k >= 6)

            def turn_qk(w, q, k):
                pe.wait_ge(normed, 4)
                pe.wait_ge(gelu_done, 8 * q + k - 1)
                for n in range(4):
                    ins = pe.transpose(bank((k + 2) % 4)[:, n * P:(n + 1) * P],
                                       qk_tm[0][:, 4 * (w % 2) + n, (w // 2) * P:(w // 2 + 1) * P], ident[:])
                ins.then_inc(turned, 1)

            for b in range(NB):
                q0 = b * QB
                if b:
                    pe.wait_ge(qkv_out, b * LT)
                else:
                    pe.wait_ge(lo_out, 11)
                    pe.wait_ge(hi_out, 12)
                up(b, 8 * q0, 0)
                up(b, 8 * q0 + 1, 1)
                if b:
                    pe.wait_ge(y_split, 4 * b)
                else:
                    pe.wait_ge(gate_rows_made, 1)
                    for n in range(NB):
                        ins = pe.matmul(bank(6)[:, 8 * n:8 * n + 8], pick_row[:, n, :], gs[:, 5, :],
                                        start=True, stop=True)
                    ins.then_inc(gate_wide, 1)
                    pe.wait_ge(experts_known, 1)
                quad(b, q0, first=True)
                if b:
                    quad(b, q0 + 1)
                    quad(b, q0 + 2, turns_from=0)
                    quad(b, q0 + 3, turns_from=4)
                    quad(b, q0 + 4)
                else:
                    with pe.Fori(q0 + 1, q0 + QB - 1) as q:
                        quad(b, q)
                quad(b, q0 + QB - 1, last=True)
                pe.wait_ge(lo_out, 11)
                pe.wait_ge(gelu_done, (b + 1) * 8 * QB)
                for i in range(LT):
                    if i % 4 == 0:
                        pe.wait_ge(y_split, 4 * b + 2 + i // 2)
                    if i >= 2:
                        pe.wait_ge(qkv_out, b * LT + i - 1)
                    s = slice(i * P, (i + 1) * P)
                    for c in range(CK):
                        three(bank(2 * i % 4), (y_hi[:, c, s], y_lo[:, c, s]),
                              (wq_h[:, c, 0:2 * C], wq_l[:, c, 0:2 * C]), c == 0, c == CK - 1)
                    for c in range(CK):
                        ins = three(bank((2 * i + 1) % 4)[:, 0:C], (y_hi[:, c, s], y_lo[:, c, s]),
                                    (wq_h[:, c, 2 * C:], wq_l[:, c, 2 * C:]), c == 0, c == CK - 1)
                    ins.then_inc(qkv_made, 1)

            PER = HG * LT

            def turn(g, r):
                pe.wait_ge(yT_out, g + 1)
                for i in range(LT):
                    ins = pe.transpose(psum[:, 2 * r + i // 4, (i % 4) * P:(i % 4 + 1) * P],
                                       yT[:, i * P:(i + 1) * P], ident[:])
                ins.then_inc(y_turned, 1)

            def turn_b(k, r):
                pe.wait_ge(normed, 8)
                for i in range(LT):
                    ins = pe.transpose(psum[:, 2 * r + i // 4, (i % 4) * P:(i % 4 + 1) * P],
                                       qk_tm[1][:, i, k * P:(k + 1) * P], ident[:])
                ins.then_inc(turned_b, 1)

            def pair_free(g, order, pos):
                if pos < 3:
                    if isinstance(g, int) and g == 0:
                        return
                    if isinstance(g, int) and g == 1:
                        if pos == 2:
                            pe.wait_ge(turned_b_read, 1)
                        else:
                            pe.wait_ge(exp_done, PER - 1 + pos)
                        return
                    pe.wait_ge(exp_done, PER * g + pos - 2)
                    return
                what, n = order[pos - 3]
                if what == "scores":
                    pe.wait_ge(exp_done, PER * g + n + 1)
                elif what == "turn":
                    pe.wait_ge(y_read, g)
                else:
                    pe.wait_ge(turned_b_read, n + 1)

            def scores(i, u, r):
                mt, j = u // HG, u % HG
                for h in range(2):
                    ins = pe.matmul(psum[:, 2 * r + h, :], k_stack[i][:, j, mt * P:(mt + 1) * P],
                                    q_stack[i][:, j, 512 * h:512 * h + 512], start=True, stop=True)
                ins.then_inc(scored, 1)

            def values(g, i, mt, h):
                if h == 0:
                    pe.wait_ge(exp_done, PER * g + HG * (mt + 1))
                    if mt == 0:
                        pe.wait_ge(v_ready, g + 1)
                        after(pe, yT_out, g)
                for j in range(HG):
                    ins = pe.matmul(psum[VW * j:VW * j + VW, 6 + h, :], v_ones[i][:, mt, j, :],
                                    pexp[mt % 2][:, j, 512 * h:512 * h + 512],
                                    start=(mt == 0), stop=(mt == LT - 1))
                if h == 1:
                    ins.then_inc(av_done, 1)

            def group(g, i, first=False):
                if isinstance(g, int) and g < 2:
                    pe.wait_ge(stack_in[i], 16 * 2 * TERMS)
                else:
                    pe.wait_ge(stack_in[i], 16 * TERMS * (g - i) + 16 * 2 * TERMS)
                order = turns(g)
                for pos, (what, u) in enumerate(order):
                    pair_free(g, order, pos)
                    if what == "turn":
                        turn(g - 1, pos % 3)
                    elif what == "qk":
                        turn_b(u, pos % 3)
                    else:
                        scores(i, u, pos % 3)
                        mt, j = u // HG, u % HG
                        if j % 2 and not (first and mt == 0):
                            if mt == 0:
                                values(g - 1, 1 - i, LT - 1, j // 2)
                            else:
                                values(g, i, mt - 1, j // 2)

            pe.wait_ge(qkv_out, TT)
            group(0, 0, first=True)
            group(1, 1)
            with pe.Fori(2, GROUPS, 2) as g:
                group(g, 0)
                group(g + 1, 1)
            values(GROUPS - 1, 1, LT - 1, 0)
            values(GROUPS - 1, 1, LT - 1, 1)
            def turn_ctx(w):
                pe.wait_ge(ctx_done, 4 if w < 4 else 8)
                after(pe, ctxT_out, w - 1)
                for n in range(4):
                    ins = pe.transpose(bank(w % 2)[:, n * P:(n + 1) * P],
                                       ctx_tm[:, 2 * w + n // 2, (n % 2) * P:(n % 2 + 1) * P], ident[:])
                ins.then_inc(ctx_turned, 1)

            pe.wait_ge(exp_done, PER * GROUPS)
            turn_ctx(0)
            def project(w):
                pe.wait_ge(ctxT_out, w + 1)
                after(pe, x2_done, w - 1)
                for n in range(4):
                    i, c = n // 2, n % 2
                    ins = pe.matmul(bank(4 + w % 2)[:, i * C:(i + 1) * C], ctxT[w % 2][:, i, c, :], projT[:, c, :],
                                    start=(c == 0), stop=(c == CK - 1))
                ins.then_inc(proj_made, 1)

            def turn_x2(w):
                if w == 0:
                    pe.wait_ge(y_read, GROUPS)
                pe.wait_ge(x2_done, 2 * (w // 2) + 2)
                after(pe, x2T_out, w - 3)
                for n in range(4):
                    ins = pe.transpose(x2_bank(w)[:, n * P:(n + 1) * P],
                                       x_tm[:, 4 * (w // 2) + n, (w % 2) * P:(w % 2 + 1) * P], ident[:])
                ins.then_inc(x2_turned, 1)

            for w in range(4):
                if w < 3:
                    turn_ctx(w + 1)
                project(w)
                if w == 0:
                    turn(GROUPS - 1, 1)
            for w in range(4):
                turn_x2(w)
            turn_ctx(4)
            for w in range(4, TT // 2):
                if w + 1 < TT // 2:
                    turn_ctx(w + 1)
                project(w)
                if w == 5:
                    turn_x2(4)
                    turn_x2(5)
            turn_x2(6)
            turn_x2(7)

            def keep_warm(n):
                for k in range(n):
                    pe.matmul(bank(6), ident[:], projT[:].rearrange("p k c -> p (k c)"),
                              start=(k == 0), stop=(k == n - 1))

            pe.wait_ge(late_in, 16 * LATE)
            pe.wait_ge(x2T_out, TT // 2)
            for k, w, src in ((1, ws_sb[:], x2T), (0, wp_sb[:, :, 0:N], convT), (2, wp_sb[:, :, N:2 * N], convT)):
                if k == 0:
                    pe.wait_ge(conv_done, NB)
                for n in range(2):
                    for c in range(CK):
                        for b in range(NB):
                            s = slice(b * L + 512 * n, b * L + 512 * n + 512)
                            ins = pe.matmul(psum[half[b], 2 * k + n, :], w[:, c, :], src[:, c, s],
                                            start=(c == 0), stop=(c == CK - 1))
                    ins.then_inc(seq_made, 1)
            keep_warm(4)
            for w in range(8):
                n, b, c = w // 4, w // 2 % 2, w % 2
                if w % 4 == 0:
                    pe.wait_ge(state_out, n + 1)
                after(pe, x3T_out, w - 3)
                pe.matmul(bank(w % 4), wo_sb[:, b, c * P:(c + 1) * P], seq_u[:, 512 * n:512 * n + 512],
                          start=True, stop=True).then_inc(x3T_made, 1)
            for n in range(2):
                for b in range(NB):
                    pe.wait_ge(x3T_out, 4 * n + 2 * b + 2)
                    for i in range(b * LT + 4 * n, b * LT + 4 * n + 4):
                        for c in range(CK):
                            ins = pe.matmul(bank(7)[:, i * RE:(i + 1) * RE], x3T[:, c, i * P:(i + 1) * P],
                                            wr_sb[:, c, :], start=(c == 0), stop=(c == CK - 1))
            ins.then_inc(logits_made, 1)

            def rank():
                pe.wait_ge(onehot_done, 1)
                flat = onehot[:].rearrange("p i e -> p (i e)")
                pe.matmul(bank(0)[:, 0:TT * RE], tri[:], flat, start=True, stop=True)
                pe.matmul(bank(1)[:, 0:TT * RE], ones[:], flat, start=True, stop=True).then_inc(ranks_made, 1)

            for w in range(TT // 2):
                if w == 4:
                    rank()
                after(pe, x3_out, w - 3)
                for n in range(4):
                    i, c = 2 * w + n // 2, n % 2
                    ins = pe.transpose(bank(3 + w % 4)[:, n * P:(n + 1) * P],
                                       x3T[:, c, i * P:(i + 1) * P], ident[:])
                ins.then_inc(x3_turned, 1)
            pe.wait_ge(x3_out, TT // 2)
            keep_warm(7)
            for i in range(TT):
                if i % 8 == 0:
                    pe.wait_ge(lanes_made, i // 8 + 1)
                ins = pe.matmul(bank(2)[:, 0:3 * TW], lane_hot[:, i, :],
                                tile_hot[:, i].rearrange("p a s -> p (a s)"), start=(i == 0), stop=(i == TT - 1))
            ins.then_inc(tokens_made, 1)

            def turn_x(s, i, n):
                pe.wait_ge(xs_in[i], 16 * n)
                after(pe, x_lo_out, s)
                for c in range(CK):
                    ins = pe.transpose(bank(6)[:, c * P:(c + 1) * P], xs[i][:, c * P:(c + 1) * P], ident[:])
                ins.then_inc(xs_turned, 1)

            def expert_up(s, i):
                pe.wait_ge(x_lo_out, s + 1)
                after(pe, fh_out, s - 1)
                for h in range(2):
                    pe.wait_ge(w1_split, 2 * s + h + 1)
                    for c in range(CK):
                        w = slice(512 * c, 512 * c + 512)
                        ins = three(psum[:, 2 * i + h, :], (xsT_hi[i][:, c, :], xsT_lo[i][:, c, :]),
                                    (w_hi[:, h, w], w_lo[:, h, w]), c == 0, c == CK - 1)
                    ins.then_inc(w1_used, 1)

            def turn_h(s, i):
                pe.wait_ge(fh_out, s + 1)
                after(pe, fhT_lo_out, 2 * s)
                for f in range(FC):
                    ins = pe.transpose(psum[:, 4 + f // 4, (f % 4) * P:(f % 4 + 1) * P],
                                       fh[i][:, f * P:(f + 1) * P], ident[:])
                ins.then_inc(fh_turned, 1)

            def expert_down(s, i):
                after(pe, fo_out, s)
                for q in range(2):
                    pe.wait_ge(fhT_lo_out, 2 * s + q + 1)
                    pe.wait_ge(w2_split, 2 * s + q + 1)
                    for f in range(4 * q, 4 * q + 4):
                        w = slice((f % 4) * C, (f % 4 + 1) * C)
                        ins = three(bank(7)[:, 0:C], (fhT_hi[:, f, :], fhT_lo[:, f, :]),
                                    (w_hi[:, 2 + q, w], w_lo[:, 2 + q, w]), f == 0, f == FC - 1)
                    ins.then_inc(w2_used, 1)

            def tile(s, i, n, up=True, turn=True):
                turn_h(s, i)
                if up:
                    expert_up(s + 1, 1 - i)
                if turn:
                    turn_x(s + 2, i, n)
                expert_down(s, i)

            pe.wait_ge(slots_done, 1)
            keep_warm(4)
            turn_x(0, 0, 1)
            expert_up(0, 0)
            turn_x(1, 1, 1)
            tile(0, 0, 2)
            with pe.Fori(0, (TILES - 3) // 2) as m:
                tile(2 * m + 1, 1, m + 2)
                tile(2 * m + 2, 0, m + 3)
            tile(TILES - 2, 1, 0, turn=False)
            tile(TILES - 1, 0, 0, up=False, turn=False)


_INS = {"x": "x", "cond": "cond_1024", "gate_w": "L0_cond_gate_w", "gate_b": "L0_cond_gate_b",
        "time_w": "L0_cond_time_w", "time_b": "L0_cond_time_b", "ew1": "L0_cond_ew1", "eb1": "L0_cond_eb1",
        "ew2": "L0_cond_ew2", "eb2": "L0_cond_eb2", "sw1": "L0_cond_sw1", "sb1": "L0_cond_sb1",
        "sw2": "L0_cond_sw2", "sb2": "L0_cond_sb2", "w_qkv": "L0_attn_w_qkv", "w_proj": "L0_attn_w_proj",
        "conv_b": "L0_cond2_conv_b", "Wp": "L0_cond2_Wp", "bp": "L0_cond2_bp", "Ws": "L0_cond2_Ws",
        "bs": "L0_cond2_bs", "A_log": "L0_cond2_A_log", "dt_log": "L0_cond2_dt_log", "Wo": "L0_cond2_Wo",
        "bo": "L0_cond2_bo", "Wr": "L0_ffn_Wr", "br": "L0_ffn_br", "W1": "L0_ffn_W1", "W2": "L0_ffn_W2"}


def kernel(**inputs):
    import numpy as _np
    import concourse.bacc as _bacc
    from concourse import mybir as _mybir
    from concourse.bass_utils import run_bass_kernel_spmd as _run

    nc = _bacc.Bacc("TRN2", target_bir_lowering=False, num_devices=1)
    arrays, args = {}, {}
    for short, name in _INS.items():
        v = _np.ascontiguousarray(inputs[name])
        arrays[f"in_{name}"] = v
        args[short] = nc.dram_tensor(f"in_{name}", v.shape, _mybir.dt.from_np(v.dtype), kind="ExternalInput").ap()
    out = nc.dram_tensor("out_0", (NB, L, C), F32, kind="ExternalOutput").ap()
    layer_kernel(nc, args, out)
    r = _run(nc, [arrays], core_ids=[0])
    return r.results[0]["out_0"]
```
